# Optimizing a Trainium2 kernel written in Bass

```python
import numpy as np
import jax
import jax.numpy as jnp

def _softmax(x, axis=-1):
    return jax.nn.softmax(x, axis=axis)

def _gelu(x):
    return jax.nn.gelu(x, approximate=True)

def _silu(x):
    return jax.nn.silu(x)

def _sigmoid(x):
    return jax.nn.sigmoid(x)

def _layernorm(x, axis=-1, eps=1e-05):
    m = jnp.mean(x, axis=axis, keepdims=True)
    v = jnp.var(x, axis=axis, keepdims=True)
    return (x - m) / jnp.sqrt(v + eps)

def _scatter_add(tgt, idx, src, axis=0):
    return tgt.at[idx].add(src)

def _segment_sum(src, seg, n):
    return jax.ops.segment_sum(src, seg, n)
kernel_name = 'mk_gnn_preln_d4_gnn_r8_87611f'

def setup_inputs(seed: int=0):
    np.random.seed(seed)
    _w = jnp.asarray

    def _rec_inputs():
        import jax
        import jax.numpy as jnp
        _gk = jax.random.key(seed)
        x = -0.0002117 + 1 * jax.random.normal(jax.random.fold_in(_gk, 1), (6250, 256), jnp.float32)
        src = jax.random.randint(jax.random.fold_in(_gk, 2), (100000,), 0, 6250, jnp.int32)
        dst = jnp.minimum((6250 * jax.random.uniform(jax.random.fold_in(_gk, 3), (100000,)) ** 2.0).astype(jnp.int32), 49999)
        _o = jnp.argsort(dst, stable=True)
        src = src[_o]
        dst = dst[_o]
        edge_type_20 = jax.random.randint(jax.random.fold_in(_gk, 13), (100000,), 0, 20, jnp.int32)
        edge_weight1 = jax.random.uniform(jax.random.fold_in(_gk, 14), (100000, 1), jnp.float32, 0.0, 0.999998)
        return (x, src, dst, edge_type_20, edge_weight1)
    x, src, dst, edge_type_20, edge_weight1 = _rec_inputs()

    def _L0_gnn_setup():
        import jax, jax.numpy as jnp
        import numpy as np
        N_NODES = 12500
        N_EDGES = 200000
        D_IN = 256
        HEADS = 8
        D_HEAD = 32
        NEG_SLOPE = 0.2
        BN_EPS = 1e-05
        key = jax.random.key(seed)
        ks = jax.random.split(key, 8)
        x = jax.random.normal(ks[0], (N_NODES, D_IN), dtype=jnp.float32)
        edge_index = jax.random.randint(ks[1], (2, N_EDGES), 0, N_NODES, dtype=jnp.int32)
        W = jax.random.normal(ks[2], (D_IN, HEADS * D_HEAD), dtype=jnp.float32) / np.sqrt(D_IN)
        att_src = jax.random.normal(ks[3], (HEADS, D_HEAD), dtype=jnp.float32) / np.sqrt(D_HEAD)
        att_dst = jax.random.normal(ks[4], (HEADS, D_HEAD), dtype=jnp.float32) / np.sqrt(D_HEAD)
        bias = jax.random.normal(ks[5], (HEADS * D_HEAD,), dtype=jnp.float32) * 0.01
        gamma = jnp.ones((HEADS * D_HEAD,), dtype=jnp.float32)
        beta = jnp.zeros((HEADS * D_HEAD,), dtype=jnp.float32)
        return {'x': x, 'edge_index': edge_index, 'W': W, 'att_src': att_src, 'att_dst': att_dst, 'bias': bias, 'gamma': gamma, 'beta': beta}
    _L0_gnn_all = _L0_gnn_setup()
    _L0_gnn_in = {k: v for k, v in _L0_gnn_all.items() if k in ('W', 'att_src', 'att_dst', 'bias', 'gamma', 'beta')}
    del _L0_gnn_all

    def _L1_gnn_setup():
        import jax, jax.numpy as jnp
        import numpy as np
        N_NODES = 6250
        N_EDGES = 100000
        IN_CH = 256
        OUT_CH = 64
        HEADS = 4
        key = jax.random.key(seed)
        k1, k2, k3, k4, k5 = jax.random.split(key, 5)
        x = jax.random.normal(k1, (N_NODES, IN_CH), dtype=jnp.float32)
        edge_index = jax.random.randint(k2, (2, N_EDGES), 0, N_NODES, dtype=jnp.int64)
        weight = jax.random.normal(k3, (HEADS, IN_CH, OUT_CH), dtype=jnp.float32) * (2.0 / (IN_CH + OUT_CH)) ** 0.5
        att_src = jax.random.normal(k4, (1, HEADS, OUT_CH), dtype=jnp.float32) * 0.1
        att_dst = jax.random.normal(k5, (1, HEADS, OUT_CH), dtype=jnp.float32) * 0.1
        bias = jnp.zeros((HEADS * OUT_CH,), dtype=jnp.float32)
        return {'x': x, 'edge_index': edge_index, 'weight': weight, 'att_src': att_src, 'att_dst': att_dst, 'bias': bias}
    _L1_gnn_all = _L1_gnn_setup()
    _L1_gnn_in = {k: v for k, v in _L1_gnn_all.items() if k in ('weight', 'att_src', 'att_dst', 'bias')}
    del _L1_gnn_all

    def _L2_gnn_setup():
        import jax, jax.numpy as jnp
        import numpy as np
        N_NODES = 1250
        N_EDGES = 40000
        NUM_RELS = 20
        IN_FEAT = 256
        OUT_FEAT = 256
        key = jax.random.key(seed)
        k1, k2, k3, k4, k5, k6 = jax.random.split(key, 6)
        h = jax.random.normal(k1, (N_NODES, IN_FEAT), dtype=jnp.float32)
        gain = float(np.sqrt(2.0))
        limit = gain * float(np.sqrt(6.0 / (IN_FEAT + OUT_FEAT)))
        weight = jax.random.uniform(k2, (NUM_RELS, IN_FEAT, OUT_FEAT), dtype=jnp.float32, minval=-limit, maxval=limit)
        norm = jax.random.uniform(k3, (N_EDGES, 1), dtype=jnp.float32)
        edge_src = jax.random.randint(k4, (N_EDGES,), 0, N_NODES, dtype=jnp.int32)
        edge_dst = jax.random.randint(k5, (N_EDGES,), 0, N_NODES, dtype=jnp.int32)
        rel_type = jax.random.randint(k6, (N_EDGES,), 0, NUM_RELS, dtype=jnp.int32)
        return {'h': h, 'weight': weight, 'norm': norm, 'edge_src': edge_src, 'edge_dst': edge_dst, 'rel_type': rel_type}
    _L2_gnn_all = _L2_gnn_setup()
    _L2_gnn_in = {k: v for k, v in _L2_gnn_all.items() if k in ('weight',)}
    del _L2_gnn_all

    def _L3_gnn_setup():
        import jax, jax.numpy as jnp
        import numpy as np
        BN_EPS = 1e-05
        key = jax.random.key(seed)
        ks = jax.random.split(key, 4)
        N, E, H = (1250, 40000, 256)
        x = jax.random.normal(ks[0], (N, H), dtype=jnp.float32)
        edge_index = jax.random.randint(ks[1], (2, E), 0, N, dtype=jnp.int64)
        weight = jax.random.normal(ks[2], (H, H), dtype=jnp.float32) * (1.0 / np.sqrt(H))
        bias = jax.random.normal(ks[3], (H,), dtype=jnp.float32) * 0.02
        gamma = jnp.ones((H,), dtype=jnp.float32)
        beta = jnp.zeros((H,), dtype=jnp.float32)
        running_mean = jnp.zeros((H,), dtype=jnp.float32)
        running_var = jnp.ones((H,), dtype=jnp.float32)
        return {'x': x, 'edge_index': edge_index, 'weight': weight, 'bias': bias, 'gamma': gamma, 'beta': beta, 'running_mean': running_mean, 'running_var': running_var}
    _L3_gnn_all = _L3_gnn_setup()
    _L3_gnn_in = {k: v for k, v in _L3_gnn_all.items() if k in ('weight', 'bias', 'gamma', 'beta', 'running_mean', 'running_var')}
    del _L3_gnn_all
    return {'x': x, 'src': src, 'dst': dst, 'edge_type_20': edge_type_20, 'edge_weight1': edge_weight1, 'L0_gnn_W': _L0_gnn_in['W'], 'L0_gnn_att_src': _L0_gnn_in['att_src'], 'L0_gnn_att_dst': _L0_gnn_in['att_dst'], 'L0_gnn_bias': _L0_gnn_in['bias'], 'L0_gnn_gamma': _L0_gnn_in['gamma'], 'L0_gnn_beta': _L0_gnn_in['beta'], 'L1_gnn_weight': _L1_gnn_in['weight'], 'L1_gnn_att_src': _L1_gnn_in['att_src'], 'L1_gnn_att_dst': _L1_gnn_in['att_dst'], 'L1_gnn_bias': _L1_gnn_in['bias'], 'L2_gnn_weight': _L2_gnn_in['weight'], 'L3_gnn_weight': _L3_gnn_in['weight'], 'L3_gnn_bias': _L3_gnn_in['bias'], 'L3_gnn_gamma': _L3_gnn_in['gamma'], 'L3_gnn_beta': _L3_gnn_in['beta'], 'L3_gnn_running_mean': _L3_gnn_in['running_mean'], 'L3_gnn_running_var': _L3_gnn_in['running_var']}

def reference(x, src, dst, edge_type_20, edge_weight1, L0_gnn_W, L0_gnn_att_src, L0_gnn_att_dst, L0_gnn_bias, L0_gnn_gamma, L0_gnn_beta, L1_gnn_weight, L1_gnn_att_src, L1_gnn_att_dst, L1_gnn_bias, L2_gnn_weight, L3_gnn_weight, L3_gnn_bias, L3_gnn_gamma, L3_gnn_beta, L3_gnn_running_mean, L3_gnn_running_var):
    import jax
    import jax.numpy as jnp

    def _L0_gnn_ref(x, edge_index, W, att_src, att_dst, bias, gamma, beta):
        import jax, jax.numpy as jnp
        import numpy as np
        N_NODES = 12500
        N_EDGES = 200000
        D_IN = 256
        HEADS = 8
        D_HEAD = 32
        NEG_SLOPE = 0.2
        BN_EPS = 1e-05
        N = x.shape[0]
        H, D = att_src.shape
        xh = (x @ W).reshape(N, H, D)
        a_src = jnp.einsum('nhd,hd->nh', xh, att_src)
        a_dst = jnp.einsum('nhd,hd->nh', xh, att_dst)
        loops = jnp.arange(N, dtype=edge_index.dtype)
        src = jnp.concatenate([edge_index[0], loops])
        dst = jnp.concatenate([edge_index[1], loops])
        e = jax.nn.leaky_relu(a_src[src] + a_dst[dst], NEG_SLOPE)
        m = jax.ops.segment_max(e, dst, num_segments=N)
        e = jnp.exp(e - m[dst])
        denom = jax.ops.segment_sum(e, dst, num_segments=N)
        alpha = e / denom[dst]
        msg = xh[src] * alpha[:, :, None]
        out = jax.ops.segment_sum(msg, dst, num_segments=N).reshape(N, H * D) + bias
        mean = jnp.mean(out, axis=0)
        var = jnp.var(out, axis=0)
        out = (out - mean) * jax.lax.rsqrt(var + BN_EPS) * gamma + beta
        return out + x

    def _L1_gnn_ref(x, edge_index, weight, att_src, att_dst, bias):
        import jax, jax.numpy as jnp
        import numpy as np
        N_NODES = 6250
        N_EDGES = 100000
        IN_CH = 256
        OUT_CH = 64
        HEADS = 4
        num_nodes = x.shape[0]
        row, col = (edge_index[0], edge_index[1])
        x_h = jnp.einsum('nf,hfc->nhc', x, weight)
        alpha_src = jnp.sum(x_h * att_src[0], axis=-1)
        alpha_dst = jnp.sum(x_h * att_dst[0], axis=-1)
        alpha = alpha_src[row] + alpha_dst[col]
        alpha = jax.nn.leaky_relu(alpha, negative_slope=0.2)
        alpha_max = jax.ops.segment_max(alpha, row, num_segments=num_nodes)
        alpha = jnp.exp(alpha - alpha_max[row])
        alpha_sum = jax.ops.segment_sum(alpha, row, num_segments=num_nodes)
        alpha = alpha / jnp.clip(alpha_sum[row], 1e-16)
        messages = alpha[:, :, None] * x_h[col]
        out = jax.ops.segment_sum(messages, row, num_segments=num_nodes)
        out = out.reshape(num_nodes, -1) + bias
        return out

    def _L2_gnn_ref(h, weight, norm, edge_src, edge_dst, rel_type):
        import jax, jax.numpy as jnp
        import numpy as np
        N_NODES = 1250
        N_EDGES = 40000
        NUM_RELS = 20
        IN_FEAT = 256
        OUT_FEAT = 256
        h_all = jnp.einsum('ni,rio->nro', h, weight)
        msg = h_all[edge_src, rel_type] * norm
        agg = jax.ops.segment_sum(msg, edge_dst, num_segments=h.shape[0])
        return jax.nn.relu(agg)

    def _L3_gnn_ref(x, edge_index, weight, bias, gamma, beta, running_mean, running_var):
        import jax, jax.numpy as jnp
        import numpy as np
        BN_EPS = 1e-05
        N = x.shape[0]
        xb = (x - running_mean) * jax.lax.rsqrt(running_var + BN_EPS) * gamma + beta
        loop = jnp.arange(N, dtype=edge_index.dtype)
        src = jnp.concatenate([edge_index[0], loop])
        dst = jnp.concatenate([edge_index[1], loop])
        deg = jax.ops.segment_sum(jnp.ones(src.shape[0], dtype=xb.dtype), dst, num_segments=N)
        dinv = jax.lax.rsqrt(deg)
        norm = dinv[src] * dinv[dst]
        h = xb @ weight
        msg = norm[:, None] * h[src]
        out = jax.ops.segment_sum(msg, dst, num_segments=N) + bias
        return jax.nn.relu(out)
    edge_index = jnp.stack([src, dst])
    h = jnp.maximum(_layernorm(x, axis=-1), 0.0)
    x = x + _L0_gnn_ref(h, edge_index, L0_gnn_W, L0_gnn_att_src, L0_gnn_att_dst, L0_gnn_bias, L0_gnn_gamma, L0_gnn_beta)
    h = jnp.maximum(_layernorm(x, axis=-1), 0.0)
    x = x + _L1_gnn_ref(h, edge_index, L1_gnn_weight, L1_gnn_att_src, L1_gnn_att_dst, L1_gnn_bias)
    h = jnp.maximum(_layernorm(x, axis=-1), 0.0)
    x = x + _L2_gnn_ref(h, L2_gnn_weight, edge_weight1, src, dst, edge_type_20)
    h = jnp.maximum(_layernorm(x, axis=-1), 0.0)
    x = x + _L3_gnn_ref(h, edge_index, L3_gnn_weight, L3_gnn_bias, L3_gnn_gamma, L3_gnn_beta, L3_gnn_running_mean, L3_gnn_running_var)
    return x

_drawn_inputs = setup_inputs


def setup_inputs(seed=0):
    import zlib

    import numpy as np

    out = dict(_drawn_inputs(seed))
    spreads = {'L0_gnn_gamma': (1.0, 0.2),
     'L0_gnn_beta': (0.0, 0.1),
     'L1_gnn_bias': (0.0, 0.1),
     'L3_gnn_gamma': (1.0, 0.6),
     'L3_gnn_beta': (0.0, 0.297),
     'L3_gnn_running_mean': (0.0, 0.311),
     'L3_gnn_running_var': (1.0, 0.6)}
    factors = {'L0_gnn_bias': 8.0, 'L1_gnn_att_src': 3.145, 'L3_gnn_bias': 8.0}
    for name, (base, spread) in spreads.items():
        noise = np.random.default_rng([zlib.crc32(name.encode()), seed]).standard_normal(out[name].shape)
        drawn = base * np.exp(spread * noise) if base else spread * noise
        out[name] = jnp.asarray(drawn.astype(out[name].dtype))
    for name, factor in factors.items():
        out[name] = (out[name] * factor).astype(out[name].dtype)
    return out
```

```python
from contextlib import ExitStack

import numpy as np

import concourse.bass as bass
from concourse import mybir
from concourse.alu_op_type import AluOpType as ALU

ACT = mybir.ActivationFunctionType
AX = mybir.AxisListType
F32 = mybir.dt.float32
I32 = mybir.dt.int32
U32 = mybir.dt.uint32

P = 128
N = 6250
D = 256
E = 100000
RELS = 20
NT = -(-N // P)
NPAD = NT * P
LAST = N - (NT - 1) * P
EP = 125
EC = E // EP
U = 8
EG = EC // U
ST = -(-((E + NT * (P - 1)) // P) // 16) * 16
SG = ST // U
PACK, PBITS = 4, 6
BIG = 1e30
EPS = 1e-5
assert EP * EC == E and EC % (4 * U) == 0 and ST % (2 * U) == 0 and NT < 1 << PBITS


def wait(eng, sem, value):
    if not (isinstance(value, int) and value <= 0):
        eng.wait_ge(sem, value)


def hold(eng, passed):
    eng.sem_inc(passed, 1)


def loop(eng, count, body):
    body(0)
    with eng.Fori(1, count) as i:
        body(i)


class Scope:

    def __init__(self, nc, ctx, name, last=False):
        self.nc, self.ctx, self.name, self.sems = nc, ctx, name, []
        if not last:
            ctx.callback(self.free_sems)

    def free_sems(self):
        if self.sems:
            self.nc.clear_and_free_semaphores(self.sems)
            self.nc.all_engine_barrier()

    def sb(self, name, shape, dt=F32):
        return self.ctx.enter_context(self.nc.sbuf_tensor(f"{self.name}_{name}", shape, dt))

    def psum(self, name, shape, dt=F32):
        return self.ctx.enter_context(self.nc.psum_tensor(f"{self.name}_{name}", shape, dt))

    def sem(self, name):
        self.sems.append(self.nc.alloc_semaphore(f"{self.name}_{name}"))
        return self.sems[-1]


def make_constants(nc, c):
    c.ident = c.sb("ident", [P, P])
    c.ones = c.sb("ones", [P, P])
    c.iota = c.sb("iota", [P, P])
    c.before = c.sb("before", [P, P])
    with ExitStack() as ctx:
        s = Scope(nc, ctx, "const")
        iota_i = s.sb("iota_i", [P, P], I32)
        filled = c.sem("filled")
        ready = c.ready = c.sem("ready")
        with nc.Block() as block:
            @block.gpsimd
            def _(pool):
                pool.memset(c.ident[:, :], 0.0).then_inc(filled, 1)
                pool.memset(c.ones[:, :], 1.0).then_inc(filled, 1)
                pool.memset(c.before[:, :], 1.0).then_inc(filled, 1)
                pool.iota(iota_i[:, :], pattern=[[1, P]], base=0, channel_multiplier=0).then_inc(ready, 1)
                pool.wait_ge(filled, 3)
                pool.affine_select(out=c.ident[:, :], in_=c.ident[:, :], compare_op=ALU.not_equal, fill=1.0,
                                   base=0, pattern=[[-1, P]], channel_multiplier=1).then_inc(ready, 1)
                pool.affine_select(out=c.before[:, :], in_=c.before[:, :], compare_op=ALU.is_gt, fill=0.0,
                                   base=0, pattern=[[1, P]], channel_multiplier=-1).then_inc(ready, 1)

            @block.vector
            def _(dve):
                dve.wait_ge(ready, 1)
                dve.tensor_copy(c.iota[:, :], iota_i[:, :]).then_inc(ready, 1)
                dve.wait_ge(ready, 4)


def sort_edges(nc, c, name, key_dram, fields, words, slots_dram, out):
    with ExitStack() as ctx:
        s = Scope(nc, ctx, name)
        key = s.sb("key", [EP, EC], I32)
        digit = s.sb("digit", [EP, EC], I32)
        hi = s.sb("hi", [EP, EC])
        lo = s.sb("lo", [EP, EC])
        pay = s.sb("pay", [EP, EC, words])
        slots = s.sb("slots", [P, ST, words])
        out.tile_f = s.sb("tile_f", [P, ST])
        hot_hi = s.sb("hot_hi", [EP, 4, U, NT])
        hot_lo = s.sb("hot_lo", [EP, 4, U, P])
        ps = s.psum("ps", [P, 8, 512])
        load_fields, emit_fields = fields(s)

        s_load, s_fill, s_init = s.sem("load"), s.sem("fill"), s.sem("init")
        s_prep = s.sem("prep")
        s_hot, s_counted = s.sem("hot"), s.sem("counted")
        s_base, s_mm = s.sem("base"), s.sem("base_mm")
        tiles_f = s.sb("tiles_f", [NT, 1])
        tiles_i = s.sb("tiles_i", [NT, 1], I32)
        total = s.sb("total", [NT, 1])
        base = s.sb("base", [NT, 1])
        first = s.sb("first", [NT, P])
        after = s.sb("after", [NT, P])
        reached = s.sb("reached", [NT, ST])
        iota_t = s.sb("iota_t", [NT, ST], I32)
        iota_tf = s.sb("iota_tf", [NT, ST])
        s_iota = s.sem("iota")
        hist = ps[0:NT, 0, 0:P]
        HALF = ST // 2
        packed = s.sb("packed", [1, ST // PACK])
        nload = load_fields(None)
        with nc.Block() as block:
            @block.sync
            def _(sp):
                sp.dma_start(key[:, :], key_dram.rearrange("(p c) -> p c", p=EP)).then_inc(s_load, 16)
                load_fields(sp, s_load)
                sp.wait_ge(s_fill, 2)
                sp.dma_start(slots_dram, slots[:, :, :]).then_inc(s_init, 16)
                sp.wait_ge(s_init, 16)

            @block.gpsimd
            def _(pool):
                pool.iota(iota_t[:, :], pattern=[[1, ST]], base=0, channel_multiplier=0).then_inc(s_iota, 1)
                pool.memset(slots[:, :, 0:words - 1], 0.0).then_inc(s_fill, 1)
                pool.memset(slots[:, :, words - 1:words], -1.0).then_inc(s_fill, 1)

            @block.vector
            def _(dve):
                done = [0]

                def link(ins):
                    done[0] += 1
                    ins.then_inc(s_prep, 1)
                    dve.wait_ge(s_prep, done[0])

                dve.wait_ge(s_load, 16 * (1 + nload))
                link(dve.tensor_scalar(digit[:, :], key[:, :], 7, None, ALU.arith_shift_right))
                link(dve.tensor_copy(hi[:, :], digit[:, :]))
                link(dve.tensor_scalar(digit[:, :], key[:, :], P - 1, None, ALU.bitwise_and))
                link(dve.tensor_copy(lo[:, :], digit[:, :]))
                link(dve.tensor_copy(pay[:, :, words - 1], key[:, :]))
                emit_fields(dve, link, pay)

                def hot(i):
                    for j in range(4):
                        g = i * 4 + j
                        wait(dve, s_counted, g - 3)
                        one_hot(dve, c, s_hot, hi, lo, hot_hi, hot_lo, g, j)

                loop(dve, EG // 4, hot)
                dve.wait_ge(s_counted, EG)

                def link(ins):
                    done[0] += 1
                    ins.then_inc(s_prep, 1)
                    dve.wait_ge(s_prep, done[0])

                link(dve.tensor_copy(out.count[:, :], hist))
                link(dve.tensor_reduce(total[:, :], out.count[:, :], AX.X, ALU.add))
                link(dve.tensor_scalar(tiles_f[:, :], total[:, :], float(P - 1), None, ALU.add))
                link(dve.tensor_copy(tiles_i[:, :], tiles_f[:, :]))
                link(dve.tensor_scalar(tiles_i[:, :], tiles_i[:, :], 7, None, ALU.arith_shift_right))
                dve.tensor_copy(tiles_f[:, :], tiles_i[:, :]).then_inc(s_base, 1)
                dve.wait_ge(s_mm, 1)
                link(dve.tensor_copy(base[:, :], ps[0:NT, 1, 0:1]))
                link(dve.tensor_tensor_scan(after[:, :], c.ones[0:NT, :], out.count[:, :], 0.0, ALU.mult, ALU.add))
                link(dve.tensor_tensor(first[:, :], after[:, :], out.count[:, :], ALU.subtract))
                link(dve.scalar_tensor_tensor(out=out.start[:, :], in0=base[:, :].to_broadcast([NT, P]), scalar=float(P),
                                              in1=first[:, :], op0=ALU.mult, op1=ALU.add))
                dve.wait_ge(s_iota, 1)
                link(dve.tensor_copy(iota_tf[:, :], iota_t[:, :]))
                dve.tensor_scalar(reached[:, :], iota_tf[:, :], base[:, 0:1], None, ALU.is_ge).then_inc(s_base, 1)
                dve.wait_ge(s_mm, 2)
                for h in range(2):
                    last = dve.tensor_scalar(out.tile_f[:, h * HALF:(h + 1) * HALF], ps[:, 2 + h, 0:HALF], -1.0, None,
                                             ALU.add)
                    link(last)
                nt4 = out.tile_f[0:1, :].rearrange("p (q k) -> p q k", k=PACK)
                link(dve.tensor_copy(packed[:, :], nt4[:, :, PACK - 1]))
                for k in reversed(range(PACK - 1)):
                    link(dve.scalar_tensor_tensor(out=packed[:, :], in0=packed[:, :], scalar=float(1 << PBITS),
                                                  in1=nt4[:, :, k], op0=ALU.mult, op1=ALU.add))
                link(dve.tensor_copy(out.tile_of[:, :], packed[:, :]))

            @block.tensor
            def _(pe):
                def count(i):
                    for j in range(4):
                        g = i * 4 + j
                        pe.wait_ge(s_hot, g * 2 + 2)
                        for u in range(U):
                            mm = pe.matmul(hist, hot_hi[:, j, u, :], hot_lo[:, j, u, :],
                                           start=isinstance(i, int) and g == 0 and u == 0, stop=False,
                                           skip_group_check=True)
                        mm.then_inc(s_counted, 1)

                loop(pe, EG // 4, count)
                pe.wait_ge(s_base, 1)
                pe.matmul(ps[0:NT, 1, 0:1], c.before[0:NT, 0:NT], tiles_f[:, :], start=True, stop=True).then_inc(s_mm, 1)
                pe.wait_ge(s_base, 2)
                for h in range(2):
                    mm = pe.matmul(ps[:, 2 + h, 0:HALF], c.ones[0:NT, :], reached[:, h * HALF:(h + 1) * HALF],
                                   start=True, stop=True)
                mm.then_inc(s_mm, 1)

        hot_hi_t = s.sb("hot_hi_t", [NT, 2, U, P])
        same = s.sb("same", [EP, 2, U, P])
        free_sb = s.sb("free_sb", [NT, 2, P])
        picked = s.sb("picked", [EP, U, P])
        pos = s.sb("pos", [EP, U])
        pos_i = s.sb("pos_i", [EP, U], I32)
        tile_i = s.sb("slot_tile_i", [EP, U], I32)
        tile_f = s.sb("slot_tile_f", [EP, U])
        row_f = s.sb("row_f", [EP, U])
        idx = s.sb("idx", [EP, 2, U], U32)
        stage = s.sb("stage", [EP, 2, U, words])
        tr = ps[:, 0:2, :].rearrange("p b (u e) -> p (b u) e", u=4)
        eq = ps[:, 2:4, :].rearrange("p b (u e) -> p (b u) e", u=4)
        look = ps[:, 4:6, :].rearrange("p b (u e) -> p (b u) e", u=4)
        free = ps[0:NT, 6, 0:P]
        s_hot2, s_tr, s_hot_t, s_eq, s_same = (s.sem(x) for x in ("hot2", "tr", "hot_t", "eq", "same"))
        s_upd, s_free, s_look, s_idx, s_stage = (s.sem(x) for x in ("upd", "free", "look", "idx", "stage"))
        s_step, s_passed = s.sem("step"), s.sem("passed")
        s_scat = [s.sem(f"scat{k}") for k in range(2)]
        STEPS = 6
        with nc.Block() as block:
            @block.vector
            def _(dve):
                def same_key(g, j):
                    wait(dve, s_eq, g + 1)
                    wait(dve, s_look, g - 1)
                    dve.tensor_tensor(same[:, j % 2, :, 0:EP], eq[0:EP, :, 0:EP],
                                      c.before[0:EP, 0:EP].unsqueeze(1).to_broadcast([EP, U, EP]), ALU.mult) \
                        .then_inc(s_same, 1)

                def place(g, j):
                    n = [0]

                    def link(ins):
                        n[0] += 1
                        ins.then_inc(s_step, 1)
                        dve.wait_ge(s_step, g * STEPS + n[0])

                    dve.wait_ge(s_look, g + 1)
                    link(dve.tensor_tensor(picked[:, :, :], look[0:EP, :, :], hot_lo[:, j % 4, :, :], ALU.mult))
                    link(dve.tensor_reduce(pos[:, :], picked[:, :, :], AX.X, ALU.add))
                    link(dve.tensor_copy(pos_i[:, :], pos[:, :]))
                    link(dve.tensor_scalar(tile_i[:, :], pos_i[:, :], 7, None, ALU.arith_shift_right))
                    link(dve.tensor_copy(tile_f[:, :], tile_i[:, :]))
                    link(dve.scalar_tensor_tensor(out=row_f[:, :], in0=tile_f[:, :], scalar=-float(P),
                                                  in1=pos[:, :], op0=ALU.mult, op1=ALU.add))
                    assert n[0] == STEPS
                    wait(dve, s_scat[j % 2], halves(g, j, 16 * U))
                    dve.scalar_tensor_tensor(out=idx[:, j % 2, :], in0=row_f[:, :], scalar=float(ST),
                                             in1=tile_f[:, :], op0=ALU.mult, op1=ALU.add).then_inc(s_idx, 1)

                def body(i):
                    for j in range(4):
                        g = i * 4 + j
                        wait(dve, s_look, g - 3)
                        one_hot(dve, c, s_hot2, hi, lo, hot_hi, hot_lo, g, j)
                        if not (isinstance(g, int) and g < 1):
                            same_key(g - 1, j - 1)
                        if not (isinstance(g, int) and g < 2):
                            place(g - 2, j - 2)

                loop(dve, EG // 4, body)
                same_key(EG - 1, 3)
                place(EG - 2, 2)
                place(EG - 1, 3)

            @block.tensor
            def _(pe):
                def lookup(g, j):
                    wait(pe, s_same, g + 1)
                    wait(pe, s_idx, g)
                    for u in range(U):
                        pe.wait_ge(s_free, g * U + u + 1)
                        pe.matmul(free, hot_hi[:, j % 4, u, :], hot_lo[:, j % 4, u, :], start=False, stop=False,
                                  skip_group_check=True).then_inc(s_upd, 1)
                        pe.matmul(look[0:EP, u, :], hot_hi_t[:, j % 2, u, 0:EP], free_sb[:, u % 2, :],
                                  start=True, stop=False, skip_group_check=True)
                        mm = pe.matmul(look[0:EP, u, :], same[:, j % 2, u, 0:EP], hot_lo[:, j % 4, u, :],
                                       start=False, stop=True, skip_group_check=True)
                    mm.then_inc(s_look, 1)

                def body(i):
                    for j in range(4):
                        g = i * 4 + j
                        pe.wait_ge(s_hot2, g * 2 + 2)
                        wait(pe, s_hot_t, g)
                        hold(pe, s_passed)
                        for u in range(U):
                            mm = pe.transpose(tr[0:NT, u, 0:EP], hot_hi[:, j, u, :], c.ident[0:EP, 0:EP])
                        mm.then_inc(s_tr, 1)
                        pe.wait_ge(s_hot_t, g + 1)
                        wait(pe, s_same, g)
                        for u in range(U):
                            mm = pe.matmul(eq[0:EP, u, 0:EP], hot_hi_t[:, j % 2, u, 0:EP], hot_hi_t[:, j % 2, u, 0:EP],
                                           start=True, stop=True)
                        mm.then_inc(s_eq, 1)
                        if not (isinstance(g, int) and g < 1):
                            lookup(g - 1, j - 1)

                pe.matmul(free, c.ident[0:NT, 0:NT], out.start[:, :], start=True, stop=False,
                          skip_group_check=True).then_inc(s_upd, 1)
                loop(pe, EG // 4, body)
                lookup(EG - 1, 3)

            @block.scalar
            def _(act):
                def free_copies(g, j):
                    for u in range(U):
                        act.wait_ge(s_upd, g * U + u + 1)
                        act.copy(free_sb[:, u % 2, :], free).then_inc(s_free, 1)

                def body(i):
                    for j in range(4):
                        g = i * 4 + j
                        act.wait_ge(s_tr, g + 1)
                        wait(act, s_look, g - 1)
                        act.copy(hot_hi_t[:, j % 2, :, 0:EP], tr[0:NT, :, 0:EP]).then_inc(s_hot_t, 1)
                        wait(act, s_scat[j % 2], halves(g, j, 16 * U))
                        act.copy(stage[:, j % 2, :, :], pay[:, bass.ds(g * U, U), :]) \
                            .then_inc(s_stage, 1)
                        if not (isinstance(g, int) and g < 1):
                            free_copies(g - 1, j - 1)

                loop(act, EG // 4, body)
                free_copies(EG - 1, 3)

            @block.gpsimd
            def _(pool):
                def body(i):
                    for j in range(4):
                        g = i * 4 + j
                        pool.wait_ge(s_idx, g + 1)
                        pool.wait_ge(s_stage, g + 1)
                        hold(pool, s_passed)
                        for u in range(U):
                            pool.indirect_dma_start(
                                slots_dram.rearrange("e t w -> (e t) w"),
                                bass.IndirectOffsetOnAxis(ap=idx[:, j % 2, u:u + 1], axis=0),
                                stage[:, j % 2, u, :], None).then_inc(s_scat[j % 2], 16)

                loop(pool, EG // 4, body)
                for k in range(2):
                    pool.wait_ge(s_scat[k], EG // 2 * 16 * U)

        s_back, s_split = s.sem("back"), s.sem("split")
        with nc.Block() as block:
            @block.sync
            def _(sp):
                sp.dma_start(slots[:, :, :], slots_dram).then_inc(s_back, 16)

            @block.vector
            def _(dve):
                dve.wait_ge(s_back, 16)
                for w, array in enumerate(out.words):
                    dve.tensor_copy(array[:, :], slots[:, :, w]).then_inc(s_split, 1)
                dve.scalar_tensor_tensor(out=out.row[:, :], in0=out.tile_f[:, :], scalar=-float(P),
                                         in1=slots[:, :, words - 1], op0=ALU.mult, op1=ALU.add).then_inc(s_split, 1)


def halves(g, j, each, more=0):
    return (g - (j & 1) + 2 * more) * (each // 2)


def one_hot(dve, c, s_hot, hi, lo, hot_hi, hot_lo, g, j):
    dve.tensor_tensor(hot_hi[:, j, :, :], c.iota[0:EP, 0:NT].unsqueeze(1).to_broadcast([EP, U, NT]),
                      hi[:, bass.ds(g * U, U)].unsqueeze(2).to_broadcast([EP, U, NT]), ALU.is_equal).then_inc(s_hot, 1)
    dve.tensor_tensor(hot_lo[:, j, :, :], c.iota[0:EP, 0:P].unsqueeze(1).to_broadcast([EP, U, P]),
                      lo[:, bass.ds(g * U, U)].unsqueeze(2).to_broadcast([EP, U, P]), ALU.is_equal).then_inc(s_hot, 1)


class Order:

    def __init__(self, c, name, words):
        self.words = [c.sb(f"{name}_{w}", [P, ST], dt) for w, dt in words]
        self.row = c.sb(f"{name}_row", [P, ST])
        self.start = c.sb(f"{name}_start", [NT, P])
        self.count = c.sb(f"{name}_count", [NT, P])
        self.tile_of = c.sb(f"{name}_tile_of", [1, ST // PACK], I32)


def dst_fields(src_dram, type_dram, norm_dram):
    def fields(s):
        src = s.sb("src", [EP, EC], I32)
        rel = s.sb("rel", [EP, EC], I32)
        norm = s.sb("norm", [EP, EC])

        def load(sp, sem=None):
            if sp is not None:
                sp.dma_start(src[:, :], src_dram.rearrange("(p c) -> p c", p=EP)).then_inc(sem, 16)
                sp.dma_start(rel[:, :], type_dram.rearrange("(p c) -> p c", p=EP)).then_inc(sem, 16)
                sp.dma_start(norm[:, :], norm_dram.rearrange("(p c) w -> p (c w)", p=EP)).then_inc(sem, 16)
            return 3

        def emit(dve, link, pay):
            link(dve.tensor_copy(pay[:, :, 0], src[:, :]))
            link(dve.scalar_tensor_tensor(out=pay[:, :, 1], in0=src[:, :],
                                          scalar=float(RELS), in1=rel[:, :], op0=ALU.mult, op1=ALU.add))
            link(dve.tensor_copy(pay[:, :, 2], norm[:, :]))
        return load, emit
    return fields


def src_fields(dst_dram):
    def fields(s):
        dst = s.sb("dst", [EP, EC], I32)

        def load(sp, sem=None):
            if sp is not None:
                sp.dma_start(dst[:, :], dst_dram.rearrange("(p c) -> p c", p=EP)).then_inc(sem, 16)
            return 1

        def emit(dve, link, pay):
            link(dve.tensor_copy(pay[:, :, 0], dst[:, :]))
        return load, emit
    return fields


def node_tiles(eng, body):
    def pair(i):
        body(2 * i, 0)
        body(2 * i + 1, 1)
    loop(eng, NT // 2, pair)
    if NT % 2:
        body(NT - 1, 0)


def groups4(eng, count, body):
    def four(i):
        for j in range(4):
            body(i * 4 + j, j)
    loop(eng, count // 4, four)


def started(g, lag):
    return not (isinstance(g, int) and g < lag)


class Chain:

    def __init__(self, eng, sem, base=0):
        self.eng, self.sem, self.base, self.n = eng, sem, base, 0

    def step(self, ins):
        self.n += 1
        ins.then_inc(self.sem, 1)
        self.eng.wait_ge(self.sem, self.base + self.n)


def load_nodes(nc, c, x_dram):
    s_zero, s_x = c.sem("x_zero"), c.sem("x")
    with nc.Block() as block:
        @block.gpsimd
        def _(pool):
            pool.memset(c.x[:, NT - 1, :], 0.0).then_inc(s_zero, 1)

        @block.sync
        def _(sp):
            sp.dma_start(c.x[:, 0:NT - 1, :], x_dram[0:(NT - 1) * P, :].rearrange("(t p) d -> p t d", p=P)).then_inc(s_x, 16)
            sp.wait_ge(s_zero, 1)
            sp.dma_start(c.x[0:LAST, NT - 1, :], x_dram[(NT - 1) * P:N, :]).then_inc(s_x, 16)
            sp.wait_ge(s_x, 32)


def layer_norm_stats(nc, c, name):
    with ExitStack() as ctx:
        s = Scope(nc, ctx, name)
        st = s.sb("stats", [P, NT, 6])
        mean = s.sb("mean", [P, NT])
        gap = s.sb("gap", [P, NT])
        var = s.sb("var", [P, NT])
        eps = s.sb("eps", [P, 1])
        std = s.sb("std", [P, NT])
        s_bn, s_step, s_var, s_std, s_end = (s.sem(x) for x in ("bn", "step", "var", "std", "end"))
        with nc.Block() as block:
            @block.vector
            def _(dve):
                dve.memset(eps[:, :], EPS).then_inc(s_bn, 1)
                loop(dve, NT, lambda i: dve.bn_stats(st[:, bass.ds(i, 1), :].rearrange("p a b -> p (a b)"),
                                                     c.x[:, bass.ds(i, 1), :].rearrange("p a b -> p (a b)"))
                     .then_inc(s_bn, 1))
                dve.wait_ge(s_bn, NT + 1)
                ch = Chain(dve, s_step)
                ch.step(dve.tensor_tensor(mean[:, :], st[:, :, 1], st[:, :, 4], ALU.add))
                ch.step(dve.tensor_tensor(gap[:, :], st[:, :, 1], st[:, :, 4], ALU.subtract))
                ch.step(dve.tensor_tensor(var[:, :], st[:, :, 2], st[:, :, 5], ALU.add))
                ch.step(dve.tensor_scalar(mean[:, :], mean[:, :], 0.5, None, ALU.mult))
                ch.step(dve.tensor_tensor(gap[:, :], gap[:, :], gap[:, :], ALU.mult))
                ch.step(dve.tensor_scalar(gap[:, :], gap[:, :], 0.25, None, ALU.mult))
                dve.scalar_tensor_tensor(out=var[:, :], in0=var[:, :], scalar=1.0 / D, in1=gap[:, :],
                                         op0=ALU.mult, op1=ALU.add).then_inc(s_var, 1)
                dve.wait_ge(s_std, 1)
                ch.step(dve.reciprocal(c.rstd[:, :], std[:, :]))
                dve.scalar_tensor_tensor(out=c.shift[:, :], in0=mean[:, :], scalar=-1.0, in1=c.rstd[:, :],
                                         op0=ALU.mult, op1=ALU.mult).then_inc(s_end, 1)

            @block.scalar
            def _(act):
                act.wait_ge(s_bn, 1)
                act.wait_ge(s_var, 1)
                act.activation(std[:, :], var[:, :], ACT.Sqrt, bias=eps[:, 0:1]).then_inc(s_std, 1)


def project(nc, c, name, w_dram, table_dram, att=None, heads=0, small_dram=None, add_h=False, affine=None,
            scale_rows=None, w_rearranged=False):
    with ExitStack() as ctx:
        s = Scope(nc, ctx, name)
        h = s.sb("h", [P, 2, D])
        h_t = s.sb("h_t", [P, 2, 2, P])
        rows = s.sb("rows", [P, 2, D])
        w = s.sb("w", [P, 2, D])
        ps = s.psum("ps", [P, 8, 512])
        s_w, s_h, s_tr, s_ht, s_mm, s_rows = (s.sem(x) for x in ("w", "h", "tr", "ht", "mm", "rows"))
        s_out = [s.sem(f"out{k}") for k in range(2)]
        s_prod, s_small, s_pre = s.sem("prod"), s.sem("small"), s.sem("pre")
        loads = [(w[:, :, :], w_dram if w_rearranged else w_dram.rearrange("(k p) n -> p k n", p=P))]
        if w_rearranged:
            loads = [(w[:, k, :].rearrange("p (h c) -> p h c", h=heads),
                      w_dram[:, k * P:(k + 1) * P, :].rearrange("h p c -> p h c")) for k in range(2)]
        if att is not None:
            vec = s.sb("vec", [P, 2, D])
            prod = s.sb("prod", [P, 2, D])
            loads += [(vec[:, i, :], att[i].partition_broadcast(P)) for i in range(2)]
        if affine is not None:
            cols = s.sb("cols", [P, 4, 2])
            eps = s.sb("eps", [P, 1])
            gain = s.sb("gain", [P, 2])
            loads += [(cols[:, i, :], a.rearrange("(k p) -> p k", p=P)) for i, a in enumerate(affine)]
        with nc.Block() as block:
            @block.sync
            def _(sp):
                for to, of in loads:
                    sp.dma_start(to, of, allow_slow_non_contiguous=affine is not None).then_inc(s_w, 16)

                def body(j, k):
                    sp.wait_ge(s_rows, j + 1)
                    sp.dma_start(table_dram[bass.ds(j * P, P), :], rows[:, k, :]).then_inc(s_out[k], 16)
                node_tiles(sp, body)
                if att is not None:
                    sp.wait_ge(s_prod, 2 * 2 * NT)
                    sp.dma_start(small_dram.rearrange("(t p) h -> p t h", p=P), c.att_g[:, :, 0:heads]) \
                        .then_inc(s_small, 16)
                    sp.wait_ge(s_small, 16)
                sp.wait_ge(s_out[0], 16 * (NT - NT // 2))
                sp.wait_ge(s_out[1], 16 * (NT // 2))

            @block.scalar
            def _(act):
                if affine is not None:
                    act.wait_ge(s_pre, 2)
                    act.activation(gain[:, :], cols[:, 3, :], ACT.Sqrt, bias=eps[:, 0:1]).then_inc(s_pre, 1)

                def body(j, k):
                    wait(act, s_tr, j - 1)
                    if add_h:
                        wait(act, s_rows, j - 1)
                    act.wait_ge(c.ready, 4)
                    act.activation(h[:, k, :], c.x[:, bass.ds(j, 1), :].rearrange("p a b -> p (a b)"), ACT.Relu,
                                   bias=c.shift[:, bass.ds(j, 1)], scale=c.rstd[:, bass.ds(j, 1)]).then_inc(s_h, 1)
                node_tiles(act, body)

            @block.tensor
            def _(pe):
                pe.wait_ge(s_w, 16 * len(loads))

                def body(j, k):
                    pe.wait_ge(s_h, j + 1)
                    wait(pe, s_ht, j - 1)
                    pe.wait_ge(c.ready, 4)
                    for half in range(2):
                        mm = pe.transpose(ps[:, k, half * P:(half + 1) * P], h[:, k, half * P:(half + 1) * P], c.ident[:, :])
                    mm.then_inc(s_tr, 1)
                    pe.wait_ge(s_ht, j + 1)
                    wait(pe, s_rows, j - 1)
                    for half in range(2):
                        mm = pe.matmul(ps[:, 2 + k, 0:D], h_t[:, k, half, :], w[:, half, :], start=half == 0, stop=half == 1)
                    mm.then_inc(s_mm, 1)
                node_tiles(pe, body)

            @block.vector
            def _(dve):
                if affine is not None:
                    ch = Chain(dve, s_pre)
                    ch.step(dve.memset(eps[:, :], EPS))
                    dve.wait_ge(s_w, 16 * len(loads))
                    ch.step(dve.tensor_copy(gain[:, :], cols[:, 3, :]))
                    dve.wait_ge(s_pre, 3)
                    ch.base = 1
                    ch.step(dve.reciprocal(gain[:, :], gain[:, :]))
                    ch.step(dve.tensor_tensor(gain[:, :], gain[:, :], cols[:, 0, :], ALU.mult))
                dve.wait_ge(s_w, 16 * len(loads))

                def body(j, k):
                    dve.wait_ge(s_tr, j + 1)
                    wait(dve, s_mm, j - 1)
                    if affine is None:
                        dve.tensor_copy(h_t[:, k, :, :], ps[:, k, 0:D].rearrange("p (a b) -> p a b", a=2)).then_inc(s_ht, 1)
                    else:
                        for half in range(2):
                            ch2 = Chain(dve, s_prod, j * 2 + half)
                            ch2.step(dve.tensor_scalar(h_t[:, k, half, :], ps[:, k, half * P:(half + 1) * P],
                                                       cols[:, 2, half:half + 1], gain[:, half:half + 1],
                                                       ALU.subtract, ALU.mult))
                            last = dve.tensor_scalar(h_t[:, k, half, :], h_t[:, k, half, :], cols[:, 1, half:half + 1], None,
                                                     ALU.add)
                        last.then_inc(s_ht, 1)
                    if add_h:
                        xj = c.x[:, bass.ds(j, 1), :].rearrange("p a b -> p (a b)")
                        dve.tensor_tensor(xj, xj, h[:, k, :], ALU.add)
                    dve.wait_ge(s_mm, j + 1)
                    wait(dve, s_out[k], halves(j, k, 16))
                    if scale_rows is not None:
                        dve.tensor_scalar(rows[:, k, :], ps[:, 2 + k, 0:D], scale_rows[:, bass.ds(j, 1)], None,
                                          ALU.mult).then_inc(s_rows, 1)
                    else:
                        dve.tensor_copy(rows[:, k, :], ps[:, 2 + k, 0:D]).then_inc(s_rows, 1)
                    if att is not None:
                        dve.wait_ge(s_rows, j + 1)
                        for i, to in enumerate((c.att_g, c.att_n)):
                            wait(dve, s_prod, j * 4 - 2 + i * 2 if i == 0 else j * 4)
                            dve.tensor_tensor(prod[:, i, :], rows[:, k, :], vec[:, i, :], ALU.mult).then_inc(s_prod, 1)
                            dve.wait_ge(s_prod, j * 4 + i * 2 + 1)
                            dve.tensor_reduce(to[:, bass.ds(j, 1), 0:heads].rearrange("p a h -> p (a h)"),
                                              prod[:, i, :].rearrange("p (h d) -> p h d", h=heads), AX.X, ALU.add) \
                                .then_inc(s_prod, 1)
                node_tiles(dve, body)


def segment_max(nc, c, name, order, gather_idx, heads, small_dram, gathered, carry_dram, carry2_dram, rows_dram):
    C = P // heads
    TB = ST // C
    L = TB * P
    with ExitStack() as ctx:
        s = Scope(nc, ctx, name)
        s_idx = [s.sem(f"idx{k}") for k in range(4)]
        s_gat = [s.sem(f"gat{k}") for k in range(4)]
        s_kept, s_passed = s.sem("kept"), s.sem("passed")
        with ExitStack() as ctx2:
            s2 = Scope(nc, ctx2, name + "g")
            idx = s2.sb("idx", [P, 4, U], U32)
            ring = s2.sb("ring", [P, 4, U, heads])
            with nc.Block() as block:
                @block.sync
                def _(sp):
                    def body(g, j):
                        wait(sp, s_gat[j], quarters(g, j, 16 * U))
                        sp.dma_start(idx[:, j, :], gather_idx[:, bass.ds(g * U, U)]).then_inc(s_idx[j], 16)
                    groups4(sp, SG, body)

                @block.gpsimd
                def _(pool):
                    def body(g, j):
                        pool.wait_ge(s_idx[j], quarters(g, j, 16, 1))
                        wait(pool, s_kept, g - 3)
                        hold(pool, s_passed)
                        for u in range(U):
                            pool.indirect_dma_start(ring[:, j, u, :], None, small_dram,
                                                    bass.IndirectOffsetOnAxis(ap=idx[:, j, u:u + 1], axis=0)) \
                                .then_inc(s_gat[j], 16)
                    groups4(pool, SG, body)

                @block.scalar
                def _(act):
                    def body(g, j):
                        act.wait_ge(s_gat[j], quarters(g, j, 16 * U, 1))
                        act.copy(gathered[:, bass.ds(g * U, U), 0:heads], ring[:, j, :, :]).then_inc(s_kept, 1)
                    groups4(act, SG, body)
                    act.wait_ge(s_kept, SG)

        key_t = s.sb("key_t", [P, TB, P])
        val_t = s.sb("val_t", [P, TB, P])
        new_t = s.sb("new_t", [P, TB, P])
        stage = s.sb("stage", [P, 2, 2, C, heads])
        ps = s.psum("ps", [P, 8, 512])
        s_st, s_tr, s_cp = s.sem("st"), s.sem("tr"), s.sem("cp")
        by_chunk = [order.key[:, :].rearrange("p (c b) -> p b c", c=C).unsqueeze(3).to_broadcast([P, TB, C, heads]),
                    gathered[:, :, 0:heads].rearrange("p (c b) h -> p b c h", c=C)]

        def batches(eng, body):
            loop(eng, TB // 2, lambda i: [body(i * 2 + k, k) for k in range(2)])

        with nc.Block() as block:
            @block.vector
            def _(dve):
                def body(b, k):
                    wait(dve, s_tr, (b - 1) * 2)
                    for i in range(2):
                        dve.tensor_copy(stage[:, k, i, :, :], by_chunk[i][:, bass.ds(b, 1), :, :].squeeze(1)) \
                            .then_inc(s_st, 1)
                batches(dve, body)

            @block.tensor
            def _(pe):
                def body(b, k):
                    pe.wait_ge(s_st, b * 2 + 2)
                    wait(pe, s_cp, (b - 1) * 2)
                    pe.wait_ge(c.ready, 4)
                    for i in range(2):
                        pe.transpose(ps[:, 2 * k + i, 0:P], stage[:, k, i, :, :].rearrange("p c h -> p (c h)"), c.ident[:, :]) \
                            .then_inc(s_tr, 1)
                batches(pe, body)

            @block.scalar
            def _(act):
                def body(b, k):
                    act.wait_ge(s_tr, b * 2 + 2)
                    for i, to in enumerate((key_t, val_t)):
                        act.copy(to[:, bass.ds(b, 1), :].rearrange("p a e -> p (a e)"), ps[:, 2 * k + i, 0:P]).then_inc(s_cp, 1)
                batches(act, body)
                act.wait_ge(s_cp, 2 * TB)

        key_l = key_t[:, :, :].rearrange("p b e -> p (b e)")
        val_l = val_t[:, :, :].rearrange("p b e -> p (b e)")
        new_l = new_t[:, :, :].rearrange("p b e -> p (b e)")
        ends = s.sb("ends", [P, 3])
        ch_in = s.sb("ch_in", [heads, C, 3])
        cont = s.sb("cont", [heads, C])
        whole = s.sb("whole", [heads, C])
        run = s.sb("run", [heads, C])
        carry = s.sb("carry", [heads, C, 2])
        carried = s.sb("carried", [P, 2])
        last_slot = s.sb("last_slot", [NT, P])
        slot_i = s.sb("slot_i", [NT, P], I32)
        tile_i = s.sb("tile_i", [NT, P], I32)
        tile_f = s.sb("tile_f", [NT, P])
        row_f = s.sb("row_f", [NT, P])
        back = s.sb("back", [P, 2, P])
        row_idx = s.sb("row_idx", [P, NT], U32)
        s_v, s_d, s_e, s_f = s.sem("v"), s.sem("d"), s.sem("e"), s.sem("f")
        s_t2, s_c2, s_b2, s_r = s.sem("t2"), s.sem("c2"), s.sem("b2"), s.sem("r")
        s_rows, s_max = s.sem("rows"), s.sem("max")
        back_e = val_t[:, :, :].rearrange("p b e -> p (b e)").rearrange("p (c b h) -> p b c h", c=C, h=heads)
        with nc.Block() as block:
            @block.sync
            def _(sp):
                sp.wait_ge(s_e, 1)
                sp.dma_start(carry_dram, ends[:, :]).then_inc(s_d, 16)
                sp.wait_ge(s_d, 16)
                sp.dma_start(ch_in[:, :, :], carry_dram.rearrange("(c h) k -> h c k", h=heads)).then_inc(s_d, 16)
                sp.wait_ge(s_e, 2)
                sp.dma_start(carry2_dram.rearrange("(c h) k -> h c k", h=heads), carry[:, :, :]).then_inc(s_d, 16)
                sp.wait_ge(s_d, 48)
                sp.dma_start(carried[:, :], carry2_dram).then_inc(s_d, 16)
                sp.wait_ge(s_c2, TB)
                sp.dma_start(rows_dram.rearrange("(e t) h -> e (t h)", e=P), val_l).then_inc(s_rows, 16)
                sp.wait_ge(s_rows, 16)

            @block.vector
            def _(dve):
                ch = Chain(dve, s_v)
                ch.step(dve.tensor_tensor(last_slot[:, :], order.start[:, :], order.count[:, :], ALU.add))
                ch.step(dve.tensor_scalar(last_slot[:, :], last_slot[:, :], -1.0, 0.0, ALU.add, ALU.max))
                ch.step(dve.tensor_copy(slot_i[:, :], last_slot[:, :]))
                ch.step(dve.tensor_scalar(tile_i[:, :], slot_i[:, :], 7, None, ALU.arith_shift_right))
                ch.step(dve.tensor_copy(tile_f[:, :], tile_i[:, :]))
                ch.step(dve.scalar_tensor_tensor(out=row_f[:, :], in0=tile_f[:, :], scalar=-float(P),
                                                 in1=last_slot[:, :], op0=ALU.mult, op1=ALU.add))
                dve.scalar_tensor_tensor(out=row_f[:, :], in0=row_f[:, :], scalar=float(ST),
                                         in1=tile_f[:, :], op0=ALU.mult, op1=ALU.add).then_inc(s_r, 1)
                dve.wait_ge(s_r, 1)
                ch.step(dve.tensor_tensor(new_l[:, 1:L], key_l[:, 1:L], key_l[:, 0:L - 1], ALU.not_equal))
                ch.step(dve.tensor_scalar(new_l[:, 1:L], new_l[:, 1:L], -BIG, None, ALU.mult))
                ch.step(dve.memset(new_l[:, 0:1], 0.0))
                ch.step(dve.tensor_copy(ends[:, 0:1], key_l[:, 0:1]))
                ch.step(dve.tensor_copy(ends[:, 1:2], key_l[:, L - 1:L]))
                ch.step(dve.tensor_tensor_scan(key_l, new_l, val_l, -BIG, ALU.add, ALU.max))
                dve.tensor_copy(ends[:, 2:3], key_l[:, L - 1:L]).then_inc(s_e, 1)
                dve.wait_ge(s_d, 32)
                ch.step(dve.tensor_tensor(cont[:, 1:C], ch_in[:, 1:C, 0], ch_in[:, 0:C - 1, 1], ALU.is_equal))
                ch.step(dve.memset(cont[:, 0:1], 0.0))
                ch.step(dve.tensor_tensor(whole[:, :], ch_in[:, :, 0], ch_in[:, :, 1], ALU.is_equal))
                ch.step(dve.tensor_tensor(whole[:, :], whole[:, :], cont[:, :], ALU.mult))
                ch.step(dve.tensor_scalar(whole[:, :], whole[:, :], 1.0, BIG, ALU.subtract, ALU.mult))
                ch.step(dve.tensor_tensor_scan(run[:, :], whole[:, :], ch_in[:, :, 2], -BIG, ALU.add, ALU.max))
                ch.step(dve.memset(carry[:, 0:1, 0:1], -BIG))
                ch.step(dve.tensor_copy(carry[:, 1:C, 0], run[:, 0:C - 1]))
                dve.tensor_scalar(carry[:, :, 1], cont[:, :], 1.0, BIG, ALU.subtract, ALU.mult).then_inc(s_e, 1)
                dve.wait_ge(s_d, 64)
                ch.step(dve.tensor_copy(new_l[:, 0:1], carried[:, 1:2]))
                dve.tensor_tensor_scan(key_l, new_l, val_l, carried[:, 0:1], ALU.add, ALU.max).then_inc(s_f, 1)
                dve.wait_ge(s_f, 1)

                def body(b, k):
                    wait(dve, s_t2, b - 1)
                    dve.tensor_copy(back[:, k, :], key_t[:, bass.ds(b, 1), :].rearrange("p a e -> p (a e)")).then_inc(s_b2, 1)
                batches(dve, body)
                dve.wait_ge(s_r, 2)
                dve.tensor_copy(row_idx[:, :], ps[:, 4, 0:NT]).then_inc(s_r, 1)
                dve.wait_ge(s_r, 3)

            @block.tensor
            def _(pe):
                pe.wait_ge(s_r, 1)
                pe.transpose(ps[:, 4, 0:NT], row_f[:, :], c.ident[0:NT, 0:NT]).then_inc(s_r, 1)

                def body(b, k):
                    pe.wait_ge(s_b2, b + 1)
                    wait(pe, s_c2, b - 1)
                    pe.wait_ge(c.ready, 4)
                    pe.transpose(ps[:, k, 0:P], back[:, k, :], c.ident[:, :]).then_inc(s_t2, 1)
                batches(pe, body)

            @block.scalar
            def _(act):
                act.wait_ge(s_f, 1)

                def body(b, k):
                    act.wait_ge(s_t2, b + 1)
                    act.copy(back_e[:, bass.ds(b, 1), :, :].squeeze(1),
                             ps[:, k, 0:P].rearrange("p (c h) -> p c h", c=C)).then_inc(s_c2, 1)
                batches(act, body)

        with nc.Block() as block:
            @block.gpsimd
            def _(pool):
                for t in range(NT):
                    pool.indirect_dma_start(c.seg_max[:, t, 0:heads], None, rows_dram,
                                            bass.IndirectOffsetOnAxis(ap=row_idx[:, t:t + 1], axis=0)).then_inc(s_max, 16)
                pool.wait_ge(s_max, 16 * NT)


def quarters(g, j, each, more=0):
    return (g - j + 4 * more) * (each // 4)


def count_columns(nc, c, name, order):
    with ExitStack() as ctx:
        s = Scope(nc, ctx, name)
        ps = s.psum("ps", [P, 512])
        s_t, s_c = s.sem("t"), s.sem("c")
        with nc.Block() as block:
            @block.tensor
            def _(pe):
                pe.transpose(ps[:, 0:NT], order.count[:, :], c.ident[0:NT, 0:NT]).then_inc(s_t, 1)

            @block.vector
            def _(dve):
                dve.wait_ge(s_t, 1)
                dve.tensor_copy(c.degree[:, :], ps[:, 0:NT]).then_inc(s_c, 1)
                dve.wait_ge(s_c, 1)


def attention_nodes(nc, c, name, heads, table_dram, loops):
    H = heads
    with ExitStack() as ctx:
        s = Scope(nc, ctx, name)
        z = s.sb("z", [P, NT, H])
        m = s.sb("m", [P, NT, H])
        has = s.sb("has", [P, NT])
        weight = s.sb("weight", [P, NT, H])
        s_x, s_v, s_z, s_w, s_end = (s.sem(a) for a in ("x", "v", "z", "w", "end"))
        with nc.Block() as block:
            @block.sync
            def _(sp):
                if loops:
                    sp.dma_start(c.acc[:, :, 0:D], table_dram.rearrange("(t p) d -> p t d", p=P)).then_inc(s_x, 16)

            @block.vector
            def _(dve):
                ch = Chain(dve, s_v)
                g, n = c.att_g[:, :, 0:H], c.att_n[:, :, 0:H]
                hb = has[:, :].unsqueeze(2).to_broadcast([P, NT, H])
                ch.step(dve.tensor_scalar(has[:, :], c.degree[:, :], 1.0, None, ALU.min))
                ch.step(dve.tensor_tensor(m[:, :, :], c.seg_max[:, :, 0:H], hb, ALU.mult))
                ch.step(dve.tensor_scalar(has[:, :], has[:, :], 1.0, BIG, ALU.subtract, ALU.mult))
                ch.step(dve.tensor_tensor(m[:, :, :], m[:, :, :], hb, ALU.add))
                if loops:
                    ch.step(dve.tensor_tensor(m[:, :, :], m[:, :, :], g, ALU.max))
                ch.step(dve.tensor_tensor(m[:, :, :], m[:, :, :], n, ALU.add))
                ch.step(dve.scalar_tensor_tensor(out=c.pair[:, :, H:2 * H], in0=m[:, :, :], scalar=0.2, in1=m[:, :, :],
                                                 op0=ALU.mult, op1=ALU.max))
                ch.step(dve.tensor_copy(c.pair[:, :, 0:H], n))
                if not loops:
                    dve.memset(c.acc[:, :, 0:D + H], 0.0).then_inc(s_end, 1)
                    dve.wait_ge(s_end, 1)
                    return
                ch.step(dve.tensor_tensor(z[:, :, :], g, n, ALU.add))
                ch.step(dve.scalar_tensor_tensor(out=z[:, :, :], in0=z[:, :, :], scalar=0.2, in1=z[:, :, :],
                                                 op0=ALU.mult, op1=ALU.max))
                dve.tensor_tensor(z[:, :, :], z[:, :, :], c.pair[:, :, H:2 * H], ALU.subtract).then_inc(s_z, 1)
                dve.wait_ge(s_w, 1)
                dve.wait_ge(s_x, 16)
                ch.step(dve.tensor_copy(c.acc[:, :, D:D + H], weight[:, :, :]))
                for t in range(0, NT, 7):
                    acc = c.acc[:, t:t + 7, 0:D].rearrange("p t (h d) -> p t h d", h=H)
                    dve.tensor_tensor(acc, acc, weight[:, t:t + 7, :].unsqueeze(3).to_broadcast([P, 7, H, D // H]),
                                      ALU.mult).then_inc(s_end, 1)
                dve.wait_ge(s_end, NT // 7)

            @block.scalar
            def _(act):
                if loops:
                    act.wait_ge(s_z, 1)
                    act.activation(weight[:, :, :], z[:, :, :], ACT.Exp).then_inc(s_w, 1)


def tile_registers(nc, eng, order, g):
    out = []
    for q in range(U // PACK):
        word = eng.value_load(order.tile_of[0:1, bass.ds(g * (U // PACK) + q, 1)], min_val=0, max_val=(1 << 24) - 1)
        out += [nc.s_assert_within((word >> (PBITS * k)) & ((1 << PBITS) - 1), 0, NT - 1, 
                                    skip_runtime_bounds_check_because="each field is a node tile by its making")
                for k in range(PACK)]
    return out


def gather_sum(nc, c, name, order, gather_idx, table_dram, heads=0, gathered=None, norm=None):
    H = heads
    W = D + H
    with ExitStack() as ctx:
        s = Scope(nc, ctx, name)
        idx = s.sb("idx", [P, 4, U], U32)
        rows = s.sb("rows", [P, 2, U, W])
        sel = s.sb("sel", [P, 2, U, P])
        ps = s.psum("ps", [P, 8, 512])
        s_idx = [s.sem(f"idx{k}") for k in range(4)]
        s_gat = [s.sem(f"gat{k}") for k in range(2)]
        s_sel, s_agg, s_acc, s_passed = (s.sem(x) for x in ("sel", "agg", "acc", "passed"))
        BANK0, BANKS = (3, 4) if H else (0, 8)
        if H:
            sel_t = s.sb("sel_t", [P, 2, U, P])
            z = s.sb("z", [P, U, H])
            y = s.sb("y", [P, U, H])
            s_tr, s_st, s_look, s_z, s_w, s_msg, s_v = (s.sem(x) for x in ("tr", "st", "look", "z", "w", "msg", "v"))
            tr = ps[:, 0:2, :].rearrange("p b (u e) -> p (b u) e", u=4)
            look = ps[:, 2, 0:U * 2 * H].rearrange("p (u h) -> p u h", u=U)
        with nc.Block() as block:
            @block.sync
            def _(sp):
                def body(g, j):
                    wait(sp, s_gat[j % 2], halves(g, j, 16 * U, -1) if started(g, 4) else 0)
                    sp.dma_start(idx[:, j, :], gather_idx[:, bass.ds(g * U, U)]).then_inc(s_idx[j], 16)
                groups4(sp, SG, body)

            @block.gpsimd
            def _(pool):
                def body(g, j):
                    pool.wait_ge(s_idx[j], quarters(g, j, 16, 1))
                    for u in range(U):
                        wait(pool, s_agg, g * U + u - 2 * U + 1 if started(g, 2) else 0)
                        hold(pool, s_passed)
                        pool.indirect_dma_start(rows[:, j % 2, u, 0:D], None, table_dram,
                                                bass.IndirectOffsetOnAxis(ap=idx[:, j, u:u + 1], axis=0)) \
                            .then_inc(s_gat[j % 2], 16)
                groups4(pool, SG, body)

            @block.vector
            def _(dve):
                def select(g, j):
                    wait(dve, s_agg, (g - 1) * U if started(g, 2) else 0)
                    row = order.row[:, bass.ds(g * U, U)]
                    if norm is None:
                        dve.tensor_tensor(sel[:, j % 2, :, :], c.iota[:, :].unsqueeze(1).to_broadcast([P, U, P]),
                                          row.unsqueeze(2).to_broadcast([P, U, P]), ALU.is_equal).then_inc(s_sel, 1)
                    else:
                        for u in range(U):
                            last = dve.tensor_scalar(sel[:, j % 2, u, :], c.iota[:, :],
                                                     order.row[:, bass.ds(g * U + u, 1)], norm[:, bass.ds(g * U + u, 1)],
                                                     ALU.is_equal, ALU.mult)
                        last.then_inc(s_sel, 1)

                def weigh(g, j):
                    ch = Chain(dve, s_v, g * 3)
                    dve.wait_ge(s_look, g + 1)
                    ch.step(dve.tensor_tensor(z[:, :, :], gathered[:, bass.ds(g * U, U), 0:H], look[:, :, 0:H], ALU.add))
                    ch.step(dve.scalar_tensor_tensor(out=y[:, :, :], in0=z[:, :, :], scalar=0.2, in1=z[:, :, :],
                                                     op0=ALU.mult, op1=ALU.max))
                    ch.step(dve.tensor_tensor(z[:, :, :], y[:, :, :], look[:, :, H:2 * H], ALU.subtract))
                    wait(dve, s_w, g)
                    dve.tensor_scalar(y[:, :, :], z[:, :, :], 0.0, None, ALU.min).then_inc(s_z, 1)
                    dve.wait_ge(s_w, g + 1)
                    dve.wait_ge(s_gat[j % 2], halves(g, j, 16 * U, 1))
                    for u in range(U):
                        r = rows[:, j % 2, u, 0:D].rearrange("p (h d) -> p h d", h=H)
                        dve.tensor_tensor(r, r, rows[:, j % 2, u, D:W].unsqueeze(2).to_broadcast([P, H, D // H]),
                                          ALU.mult).then_inc(s_msg, 1)

                def add(g, j):
                    regs = tile_registers(nc, dve, order, g)
                    for u in range(U):
                        t = g * U + u
                        wait(dve, s_acc, t)
                        dve.wait_ge(s_agg, t + 1)
                        acc = c.acc[:, bass.ds(regs[u], 1), 0:W].rearrange("p a d -> p (a d)")
                        dve.tensor_tensor(acc, acc, ps[:, BANK0 + u % BANKS, 0:W], ALU.add).then_inc(s_acc, 1)

                def body(g, j):
                    select(g, j)
                    if started(g, 1):
                        if H:
                            weigh(g - 1, j - 1)
                        add(g - 1, j - 1)
                groups4(dve, SG, body)
                if H:
                    weigh(SG - 1, 3)
                add(SG - 1, 3)
                dve.wait_ge(s_acc, ST)

            @block.tensor
            def _(pe):
                def lookup(g, j):
                    regs = tile_registers(nc, pe, order, g)
                    pe.wait_ge(s_sel, g + 1)
                    wait(pe, s_st, g)
                    pe.wait_ge(c.ready, 4)
                    for u in range(U):
                        mm = pe.transpose(tr[:, u, :], sel[:, j % 2, u, :], c.ident[:, :])
                    mm.then_inc(s_tr, 1)
                    pe.wait_ge(s_st, g + 1)
                    wait(pe, s_z, g)
                    for u in range(U):
                        mm = pe.matmul(look[:, u, :], sel_t[:, j % 2, u, :],
                                       c.pair[:, bass.ds(regs[u], 1), 0:2 * H].rearrange("p a h -> p (a h)"),
                                       start=True, stop=True)
                    mm.then_inc(s_look, 1)

                def sums(g, j):
                    if not H:
                        pe.wait_ge(s_sel, g + 1)
                        pe.wait_ge(s_gat[j % 2], halves(g, j, 16 * U, 1))
                    for u in range(U):
                        t = g * U + u
                        if H:
                            pe.wait_ge(s_msg, t + 1)
                        wait(pe, s_acc, t - BANKS + 1 if not (isinstance(t, int) and t < BANKS) else 0)
                        pe.matmul(ps[:, BANK0 + u % BANKS, 0:W], sel[:, j % 2, u, :], rows[:, j % 2, u, 0:W],
                                  start=True, stop=True).then_inc(s_agg, 1)

                def body(g, j):
                    if H:
                        lookup(g, j)
                        if started(g, 1):
                            sums(g - 1, j - 1)
                    else:
                        sums(g, j)
                groups4(pe, SG, body)
                if H:
                    sums(SG - 1, 3)

            if H:
                @block.scalar
                def _(act):
                    def weights(g, j):
                        act.wait_ge(s_z, g + 1)
                        wait(act, s_agg, (g - 1) * U if started(g, 2) else 0)
                        act.wait_ge(c.ready, 4)
                        act.activation(rows[:, j % 2, :, D:W], y[:, :, :], ACT.Exp).then_inc(s_w, 1)

                    def body(g, j):
                        act.wait_ge(s_tr, g + 1)
                        wait(act, s_look, g - 1)
                        act.copy(sel_t[:, j % 2, :, :], tr[:, :, :]).then_inc(s_st, 1)
                        if started(g, 1):
                            weights(g - 1, j - 1)
                    groups4(act, SG, body)
                    weights(SG - 1, 3)


def softmax_mean(nc, c, name, heads, bias_dram):
    H = heads
    with ExitStack() as ctx:
        s = Scope(nc, ctx, name)
        bias = s.sb("bias", [P, D])
        den = s.sb("den", [P, NT, H])
        s_b, s_v = s.sem("b"), s.sem("v")
        with nc.Block() as block:
            @block.sync
            def _(sp):
                sp.dma_start(bias[:, :], bias_dram.partition_broadcast(P)).then_inc(s_b, 16)

            @block.vector
            def _(dve):
                ch = Chain(dve, s_v)
                ch.step(dve.tensor_scalar(den[:, :, :], c.acc[:, :, D:D + H], 1e-16, None, ALU.max))
                ch.step(dve.reciprocal(den[:, :, :], den[:, :, :]))
                a4 = c.acc[:, :, 0:D].rearrange("p t (h d) -> p t h d", h=H)
                ch.step(dve.tensor_tensor(a4, a4, den[:, :, :].unsqueeze(3).to_broadcast([P, NT, H, D // H]), ALU.mult))
                dve.wait_ge(s_b, 16)
                ch.step(dve.tensor_tensor(c.acc[:, :, 0:D], c.acc[:, :, 0:D],
                                          bias[:, :].unsqueeze(1).to_broadcast([P, NT, D]), ALU.add))


def batch_norm_add(nc, c, name, gamma_dram, beta_dram):
    with ExitStack() as ctx:
        s = Scope(nc, ctx, name)
        gamma = s.sb("gamma", [P, D])
        beta = s.sb("beta", [P, D])
        mean = s.sb("mean", [P, D])
        std = s.sb("std", [P, D])
        eps = s.sb("eps", [P, 1])
        sq = s.sb("sq", [P, 2, D])
        ps = s.psum("ps", [P, 2, 512])
        s_b, s_v, s_sum, s_dev, s_sq, s_sq_mm, s_var, s_std = (
            s.sem(x) for x in ("b", "v", "sum", "dev", "sq", "sq_mm", "var", "std"))
        FULL = NT - 1

        with nc.Block() as block:
            @block.sync
            def _(sp):
                sp.dma_start(gamma[:, :], gamma_dram.partition_broadcast(P)).then_inc(s_b, 16)
                sp.dma_start(beta[:, :], beta_dram.partition_broadcast(P)).then_inc(s_b, 16)

            @block.tensor
            def _(pe):
                pe.matmul(ps[:, 0, 0:D], c.ones[0:LAST, :], c.acc[0:LAST, NT - 1, 0:D], start=True, stop=False,
                          skip_group_check=True)
                loop(pe, FULL, lambda i: pe.matmul(
                    ps[:, 0, 0:D], c.ones[:, :], c.acc[:, bass.ds(i, 1), 0:D].rearrange("p a d -> p (a d)"),
                    start=False, stop=False, skip_group_check=True).then_inc(s_sum, 1))

                def squares(j, k):
                    pe.wait_ge(s_sq, j + 1)
                    M = LAST if isinstance(j, int) and j == NT - 1 else P
                    pe.matmul(ps[:, 1, 0:D], c.ones[0:M, :], sq[0:M, k, :], start=isinstance(j, int) and j == 0,
                              stop=False, skip_group_check=True).then_inc(s_sq_mm, 1)
                node_tiles(pe, squares)

            @block.scalar
            def _(act):
                act.wait_ge(s_dev, 1)

                def squares(j, k):
                    wait(act, s_sq_mm, j - 1)
                    act.wait_ge(s_dev, 1)
                    act.activation(sq[:, k, :], c.acc[:, bass.ds(j, 1), 0:D].rearrange("p a d -> p (a d)"),
                                   ACT.Square).then_inc(s_sq, 1)
                node_tiles(act, squares)
                act.wait_ge(s_var, 1)
                act.activation(std[:, :], std[:, :], ACT.Sqrt, bias=eps[:, 0:1]).then_inc(s_std, 1)

            @block.vector
            def _(dve):
                ch = Chain(dve, s_v)
                acc = c.acc[:, :, 0:D]

                def rows(ap):
                    return ap[:, :].unsqueeze(1).to_broadcast([P, NT, D])
                ch.step(dve.memset(eps[:, :], EPS))
                dve.wait_ge(s_sum, FULL)
                ch.step(dve.tensor_scalar(mean[:, :], ps[:, 0, 0:D], 1.0 / N, None, ALU.mult))
                dve.tensor_tensor(acc, acc, rows(mean), ALU.subtract).then_inc(s_dev, 1)
                dve.wait_ge(s_sq_mm, NT)
                dve.tensor_scalar(std[:, :], ps[:, 1, 0:D], 1.0 / N, None, ALU.mult).then_inc(s_var, 1)
                dve.wait_ge(s_std, 1)
                dve.wait_ge(s_b, 32)
                ch.step(dve.reciprocal(std[:, :], std[:, :]))
                ch.step(dve.tensor_tensor(std[:, :], std[:, :], gamma[:, :], ALU.mult))
                dve.wait_ge(s_dev, 1)
                ch.step(dve.tensor_tensor(acc, acc, rows(std), ALU.mult))
                ch.step(dve.tensor_tensor(acc, acc, rows(beta), ALU.add))
                ch.step(dve.tensor_tensor(c.x[:, :, :], c.x[:, :, :], acc, ALU.add))


def add_nodes(nc, c, name, relu):
    with ExitStack() as ctx:
        s = Scope(nc, ctx, name)
        s_v = s.sem("v")
        with nc.Block() as block:
            @block.vector
            def _(dve):
                ch = Chain(dve, s_v)
                if relu:
                    ch.step(dve.scalar_tensor_tensor(out=c.x[:, :, :], in0=c.acc[:, :, 0:D], scalar=0.0, in1=c.x[:, :, :],
                                                     op0=ALU.max, op1=ALU.add))
                else:
                    ch.step(dve.tensor_tensor(c.x[:, :, :], c.x[:, :, :], c.acc[:, :, 0:D], ALU.add))


def start_acc(nc, c, name, table_dram=None):
    with ExitStack() as ctx:
        s = Scope(nc, ctx, name)
        s_v = s.sem("v")
        with nc.Block() as block:
            if table_dram is None:
                @block.vector
                def _(dve):
                    dve.memset(c.acc[:, :, 0:D], 0.0).then_inc(s_v, 16)
                    dve.wait_ge(s_v, 16)
            else:
                @block.sync
                def _(sp):
                    sp.dma_start(c.acc[:, :, 0:D], table_dram.rearrange("(t p) d -> p t d", p=P)).then_inc(s_v, 16)
                    sp.wait_ge(s_v, 16)


def relation_tables(nc, c, name, w_dram, table_dram):
    PAIRS = RELS // 2
    RING = 5
    with ExitStack() as ctx:
        s = Scope(nc, ctx, name)
        h = s.sb("h", [P, 2, D])
        h_t = s.sb("h_t", [P, 2, 2, P])
        w = s.sb("w", [P, 2, RELS * D])
        stage = s.sb("stage", [P, 2, RELS * D])
        ps = s.psum("ps", [P, 8, 512])
        s_w, s_h, s_tr, s_ht, s_mm = (s.sem(x) for x in ("w", "h", "tr", "ht", "mm"))
        s_even, s_odd = s.sem("even"), s.sem("odd")
        s_out = [s.sem(f"out{k}") for k in range(2)]
        with nc.Block() as block:
            @block.sync
            def _(sp):
                for half in range(2):
                    sp.dma_start(w[:, half, :].rearrange("p (r n) -> p r n", r=RELS),
                                 w_dram[:, half * P:(half + 1) * P, :].rearrange("r p n -> p r n")).then_inc(s_w, 16)

                def body(j, k):
                    sp.wait_ge(s_even, (j + 1) * (PAIRS // 2))
                    sp.wait_ge(s_odd, (j + 1) * (PAIRS // 2))
                    sp.dma_start(table_dram[bass.ds(j * P, P), :], stage[:, k, :]).then_inc(s_out[k], 16)
                node_tiles(sp, body)
                sp.wait_ge(s_out[0], 16 * (NT - NT // 2))
                sp.wait_ge(s_out[1], 16 * (NT // 2))

            def copies(eng, copy, parity, sem, j, k):
                wait(eng, s_out[k], halves(j, k, 16))
                for m in range(parity, PAIRS, 2):
                    eng.wait_ge(s_mm, j * PAIRS + m + 1)
                    copy(stage[:, k, m * 512:(m + 1) * 512], ps[:, 2 + m % RING, :]).then_inc(sem, 1)

            @block.scalar
            def _(act):
                def hidden(j, k):
                    wait(act, s_tr, j - 1)
                    act.wait_ge(c.ready, 4)
                    act.activation(h[:, k, :], c.x[:, bass.ds(j, 1), :].rearrange("p a b -> p (a b)"), ACT.Relu,
                                   bias=c.shift[:, bass.ds(j, 1)], scale=c.rstd[:, bass.ds(j, 1)]).then_inc(s_h, 1)

                def body(j, k):
                    if not isinstance(j, int):
                        hidden(j + 1, 1 - k)
                    elif j + 1 < NT:
                        hidden(j + 1, 1 - k)
                    copies(act, act.copy, 0, s_even, j, k)
                hidden(0, 0)
                node_tiles(act, body)

            @block.vector
            def _(dve):
                def turned(j, k):
                    dve.wait_ge(s_tr, j + 1)
                    wait(dve, s_mm, (j - 1) * PAIRS)
                    dve.tensor_copy(h_t[:, k, :, :], ps[:, k, 0:D].rearrange("p (a b) -> p a b", a=2)).then_inc(s_ht, 1)

                def body(j, k):
                    if not isinstance(j, int) or j + 1 < NT:
                        turned(j + 1, 1 - k)
                    copies(dve, dve.tensor_copy, 1, s_odd, j, k)
                turned(0, 0)
                node_tiles(dve, body)

            @block.tensor
            def _(pe):
                def turn(j, k):
                    pe.wait_ge(s_h, j + 1)
                    wait(pe, s_ht, j - 1)
                    pe.wait_ge(c.ready, 4)
                    for half in range(2):
                        mm = pe.transpose(ps[:, k, half * P:(half + 1) * P], h[:, k, half * P:(half + 1) * P], c.ident[:, :])
                    mm.then_inc(s_tr, 1)

                def body(j, k):
                    if not isinstance(j, int) or j + 1 < NT:
                        turn(j + 1, 1 - k)
                    pe.wait_ge(s_ht, j + 1)
                    for m in range(PAIRS):
                        before = m - RING
                        at = j if before >= 0 else j - 1
                        before %= PAIRS
                        wait(pe, s_odd if before % 2 else s_even,
                             at * (PAIRS // 2) + before // 2 + 1 if started(at, 0) and not (isinstance(at, int) and at < 0) else 0)
                        for half in range(2):
                            mm = pe.matmul(ps[:, 2 + m % RING, :], h_t[:, k, half, :], w[:, half, m * 512:(m + 1) * 512],
                                           start=half == 0, stop=half == 1)
                        mm.then_inc(s_mm, 1)
                pe.wait_ge(s_w, 32)
                turn(0, 0)
                node_tiles(pe, body)


def inverse_degrees(nc, c, name):
    with ExitStack() as ctx:
        s = Scope(nc, ctx, name)
        s_a, s_v = s.sem("a"), s.sem("v")
        with nc.Block() as block:
            @block.scalar
            def _(act):
                act.activation(c.dinv[:, :], c.degree[:, :], ACT.Sqrt, bias=c.ones[:, 0:1]).then_inc(s_a, 1)

            @block.vector
            def _(dve):
                dve.wait_ge(s_a, 1)
                dve.reciprocal(c.dinv[:, :], c.dinv[:, :]).then_inc(s_v, 1)
                dve.wait_ge(s_v, 1)


def finish(nc, c, name, bias_dram, out_dram):
    PARTS = 7
    with ExitStack() as ctx:
        s = Scope(nc, ctx, name, last=True)
        bias = s.sb("bias", [P, D])
        s_b, s_v, s_part, s_out = s.sem("b"), s.sem("v"), s.sem("part"), s.sem("out")
        with nc.Block() as block:
            @block.sync
            def _(sp):
                sp.dma_start(bias[:, :], bias_dram.partition_broadcast(P)).then_inc(s_b, 16)
                for i, t in enumerate(range(0, NT, PARTS)):
                    sp.wait_ge(s_part, i + 1)
                    full = min(t + PARTS, NT - 1)
                    sp.dma_start(out_dram[t * P:full * P, :].rearrange("(t p) d -> p t d", p=P), c.x[:, t:full, :]) \
                        .then_inc(s_out, 16)
                sp.dma_start(out_dram[(NT - 1) * P:N, :], c.x[0:LAST, NT - 1, :]).then_inc(s_out, 16)
                sp.wait_ge(s_out, 16 * (NT // PARTS + 1))

            @block.vector
            def _(dve):
                ch = Chain(dve, s_v)
                dve.wait_ge(s_b, 16)
                for t in range(0, NT, PARTS):
                    acc = c.acc[:, t:t + PARTS, 0:D]
                    x = c.x[:, t:t + PARTS, :]
                    ch.step(dve.tensor_tensor(acc, acc, c.dinv[:, t:t + PARTS].unsqueeze(2).to_broadcast([P, PARTS, D]),
                                              ALU.mult))
                    ch.step(dve.tensor_tensor(acc, acc, bias[:, :].unsqueeze(1).to_broadcast([P, PARTS, D]), ALU.add))
                    dve.scalar_tensor_tensor(out=x, in0=acc, scalar=0.0, in1=x, op0=ALU.max, op1=ALU.add) \
                        .then_inc(s_part, 1)


def gnn_kernel(nc, a, out_dram):
    def dram(name, shape):
        return nc.dram_tensor(name, shape, F32, kind="Internal").ap()

    slots_by_dst = dram("slots_by_dst", (P, ST, 4))
    slots_by_src = dram("slots_by_src", (P, ST, 2))
    rows0, rows1, rows3 = (dram(f"rows{i}", (NPAD, D)) for i in (0, 1, 3))
    rows2 = dram("rows2", (NPAD, RELS * D))
    with ExitStack() as ctx:
        c = Scope(nc, ctx, "c", last=True)
        make_constants(nc, c)
        by_dst = Order(c, "by_dst", (("src", U32), ("src_rel", U32), ("norm", F32), ("dst", F32)))
        by_dst.key = by_dst.words[3]
        by_src = Order(c, "by_src", (("dst", U32), ("src", F32)))
        by_src.key = by_src.words[1]
        c.x = c.sb("x", [P, NT, D])
        c.rstd = c.sb("rstd", [P, NT])
        c.shift = c.sb("shift", [P, NT])
        c.degree = c.sb("degree", [P, NT])
        c.dinv = c.sb("dinv", [P, NT])
        load_nodes(nc, c, a["x"])
        sort_edges(nc, c, "sort_dst", a["dst"], dst_fields(a["src"], a["edge_type_20"], a["edge_weight1"]), 4,
                   slots_by_dst, by_dst)
        sort_edges(nc, c, "sort_src", a["src"], src_fields(a["dst"]), 2, slots_by_src, by_src)

        for layer, heads, order, rows in ((0, 8, by_dst, rows0), (1, 4, by_src, rows1)):
            with ExitStack() as layer_ctx:
                s = Scope(nc, layer_ctx, f"layer{layer}")
                c.att_g = s.sb("att_g", [P, NT, heads])
                c.att_n = s.sb("att_n", [P, NT, heads])
                c.seg_max = s.sb("seg_max", [P, NT, heads])
                c.pair = s.sb("pair", [P, NT, 2 * heads])
                gathered = s.sb("gathered", [P, ST, heads])
                small = dram(f"small{layer}", (NPAD, heads))
                layer_norm_stats(nc, c, f"ln{layer}")
                if layer == 0:
                    att = [a[n].rearrange("h d -> (h d)") for n in ("L0_gnn_att_src", "L0_gnn_att_dst")]
                    project(nc, c, "proj0", a["L0_gnn_W"], rows, att, heads, small, add_h=True)
                else:
                    att = [a[n].rearrange("a h d -> (a h d)") for n in ("L1_gnn_att_dst", "L1_gnn_att_src")]
                    project(nc, c, "proj1", a["L1_gnn_weight"], rows, att, heads, small, w_rearranged=True)
                segment_max(nc, c, f"max{layer}", order, order.words[0], heads, small, gathered,
                            dram(f"ends{layer}", (P, 3)), dram(f"carry{layer}", (P, 2)),
                            dram(f"maxima{layer}", (P * ST, heads)))
                count_columns(nc, c, f"count{layer}", order)
                c.acc = s.sb("acc", [P, NT, D + heads])
                attention_nodes(nc, c, f"nodes{layer}", heads, rows, loops=layer == 0)
                gather_sum(nc, c, f"sum{layer}", order, order.words[0], rows, heads, gathered)
                softmax_mean(nc, c, f"mean{layer}", heads, a[f"L{layer}_gnn_bias"])
                if layer == 0:
                    batch_norm_add(nc, c, "bn0", a["L0_gnn_gamma"], a["L0_gnn_beta"])
                else:
                    add_nodes(nc, c, "add1", relu=False)

        layer_norm_stats(nc, c, "ln2")
        relation_tables(nc, c, "proj2", a["L2_gnn_weight"], rows2)
        c.acc = c.sb("acc", [P, NT, D])
        start_acc(nc, c, "start2")
        gather_sum(nc, c, "sum2", by_dst, by_dst.words[1], rows2.rearrange("n (r d) -> (n r) d", r=RELS),
                   norm=by_dst.words[2])
        add_nodes(nc, c, "add2", relu=True)

        layer_norm_stats(nc, c, "ln3")
        count_columns(nc, c, "count3", by_dst)
        inverse_degrees(nc, c, "deg3")
        project(nc, c, "proj3", a["L3_gnn_weight"], rows3, scale_rows=c.dinv,
                affine=[a[f"L3_gnn_{n}"] for n in ("gamma", "beta", "running_mean", "running_var")])
        start_acc(nc, c, "start3", rows3)
        gather_sum(nc, c, "sum3", by_dst, by_dst.words[0], rows3)
        finish(nc, c, "finish", a["L3_gnn_bias"], out_dram)


_INS = ["x", "src", "dst", "edge_type_20", "edge_weight1",
        "L0_gnn_W", "L0_gnn_att_src", "L0_gnn_att_dst", "L0_gnn_bias", "L0_gnn_gamma", "L0_gnn_beta",
        "L1_gnn_weight", "L1_gnn_att_src", "L1_gnn_att_dst", "L1_gnn_bias", "L2_gnn_weight",
        "L3_gnn_weight", "L3_gnn_bias", "L3_gnn_gamma", "L3_gnn_beta", "L3_gnn_running_mean", "L3_gnn_running_var"]


def kernel(**inputs):
    import concourse.bacc as bacc
    from concourse.bass_utils import run_bass_kernel_spmd

    nc = bacc.Bacc("TRN2", target_bir_lowering=False, num_devices=1)
    arrays, aps = {}, {}
    for name in _INS:
        array = np.ascontiguousarray(inputs[name])
        arrays[f"in_{name}"] = array
        aps[name] = nc.dram_tensor(f"in_{name}", array.shape, mybir.dt.from_np(array.dtype), kind="ExternalInput").ap()
    out = nc.dram_tensor("out_0", (N, D), F32, kind="ExternalOutput").ap()
    gnn_kernel(nc, aps, out)
    result = run_bass_kernel_spmd(nc, [arrays], core_ids=[0])
    return result.results[0]["out_0"]
```

```python
from contextlib import ExitStack

import numpy as np

import concourse.bass as bass
from concourse import mybir
from concourse.alu_op_type import AluOpType as ALU

ACT = mybir.ActivationFunctionType
AX = mybir.AxisListType
F32 = mybir.dt.float32
I32 = mybir.dt.int32
U32 = mybir.dt.uint32
F16 = mybir.dt.float16

P = 128
N = 6250
D = 256
E = 100000
RELS = 20
NT = -(-N // P)
NPAD = NT * P
LAST = N - (NT - 1) * P
EP = 125
EC = E // EP
U = 8
EG = EC // U
ST = -(-((E + NT * (P - 1)) // P) // 16) * 16
SG = ST // U
PACK, PBITS = 4, 6
BIG = 1e30
EPS = 1e-5
assert EP * EC == E and EC % (4 * U) == 0 and ST % (4 * U) == 0 and U == 2 * PACK and NT < 1 << PBITS


def wait(eng, sem, value):
    if not (isinstance(value, int) and value <= 0):
        eng.wait_ge(sem, value)


def hold(eng, passed):
    eng.sem_inc(passed, 1)


def loop(eng, count, body):
    body(0)
    with eng.Fori(1, count) as i:
        body(i)


class Scope:

    def __init__(self, nc, ctx, name, last=False):
        self.nc, self.ctx, self.name, self.sems = nc, ctx, name, []
        if not last:
            ctx.callback(self.free_sems)

    def free_sems(self):
        if self.sems:
            self.nc.clear_and_free_semaphores(self.sems)
            self.nc.all_engine_barrier()

    def sb(self, name, shape, dt=F32):
        return self.ctx.enter_context(self.nc.sbuf_tensor(f"{self.name}_{name}", shape, dt))

    def psum(self, name, shape, dt=F32):
        return self.ctx.enter_context(self.nc.psum_tensor(f"{self.name}_{name}", shape, dt))

    def sem(self, name):
        self.sems.append(self.nc.alloc_semaphore(f"{self.name}_{name}"))
        return self.sems[-1]


def make_constants(nc, c):
    c.ident = c.sb("ident", [P, P])
    c.ones = c.sb("ones", [P, P])
    c.iota = c.sb("iota", [P, P])
    c.before = c.sb("before", [P, P])
    c.ident16 = c.sb("ident16", [P, P], F16)
    with ExitStack() as ctx:
        s = Scope(nc, ctx, "const")
        iota_i = s.sb("iota_i", [P, P], I32)
        filled = c.sem("filled")
        ready = c.ready = c.sem("ready")
        with nc.Block() as block:
            @block.gpsimd
            def _(pool):
                pool.memset(c.ident[:, :], 0.0).then_inc(filled, 1)
                pool.memset(c.ones[:, :], 1.0).then_inc(filled, 1)
                pool.memset(c.before[:, :], 1.0).then_inc(filled, 1)
                pool.iota(iota_i[:, :], pattern=[[1, P]], base=0, channel_multiplier=0).then_inc(ready, 1)
                pool.wait_ge(filled, 3)
                pool.affine_select(out=c.ident[:, :], in_=c.ident[:, :], compare_op=ALU.not_equal, fill=1.0,
                                   base=0, pattern=[[-1, P]], channel_multiplier=1).then_inc(ready, 1)
                pool.affine_select(out=c.before[:, :], in_=c.before[:, :], compare_op=ALU.is_gt, fill=0.0,
                                   base=0, pattern=[[1, P]], channel_multiplier=-1).then_inc(ready, 1)

            @block.vector
            def _(dve):
                dve.wait_ge(ready, 1)
                dve.tensor_copy(c.iota[:, :], iota_i[:, :]).then_inc(ready, 1)
                dve.wait_ge(ready, 4)
                dve.tensor_copy(c.ident16[:, :], c.ident[:, :]).then_inc(ready, 1)
                dve.wait_ge(ready, 5)


def sort_edges(nc, c, name, key_dram, fields, words, slots_dram, out):
    with ExitStack() as ctx:
        s = Scope(nc, ctx, name)
        key = s.sb("key", [EP, EC], I32)
        digit = s.sb("digit", [EP, EC], I32)
        hi = s.sb("hi", [EP, EC])
        lo = s.sb("lo", [EP, EC])
        pay = s.sb("pay", [EP, EC, words])
        slots = s.sb("slots", [P, ST, words])
        out.tile_f = s.sb("tile_f", [P, ST])
        hot_hi = s.sb("hot_hi", [EP, 4, U, NT], F16)
        hot_lo = s.sb("hot_lo", [EP, 4, U, P], F16)
        ps = s.psum("ps", [P, 8, 512])
        load_fields, emit_fields = fields(s)

        s_load, s_fill, s_init = s.sem("load"), s.sem("fill"), s.sem("init")
        s_prep = s.sem("prep")
        s_hot, s_counted = s.sem("hot"), s.sem("counted")
        s_base, s_mm = s.sem("base"), s.sem("base_mm")
        tiles_f = s.sb("tiles_f", [NT, 1])
        tiles_i = s.sb("tiles_i", [NT, 1], I32)
        total = s.sb("total", [NT, 1])
        base = s.sb("base", [NT, 1])
        first = s.sb("first", [NT, P])
        after = s.sb("after", [NT, P])
        reached = s.sb("reached", [NT, ST])
        iota_t = s.sb("iota_t", [NT, ST], I32)
        iota_tf = s.sb("iota_tf", [NT, ST])
        s_iota = s.sem("iota")
        hist = ps[0:NT, 0, 0:P]
        HALF = ST // 2
        packed = s.sb("packed", [1, ST // PACK])
        nload = load_fields(None)
        with nc.Block() as block:
            @block.sync
            def _(sp):
                sp.dma_start(key[:, :], key_dram.rearrange("(p c) -> p c", p=EP)).then_inc(s_load, 16)
                load_fields(sp, s_load)
                sp.wait_ge(s_fill, 2)
                sp.dma_start(slots_dram, slots[:, :, :]).then_inc(s_init, 16)
                sp.wait_ge(s_init, 16)

            @block.gpsimd
            def _(pool):
                pool.iota(iota_t[:, :], pattern=[[1, ST]], base=0, channel_multiplier=0).then_inc(s_iota, 1)
                pool.memset(slots[:, :, 0:words - 1], 0.0).then_inc(s_fill, 1)
                pool.memset(slots[:, :, words - 1:words], -1.0).then_inc(s_fill, 1)

            @block.vector
            def _(dve):
                done = [0]

                def link(ins):
                    done[0] += 1
                    ins.then_inc(s_prep, 1)
                    dve.wait_ge(s_prep, done[0])

                dve.wait_ge(s_load, 16 * (1 + nload))
                link(dve.tensor_scalar(digit[:, :], key[:, :], 7, None, ALU.arith_shift_right))
                link(dve.tensor_copy(hi[:, :], digit[:, :]))
                link(dve.tensor_scalar(digit[:, :], key[:, :], P - 1, None, ALU.bitwise_and))
                link(dve.tensor_copy(lo[:, :], digit[:, :]))
                link(dve.tensor_copy(pay[:, :, words - 1], key[:, :]))
                emit_fields(dve, link, pay)

                def hot(i):
                    for j in range(4):
                        g = i * 4 + j
                        wait(dve, s_counted, g - 3)
                        one_hot(dve, c, s_hot, hi, lo, hot_hi, hot_lo, g, j)

                loop(dve, EG // 4, hot)
                dve.wait_ge(s_counted, EG)

                def link(ins):
                    done[0] += 1
                    ins.then_inc(s_prep, 1)
                    dve.wait_ge(s_prep, done[0])

                link(dve.tensor_copy(out.count[:, :], hist))
                link(dve.tensor_reduce(total[:, :], out.count[:, :], AX.X, ALU.add))
                link(dve.tensor_scalar(tiles_f[:, :], total[:, :], float(P - 1), None, ALU.add))
                link(dve.tensor_copy(tiles_i[:, :], tiles_f[:, :]))
                link(dve.tensor_scalar(tiles_i[:, :], tiles_i[:, :], 7, None, ALU.arith_shift_right))
                dve.tensor_copy(tiles_f[:, :], tiles_i[:, :]).then_inc(s_base, 1)
                dve.wait_ge(s_mm, 1)
                link(dve.tensor_copy(base[:, :], ps[0:NT, 1, 0:1]))
                link(dve.tensor_tensor_scan(after[:, :], c.ones[0:NT, :], out.count[:, :], 0.0, ALU.mult, ALU.add))
                link(dve.tensor_tensor(first[:, :], after[:, :], out.count[:, :], ALU.subtract))
                link(dve.scalar_tensor_tensor(out=out.start[:, :], in0=base[:, :].to_broadcast([NT, P]), scalar=float(P),
                                              in1=first[:, :], op0=ALU.mult, op1=ALU.add))
                dve.wait_ge(s_iota, 1)
                link(dve.tensor_copy(iota_tf[:, :], iota_t[:, :]))
                dve.tensor_scalar(reached[:, :], iota_tf[:, :], base[:, 0:1], None, ALU.is_ge).then_inc(s_base, 1)
                dve.wait_ge(s_mm, 2)
                for h in range(2):
                    last = dve.tensor_scalar(out.tile_f[:, h * HALF:(h + 1) * HALF], ps[:, 2 + h, 0:HALF], -1.0, None,
                                             ALU.add)
                    link(last)
                nt4 = out.tile_f[0:1, :].rearrange("p (q k) -> p q k", k=PACK)
                link(dve.tensor_copy(packed[:, :], nt4[:, :, PACK - 1]))
                for k in reversed(range(PACK - 1)):
                    link(dve.scalar_tensor_tensor(out=packed[:, :], in0=packed[:, :], scalar=float(1 << PBITS),
                                                  in1=nt4[:, :, k], op0=ALU.mult, op1=ALU.add))
                link(dve.tensor_copy(out.tile_of[:, :], packed[:, :]))

            @block.tensor
            def _(pe):
                def count(i):
                    for j in range(4):
                        g = i * 4 + j
                        pe.wait_ge(s_hot, g * 2 + 2)
                        for u in range(U):
                            mm = pe.matmul(hist, hot_hi[:, j, u, :], hot_lo[:, j, u, :],
                                           start=isinstance(i, int) and g == 0 and u == 0, stop=False,
                                           skip_group_check=True)
                        mm.then_inc(s_counted, 1)

                loop(pe, EG // 4, count)
                pe.wait_ge(s_base, 1)
                pe.matmul(ps[0:NT, 1, 0:1], c.before[0:NT, 0:NT], tiles_f[:, :], start=True, stop=True).then_inc(s_mm, 1)
                pe.wait_ge(s_base, 2)
                for h in range(2):
                    mm = pe.matmul(ps[:, 2 + h, 0:HALF], c.ones[0:NT, :], reached[:, h * HALF:(h + 1) * HALF],
                                   start=True, stop=True)
                mm.then_inc(s_mm, 1)

        assert U * EP <= 2048
        hot_hi_t = s.sb("hot_hi_t", [NT, 2, U, P])
        hot_hi_t16 = s.sb("hot_hi_t16", [NT, 2, U, P], F16)
        same = s.sb("same", [EP, 2, U, P], F16)
        free = s.sb("free", [NT, 2, P])
        earlier = s.sb("earlier", [NT, 2, U, P], F16)
        picked = s.sb("picked", [EP, U, P])
        pos = s.sb("pos", [EP, U])
        pos_i = s.sb("pos_i", [EP, U], I32)
        tile_i = s.sb("slot_tile_i", [EP, U], I32)
        tile_f = s.sb("slot_tile_f", [EP, U])
        row_f = s.sb("row_f", [EP, U])
        idx = s.sb("idx", [EP, 2, U], U32)
        stage = s.sb("stage", [EP, 2, U, words])
        tr = ps[:, 0, :].bitcast(F16).rearrange("p (u e) -> p u e", u=U)
        eq = ps[:, 1:3, :].rearrange("p b (u e) -> p (b u) e", u=4)
        look = ps[:, 3:5, :].rearrange("p b (u e) -> p (b u) e", u=4)
        prefix = ps[0:NT, 5:7, :].rearrange("p b (u e) -> p (b u) e", u=4)
        in_group = ps[0:NT, 7, 0:P]
        s_hot2, s_tr, s_hot_t, s_eq, s_same = (s.sem(x) for x in ("hot2", "tr", "hot_t", "eq", "same"))
        s_pre, s_free, s_early, s_look, s_idx, s_stage = (
            s.sem(x) for x in ("pre", "free", "early", "look", "idx", "stage"))
        s_step, s_passed = s.sem("step"), s.sem("passed")
        s_scat = [s.sem(f"scat{k}") for k in range(2)]
        STEPS = 6
        with nc.Block() as block:
            @block.vector
            def _(dve):
                def next_free(g, j):
                    if not started(g, 1):
                        dve.tensor_copy(free[:, 0, :], out.start[:, :]).then_inc(s_free, 1)
                        return
                    dve.wait_ge(s_pre, g)
                    dve.wait_ge(s_free, g)
                    wait(dve, s_look, g - 1)
                    dve.tensor_tensor(free[:, j % 2, :], free[:, (j + 1) % 2, :], in_group, ALU.add).then_inc(s_free, 1)

                def same_key(g, j):
                    wait(dve, s_eq, g + 1)
                    wait(dve, s_look, g - 1)
                    dve.tensor_tensor(same[:, j % 2, :, 0:EP], eq[0:EP, :, 0:EP],
                                      c.before[0:EP, 0:EP].unsqueeze(1).to_broadcast([EP, U, EP]), ALU.mult) \
                        .then_inc(s_same, 1)

                def place(g, j):
                    ch = Chain(dve, s_step, g * STEPS)
                    dve.wait_ge(s_look, g + 1)
                    ch.step(dve.tensor_tensor(picked[:, :, :], look[0:EP, :, :], hot_lo[:, j % 4, :, :], ALU.mult))
                    ch.step(dve.tensor_reduce(pos[:, :], picked[:, :, :], AX.X, ALU.add))
                    ch.step(dve.tensor_copy(pos_i[:, :], pos[:, :]))
                    ch.step(dve.tensor_scalar(tile_i[:, :], pos_i[:, :], 7, None, ALU.arith_shift_right))
                    ch.step(dve.tensor_copy(tile_f[:, :], tile_i[:, :]))
                    ch.step(dve.scalar_tensor_tensor(out=row_f[:, :], in0=tile_f[:, :], scalar=-float(P),
                                                     in1=pos[:, :], op0=ALU.mult, op1=ALU.add))
                    assert ch.n == STEPS
                    wait(dve, s_scat[j % 2], halves(g, j, 16 * U))
                    dve.scalar_tensor_tensor(out=idx[:, j % 2, :], in0=row_f[:, :], scalar=float(ST),
                                             in1=tile_f[:, :], op0=ALU.mult, op1=ALU.add).then_inc(s_idx, 1)

                def body(i):
                    for j in range(4):
                        g = i * 4 + j
                        wait(dve, s_look, g - 3)
                        one_hot(dve, c, s_hot2, hi, lo, hot_hi, hot_lo, g, j)
                        next_free(g, j)
                        if started(g, 1):
                            same_key(g - 1, j - 1)
                        if started(g, 2):
                            place(g - 2, j - 2)

                loop(dve, EG // 4, body)
                same_key(EG - 1, 3)
                place(EG - 2, 2)
                place(EG - 1, 3)

            @block.tensor
            def _(pe):
                def counts(g, j):
                    wait(pe, s_early, g)
                    wait(pe, s_free, g + 1 if started(g, 1) else 0)
                    for u in range(U):
                        for bank in range(2):
                            a, b = max(u + 1, 4 * bank), 4 * bank + 4
                            if a < b:
                                pe.matmul(prefix[:, a:b, :], hot_hi[:, j, u, :],
                                          hot_lo[:, j, u, :].unsqueeze(1).to_broadcast([EP, b - a, P]),
                                          start=u == 0, stop=False, skip_group_check=True)
                        mm = pe.matmul(in_group, hot_hi[:, j, u, :], hot_lo[:, j, u, :], start=u == 0, stop=False,
                                       skip_group_check=True)
                    mm.then_inc(s_pre, 1)

                def lookup(g, j):
                    wait(pe, s_same, g + 1)
                    wait(pe, s_early, g + 1)
                    wait(pe, s_free, g + 1)
                    wait(pe, s_idx, g)
                    for u in range(U):
                        pe.matmul(look[0:EP, u, :], hot_hi_t[:, j % 2, u, 0:EP], free[:, j % 2, :],
                                  start=True, stop=False, skip_group_check=True)
                        if u:
                            pe.matmul(look[0:EP, u, :], hot_hi_t16[:, j % 2, u, 0:EP], earlier[:, j % 2, u, :],
                                      start=False, stop=False, skip_group_check=True)
                        mm = pe.matmul(look[0:EP, u, :], same[:, j % 2, u, 0:EP], hot_lo[:, j % 4, u, :],
                                       start=False, stop=True, skip_group_check=True)
                    mm.then_inc(s_look, 1)

                def body(i):
                    for j in range(4):
                        g = i * 4 + j
                        pe.wait_ge(s_hot2, g * 2 + 2)
                        wait(pe, s_hot_t, g * 2)
                        hold(pe, s_passed)
                        for u in range(U):
                            mm = pe.transpose(tr[0:NT, u, 0:EP], hot_hi[:, j, u, :], c.ident16[0:EP, 0:EP])
                        mm.then_inc(s_tr, 1)
                        counts(g, j)
                        pe.wait_ge(s_hot_t, g * 2 + 2)
                        wait(pe, s_same, g)
                        for u in range(U):
                            mm = pe.matmul(eq[0:EP, u, 0:EP], hot_hi_t16[:, j % 2, u, 0:EP], hot_hi_t16[:, j % 2, u, 0:EP],
                                           start=True, stop=True)
                        mm.then_inc(s_eq, 1)
                        if started(g, 1):
                            lookup(g - 1, j - 1)

                loop(pe, EG // 4, body)
                lookup(EG - 1, 3)

            @block.scalar
            def _(act):
                def body(i):
                    for j in range(4):
                        g = i * 4 + j
                        act.wait_ge(s_tr, g + 1)
                        wait(act, s_look, g - 1)
                        act.copy(hot_hi_t16[:, j % 2, :, 0:EP], tr[0:NT, :, 0:EP]).then_inc(s_hot_t, 1)
                        act.copy(hot_hi_t[:, j % 2, :, 0:EP], tr[0:NT, :, 0:EP]).then_inc(s_hot_t, 1)
                        act.wait_ge(s_pre, g + 1)
                        act.copy(earlier[:, j % 2, 1:U, :], prefix[:, 1:U, :]).then_inc(s_early, 1)
                        wait(act, s_scat[j % 2], halves(g, j, 16 * U))
                        act.copy(stage[:, j % 2, :, :], pay[:, bass.ds(g * U, U), :]) \
                            .then_inc(s_stage, 1)

                loop(act, EG // 4, body)

            @block.gpsimd
            def _(pool):
                def body(i):
                    for j in range(4):
                        g = i * 4 + j
                        pool.wait_ge(s_idx, g + 1)
                        pool.wait_ge(s_stage, g + 1)
                        hold(pool, s_passed)
                        for u in range(U):
                            pool.indirect_dma_start(
                                slots_dram.rearrange("e t w -> (e t) w"),
                                bass.IndirectOffsetOnAxis(ap=idx[:, j % 2, u:u + 1], axis=0),
                                stage[:, j % 2, u, :], None).then_inc(s_scat[j % 2], 16)

                loop(pool, EG // 4, body)
                for k in range(2):
                    pool.wait_ge(s_scat[k], EG // 2 * 16 * U)

        s_back, s_split = s.sem("back"), s.sem("split")
        with nc.Block() as block:
            @block.sync
            def _(sp):
                sp.dma_start(slots[:, :, :], slots_dram).then_inc(s_back, 16)

            @block.vector
            def _(dve):
                dve.wait_ge(s_back, 16)
                for w, array in enumerate(out.words):
                    dve.tensor_copy(array[:, :], slots[:, :, w]).then_inc(s_split, 1)
                dve.scalar_tensor_tensor(out=out.row[:, :], in0=out.tile_f[:, :], scalar=-float(P),
                                         in1=slots[:, :, words - 1], op0=ALU.mult, op1=ALU.add).then_inc(s_split, 1)


def halves(g, j, each, more=0):
    return (g - (j & 1) + 2 * more) * (each // 2)


def one_hot(dve, c, s_hot, hi, lo, hot_hi, hot_lo, g, j):
    dve.tensor_tensor(hot_hi[:, j, :, :], c.iota[0:EP, 0:NT].unsqueeze(1).to_broadcast([EP, U, NT]),
                      hi[:, bass.ds(g * U, U)].unsqueeze(2).to_broadcast([EP, U, NT]), ALU.is_equal).then_inc(s_hot, 1)
    dve.tensor_tensor(hot_lo[:, j, :, :], c.iota[0:EP, 0:P].unsqueeze(1).to_broadcast([EP, U, P]),
                      lo[:, bass.ds(g * U, U)].unsqueeze(2).to_broadcast([EP, U, P]), ALU.is_equal).then_inc(s_hot, 1)


class Order:

    def __init__(self, c, name, words):
        self.words = [c.sb(f"{name}_{w}", [P, ST], dt) for w, dt in words]
        self.row = c.sb(f"{name}_row", [P, ST])
        self.start = c.sb(f"{name}_start", [NT, P])
        self.count = c.sb(f"{name}_count", [NT, P])
        self.tile_of = c.sb(f"{name}_tile_of", [1, ST // PACK], I32)


def dst_fields(src_dram, type_dram, norm_dram):
    def fields(s):
        src = s.sb("src", [EP, EC], I32)
        rel = s.sb("rel", [EP, EC], I32)
        norm = s.sb("norm", [EP, EC])

        def load(sp, sem=None):
            if sp is not None:
                sp.dma_start(src[:, :], src_dram.rearrange("(p c) -> p c", p=EP)).then_inc(sem, 16)
                sp.dma_start(rel[:, :], type_dram.rearrange("(p c) -> p c", p=EP)).then_inc(sem, 16)
                sp.dma_start(norm[:, :], norm_dram.rearrange("(p c) w -> p (c w)", p=EP)).then_inc(sem, 16)
            return 3

        def emit(dve, link, pay):
            link(dve.tensor_copy(pay[:, :, 0], src[:, :]))
            link(dve.scalar_tensor_tensor(out=pay[:, :, 1], in0=src[:, :],
                                          scalar=float(RELS), in1=rel[:, :], op0=ALU.mult, op1=ALU.add))
            link(dve.tensor_copy(pay[:, :, 2], norm[:, :]))
        return load, emit
    return fields


def src_fields(dst_dram):
    def fields(s):
        dst = s.sb("dst", [EP, EC], I32)

        def load(sp, sem=None):
            if sp is not None:
                sp.dma_start(dst[:, :], dst_dram.rearrange("(p c) -> p c", p=EP)).then_inc(sem, 16)
            return 1

        def emit(dve, link, pay):
            link(dve.tensor_copy(pay[:, :, 0], dst[:, :]))
        return load, emit
    return fields


def node_tiles(eng, body):
    def pair(i):
        body(2 * i, 0)
        body(2 * i + 1, 1)
    loop(eng, NT // 2, pair)
    if NT % 2:
        body(NT - 1, 0)


def groups4(eng, count, body):
    def four(i):
        for j in range(4):
            body(i * 4 + j, j)
    loop(eng, count // 4, four)


def started(g, lag):
    return not (isinstance(g, int) and g < lag)


class Chain:

    def __init__(self, eng, sem, base=0):
        self.eng, self.sem, self.base, self.n = eng, sem, base, 0

    def step(self, ins):
        self.n += 1
        ins.then_inc(self.sem, 1)
        self.eng.wait_ge(self.sem, self.base + self.n)


def load_nodes(nc, c, x_dram):
    s_zero, s_x = c.sem("x_zero"), c.sem("x")
    with nc.Block() as block:
        @block.gpsimd
        def _(pool):
            pool.memset(c.x[:, NT - 1, :], 0.0).then_inc(s_zero, 1)

        @block.sync
        def _(sp):
            sp.dma_start(c.x[:, 0:NT - 1, :], x_dram[0:(NT - 1) * P, :].rearrange("(t p) d -> p t d", p=P)).then_inc(s_x, 16)
            sp.wait_ge(s_zero, 1)
            sp.dma_start(c.x[0:LAST, NT - 1, :], x_dram[(NT - 1) * P:N, :]).then_inc(s_x, 16)
            sp.wait_ge(s_x, 32)


def layer_norm_stats(nc, c, name):
    with ExitStack() as ctx:
        s = Scope(nc, ctx, name)
        st = s.sb("stats", [P, NT, 6])
        mean = s.sb("mean", [P, NT])
        gap = s.sb("gap", [P, NT])
        var = s.sb("var", [P, NT])
        eps = s.sb("eps", [P, 1])
        std = s.sb("std", [P, NT])
        s_bn, s_step, s_var, s_std, s_end = (s.sem(x) for x in ("bn", "step", "var", "std", "end"))
        with nc.Block() as block:
            @block.vector
            def _(dve):
                dve.memset(eps[:, :], EPS).then_inc(s_bn, 1)
                loop(dve, NT, lambda i: dve.bn_stats(st[:, bass.ds(i, 1), :].rearrange("p a b -> p (a b)"),
                                                     c.x[:, bass.ds(i, 1), :].rearrange("p a b -> p (a b)"))
                     .then_inc(s_bn, 1))
                dve.wait_ge(s_bn, NT + 1)
                ch = Chain(dve, s_step)
                ch.step(dve.tensor_tensor(mean[:, :], st[:, :, 1], st[:, :, 4], ALU.add))
                ch.step(dve.tensor_tensor(gap[:, :], st[:, :, 1], st[:, :, 4], ALU.subtract))
                ch.step(dve.tensor_tensor(var[:, :], st[:, :, 2], st[:, :, 5], ALU.add))
                ch.step(dve.tensor_scalar(mean[:, :], mean[:, :], 0.5, None, ALU.mult))
                ch.step(dve.tensor_tensor(gap[:, :], gap[:, :], gap[:, :], ALU.mult))
                ch.step(dve.tensor_scalar(gap[:, :], gap[:, :], 0.25, None, ALU.mult))
                dve.scalar_tensor_tensor(out=var[:, :], in0=var[:, :], scalar=1.0 / D, in1=gap[:, :],
                                         op0=ALU.mult, op1=ALU.add).then_inc(s_var, 1)
                dve.wait_ge(s_std, 1)
                ch.step(dve.reciprocal(c.rstd[:, :], std[:, :]))
                dve.scalar_tensor_tensor(out=c.shift[:, :], in0=mean[:, :], scalar=-1.0, in1=c.rstd[:, :],
                                         op0=ALU.mult, op1=ALU.mult).then_inc(s_end, 1)

            @block.scalar
            def _(act):
                act.wait_ge(s_bn, 1)
                act.wait_ge(s_var, 1)
                act.activation(std[:, :], var[:, :], ACT.Sqrt, bias=eps[:, 0:1]).then_inc(s_std, 1)


def project(nc, c, name, w_dram, table_dram, att=None, heads=0, small_dram=None, add_h=False, affine=None,
            scale_rows=None, w_rearranged=False):
    with ExitStack() as ctx:
        s = Scope(nc, ctx, name)
        h = s.sb("h", [P, 2, D])
        h_t = s.sb("h_t", [P, 2, 2, P])
        rows = s.sb("rows", [P, 2, D])
        w = s.sb("w", [P, 2, D])
        ps = s.psum("ps", [P, 8, 512])
        s_w, s_h, s_tr, s_ht, s_mm, s_rows = (s.sem(x) for x in ("w", "h", "tr", "ht", "mm", "rows"))
        s_out = [s.sem(f"out{k}") for k in range(2)]
        s_prod, s_small, s_pre = s.sem("prod"), s.sem("small"), s.sem("pre")
        loads = [(w[:, :, :], w_dram if w_rearranged else w_dram.rearrange("(k p) n -> p k n", p=P))]
        if w_rearranged:
            loads = [(w[:, k, :].rearrange("p (h c) -> p h c", h=heads),
                      w_dram[:, k * P:(k + 1) * P, :].rearrange("h p c -> p h c")) for k in range(2)]
        if att is not None:
            vec = s.sb("vec", [P, 2, D])
            prod = s.sb("prod", [P, 2, D])
            loads += [(vec[:, i, :], att[i].partition_broadcast(P)) for i in range(2)]
        if affine is not None:
            cols = s.sb("cols", [P, 4, 2])
            eps = s.sb("eps", [P, 1])
            gain = s.sb("gain", [P, 2])
            loads += [(cols[:, i, :], a.rearrange("(k p) -> p k", p=P)) for i, a in enumerate(affine)]
        with nc.Block() as block:
            @block.sync
            def _(sp):
                for to, of in loads:
                    sp.dma_start(to, of, allow_slow_non_contiguous=affine is not None).then_inc(s_w, 16)

                def body(j, k):
                    sp.wait_ge(s_rows, j + 1)
                    sp.dma_start(table_dram[bass.ds(j * P, P), :], rows[:, k, :]).then_inc(s_out[k], 16)
                node_tiles(sp, body)
                if att is not None:
                    sp.wait_ge(s_prod, 2 * 2 * NT)
                    sp.dma_start(small_dram.rearrange("(t p) h -> p t h", p=P), c.att_g[:, :, 0:heads]) \
                        .then_inc(s_small, 16)
                    sp.wait_ge(s_small, 16)
                sp.wait_ge(s_out[0], 16 * (NT - NT // 2))
                sp.wait_ge(s_out[1], 16 * (NT // 2))

            @block.scalar
            def _(act):
                if affine is not None:
                    act.wait_ge(s_pre, 2)
                    act.activation(gain[:, :], cols[:, 3, :], ACT.Sqrt, bias=eps[:, 0:1]).then_inc(s_pre, 1)

                def body(j, k):
                    wait(act, s_tr, j - 1)
                    if add_h:
                        wait(act, s_rows, j - 1)
                    act.wait_ge(c.ready, 5)
                    act.activation(h[:, k, :], c.x[:, bass.ds(j, 1), :].rearrange("p a b -> p (a b)"), ACT.Relu,
                                   bias=c.shift[:, bass.ds(j, 1)], scale=c.rstd[:, bass.ds(j, 1)]).then_inc(s_h, 1)
                node_tiles(act, body)

            @block.tensor
            def _(pe):
                pe.wait_ge(s_w, 16 * len(loads))

                def body(j, k):
                    pe.wait_ge(s_h, j + 1)
                    wait(pe, s_ht, j - 1)
                    pe.wait_ge(c.ready, 5)
                    for half in range(2):
                        mm = pe.transpose(ps[:, k, half * P:(half + 1) * P], h[:, k, half * P:(half + 1) * P], c.ident[:, :])
                    mm.then_inc(s_tr, 1)
                    pe.wait_ge(s_ht, j + 1)
                    wait(pe, s_rows, j - 1)
                    for half in range(2):
                        mm = pe.matmul(ps[:, 2 + k, 0:D], h_t[:, k, half, :], w[:, half, :], start=half == 0, stop=half == 1)
                    mm.then_inc(s_mm, 1)
                node_tiles(pe, body)

            @block.vector
            def _(dve):
                if affine is not None:
                    ch = Chain(dve, s_pre)
                    ch.step(dve.memset(eps[:, :], EPS))
                    dve.wait_ge(s_w, 16 * len(loads))
                    ch.step(dve.tensor_copy(gain[:, :], cols[:, 3, :]))
                    dve.wait_ge(s_pre, 3)
                    ch.base = 1
                    ch.step(dve.reciprocal(gain[:, :], gain[:, :]))
                    ch.step(dve.tensor_tensor(gain[:, :], gain[:, :], cols[:, 0, :], ALU.mult))
                dve.wait_ge(s_w, 16 * len(loads))

                def body(j, k):
                    dve.wait_ge(s_tr, j + 1)
                    wait(dve, s_mm, j - 1)
                    if affine is None:
                        dve.tensor_copy(h_t[:, k, :, :], ps[:, k, 0:D].rearrange("p (a b) -> p a b", a=2)).then_inc(s_ht, 1)
                    else:
                        for half in range(2):
                            ch2 = Chain(dve, s_prod, j * 2 + half)
                            ch2.step(dve.tensor_scalar(h_t[:, k, half, :], ps[:, k, half * P:(half + 1) * P],
                                                       cols[:, 2, half:half + 1], gain[:, half:half + 1],
                                                       ALU.subtract, ALU.mult))
                            last = dve.tensor_scalar(h_t[:, k, half, :], h_t[:, k, half, :], cols[:, 1, half:half + 1], None,
                                                     ALU.add)
                        last.then_inc(s_ht, 1)
                    if add_h:
                        xj = c.x[:, bass.ds(j, 1), :].rearrange("p a b -> p (a b)")
                        dve.tensor_tensor(xj, xj, h[:, k, :], ALU.add)
                    dve.wait_ge(s_mm, j + 1)
                    wait(dve, s_out[k], halves(j, k, 16))
                    if scale_rows is not None:
                        dve.tensor_scalar(rows[:, k, :], ps[:, 2 + k, 0:D], scale_rows[:, bass.ds(j, 1)], None,
                                          ALU.mult).then_inc(s_rows, 1)
                    else:
                        dve.tensor_copy(rows[:, k, :], ps[:, 2 + k, 0:D]).then_inc(s_rows, 1)
                    if att is not None:
                        dve.wait_ge(s_rows, j + 1)
                        for i, to in enumerate((c.att_g, c.att_n)):
                            wait(dve, s_prod, j * 4 - 2 + i * 2 if i == 0 else j * 4)
                            dve.tensor_tensor(prod[:, i, :], rows[:, k, :], vec[:, i, :], ALU.mult).then_inc(s_prod, 1)
                            dve.wait_ge(s_prod, j * 4 + i * 2 + 1)
                            dve.tensor_reduce(to[:, bass.ds(j, 1), 0:heads].rearrange("p a h -> p (a h)"),
                                              prod[:, i, :].rearrange("p (h d) -> p h d", h=heads), AX.X, ALU.add) \
                                .then_inc(s_prod, 1)
                node_tiles(dve, body)


def segment_max(nc, c, name, order, gather_idx, heads, small_dram, gathered, carry_dram, carry2_dram, rows_dram):
    C = P // heads
    TB = ST // C
    L = TB * P
    with ExitStack() as ctx:
        s = Scope(nc, ctx, name)
        s_idx = [s.sem(f"idx{k}") for k in range(4)]
        s_gat = [s.sem(f"gat{k}") for k in range(4)]
        s_kept, s_passed = s.sem("kept"), s.sem("passed")
        with ExitStack() as ctx2:
            s2 = Scope(nc, ctx2, name + "g")
            idx = s2.sb("idx", [P, 4, U], U32)
            ring = s2.sb("ring", [P, 4, U, heads])
            with nc.Block() as block:
                @block.sync
                def _(sp):
                    def body(g, j):
                        wait(sp, s_gat[j], quarters(g, j, 16 * U))
                        sp.dma_start(idx[:, j, :], gather_idx[:, bass.ds(g * U, U)]).then_inc(s_idx[j], 16)
                    groups4(sp, SG, body)

                @block.gpsimd
                def _(pool):
                    def body(g, j):
                        pool.wait_ge(s_idx[j], quarters(g, j, 16, 1))
                        wait(pool, s_kept, g - 3)
                        hold(pool, s_passed)
                        for u in range(U):
                            pool.indirect_dma_start(ring[:, j, u, :], None, small_dram,
                                                    bass.IndirectOffsetOnAxis(ap=idx[:, j, u:u + 1], axis=0)) \
                                .then_inc(s_gat[j], 16)
                    groups4(pool, SG, body)

                @block.scalar
                def _(act):
                    def body(g, j):
                        act.wait_ge(s_gat[j], quarters(g, j, 16 * U, 1))
                        act.copy(gathered[:, bass.ds(g * U, U), 0:heads], ring[:, j, :, :]).then_inc(s_kept, 1)
                    groups4(act, SG, body)
                    act.wait_ge(s_kept, SG)

        key_t = s.sb("key_t", [P, TB, P])
        val_t = s.sb("val_t", [P, TB, P])
        new_t = s.sb("new_t", [P, TB, P])
        stage = s.sb("stage", [P, 2, 2, C, heads])
        ps = s.psum("ps", [P, 8, 512])
        s_st, s_tr, s_cp = s.sem("st"), s.sem("tr"), s.sem("cp")
        by_chunk = [order.key[:, :].rearrange("p (c b) -> p b c", c=C).unsqueeze(3).to_broadcast([P, TB, C, heads]),
                    gathered[:, :, 0:heads].rearrange("p (c b) h -> p b c h", c=C)]

        def batches(eng, body):
            loop(eng, TB // 2, lambda i: [body(i * 2 + k, k) for k in range(2)])

        with nc.Block() as block:
            @block.vector
            def _(dve):
                def body(b, k):
                    wait(dve, s_tr, (b - 1) * 2)
                    for i in range(2):
                        dve.tensor_copy(stage[:, k, i, :, :], by_chunk[i][:, bass.ds(b, 1), :, :].squeeze(1)) \
                            .then_inc(s_st, 1)
                batches(dve, body)

            @block.tensor
            def _(pe):
                def body(b, k):
                    pe.wait_ge(s_st, b * 2 + 2)
                    wait(pe, s_cp, (b - 1) * 2)
                    pe.wait_ge(c.ready, 5)
                    for i in range(2):
                        pe.transpose(ps[:, 2 * k + i, 0:P], stage[:, k, i, :, :].rearrange("p c h -> p (c h)"), c.ident[:, :]) \
                            .then_inc(s_tr, 1)
                batches(pe, body)

            @block.scalar
            def _(act):
                def body(b, k):
                    act.wait_ge(s_tr, b * 2 + 2)
                    for i, to in enumerate((key_t, val_t)):
                        act.copy(to[:, bass.ds(b, 1), :].rearrange("p a e -> p (a e)"), ps[:, 2 * k + i, 0:P]).then_inc(s_cp, 1)
                batches(act, body)
                act.wait_ge(s_cp, 2 * TB)

        key_l = key_t[:, :, :].rearrange("p b e -> p (b e)")
        val_l = val_t[:, :, :].rearrange("p b e -> p (b e)")
        new_l = new_t[:, :, :].rearrange("p b e -> p (b e)")
        ends = s.sb("ends", [P, 3])
        ch_in = s.sb("ch_in", [heads, C, 3])
        cont = s.sb("cont", [heads, C])
        whole = s.sb("whole", [heads, C])
        run = s.sb("run", [heads, C])
        carry = s.sb("carry", [heads, C, 2])
        carried = s.sb("carried", [P, 2])
        last_slot = s.sb("last_slot", [NT, P])
        slot_i = s.sb("slot_i", [NT, P], I32)
        tile_i = s.sb("tile_i", [NT, P], I32)
        tile_f = s.sb("tile_f", [NT, P])
        row_f = s.sb("row_f", [NT, P])
        back = s.sb("back", [P, 2, P])
        row_idx = s.sb("row_idx", [P, NT], U32)
        s_v, s_d, s_e, s_f = s.sem("v"), s.sem("d"), s.sem("e"), s.sem("f")
        s_t2, s_c2, s_b2, s_r = s.sem("t2"), s.sem("c2"), s.sem("b2"), s.sem("r")
        s_rows, s_max = s.sem("rows"), s.sem("max")
        back_e = val_t[:, :, :].rearrange("p b e -> p (b e)").rearrange("p (c b h) -> p b c h", c=C, h=heads)
        with nc.Block() as block:
            @block.sync
            def _(sp):
                sp.wait_ge(s_e, 1)
                sp.dma_start(carry_dram, ends[:, :]).then_inc(s_d, 16)
                sp.wait_ge(s_d, 16)
                sp.dma_start(ch_in[:, :, :], carry_dram.rearrange("(c h) k -> h c k", h=heads)).then_inc(s_d, 16)
                sp.wait_ge(s_e, 2)
                sp.dma_start(carry2_dram.rearrange("(c h) k -> h c k", h=heads), carry[:, :, :]).then_inc(s_d, 16)
                sp.wait_ge(s_d, 48)
                sp.dma_start(carried[:, :], carry2_dram).then_inc(s_d, 16)
                sp.wait_ge(s_c2, TB)
                sp.dma_start(rows_dram.rearrange("(e t) h -> e (t h)", e=P), val_l).then_inc(s_rows, 16)
                sp.wait_ge(s_rows, 16)

            @block.vector
            def _(dve):
                ch = Chain(dve, s_v)
                ch.step(dve.tensor_tensor(last_slot[:, :], order.start[:, :], order.count[:, :], ALU.add))
                ch.step(dve.tensor_scalar(last_slot[:, :], last_slot[:, :], -1.0, 0.0, ALU.add, ALU.max))
                ch.step(dve.tensor_copy(slot_i[:, :], last_slot[:, :]))
                ch.step(dve.tensor_scalar(tile_i[:, :], slot_i[:, :], 7, None, ALU.arith_shift_right))
                ch.step(dve.tensor_copy(tile_f[:, :], tile_i[:, :]))
                ch.step(dve.scalar_tensor_tensor(out=row_f[:, :], in0=tile_f[:, :], scalar=-float(P),
                                                 in1=last_slot[:, :], op0=ALU.mult, op1=ALU.add))
                dve.scalar_tensor_tensor(out=row_f[:, :], in0=row_f[:, :], scalar=float(ST),
                                         in1=tile_f[:, :], op0=ALU.mult, op1=ALU.add).then_inc(s_r, 1)
                dve.wait_ge(s_r, 1)
                ch.step(dve.tensor_tensor(new_l[:, 1:L], key_l[:, 1:L], key_l[:, 0:L - 1], ALU.not_equal))
                ch.step(dve.tensor_scalar(new_l[:, 1:L], new_l[:, 1:L], -BIG, None, ALU.mult))
                ch.step(dve.memset(new_l[:, 0:1], 0.0))
                ch.step(dve.tensor_copy(ends[:, 0:1], key_l[:, 0:1]))
                ch.step(dve.tensor_copy(ends[:, 1:2], key_l[:, L - 1:L]))
                ch.step(dve.tensor_tensor_scan(key_l, new_l, val_l, -BIG, ALU.add, ALU.max))
                dve.tensor_copy(ends[:, 2:3], key_l[:, L - 1:L]).then_inc(s_e, 1)
                dve.wait_ge(s_d, 32)
                ch.step(dve.tensor_tensor(cont[:, 1:C], ch_in[:, 1:C, 0], ch_in[:, 0:C - 1, 1], ALU.is_equal))
                ch.step(dve.memset(cont[:, 0:1], 0.0))
                ch.step(dve.tensor_tensor(whole[:, :], ch_in[:, :, 0], ch_in[:, :, 1], ALU.is_equal))
                ch.step(dve.tensor_tensor(whole[:, :], whole[:, :], cont[:, :], ALU.mult))
                ch.step(dve.tensor_scalar(whole[:, :], whole[:, :], 1.0, BIG, ALU.subtract, ALU.mult))
                ch.step(dve.tensor_tensor_scan(run[:, :], whole[:, :], ch_in[:, :, 2], -BIG, ALU.add, ALU.max))
                ch.step(dve.memset(carry[:, 0:1, 0:1], -BIG))
                ch.step(dve.tensor_copy(carry[:, 1:C, 0], run[:, 0:C - 1]))
                dve.tensor_scalar(carry[:, :, 1], cont[:, :], 1.0, BIG, ALU.subtract, ALU.mult).then_inc(s_e, 1)
                dve.wait_ge(s_d, 64)
                ch.step(dve.tensor_copy(new_l[:, 0:1], carried[:, 1:2]))
                dve.tensor_tensor_scan(key_l, new_l, val_l, carried[:, 0:1], ALU.add, ALU.max).then_inc(s_f, 1)
                dve.wait_ge(s_f, 1)

                def body(b, k):
                    wait(dve, s_t2, b - 1)
                    dve.tensor_copy(back[:, k, :], key_t[:, bass.ds(b, 1), :].rearrange("p a e -> p (a e)")).then_inc(s_b2, 1)
                batches(dve, body)
                dve.wait_ge(s_r, 2)
                dve.tensor_copy(row_idx[:, :], ps[:, 4, 0:NT]).then_inc(s_r, 1)
                dve.wait_ge(s_r, 3)

            @block.tensor
            def _(pe):
                pe.wait_ge(s_r, 1)
                pe.transpose(ps[:, 4, 0:NT], row_f[:, :], c.ident[0:NT, 0:NT]).then_inc(s_r, 1)

                def body(b, k):
                    pe.wait_ge(s_b2, b + 1)
                    wait(pe, s_c2, b - 1)
                    pe.wait_ge(c.ready, 5)
                    pe.transpose(ps[:, k, 0:P], back[:, k, :], c.ident[:, :]).then_inc(s_t2, 1)
                batches(pe, body)

            @block.scalar
            def _(act):
                act.wait_ge(s_f, 1)

                def body(b, k):
                    act.wait_ge(s_t2, b + 1)
                    act.copy(back_e[:, bass.ds(b, 1), :, :].squeeze(1),
                             ps[:, k, 0:P].rearrange("p (c h) -> p c h", c=C)).then_inc(s_c2, 1)
                batches(act, body)

        with nc.Block() as block:
            @block.gpsimd
            def _(pool):
                for t in range(NT):
                    pool.indirect_dma_start(c.seg_max[:, t, 0:heads], None, rows_dram,
                                            bass.IndirectOffsetOnAxis(ap=row_idx[:, t:t + 1], axis=0)).then_inc(s_max, 16)
                pool.wait_ge(s_max, 16 * NT)


def quarters(g, j, each, more=0):
    return (g - j + 4 * more) * (each // 4)


def count_columns(nc, c, name, order):
    with ExitStack() as ctx:
        s = Scope(nc, ctx, name)
        ps = s.psum("ps", [P, 512])
        s_t, s_c = s.sem("t"), s.sem("c")
        with nc.Block() as block:
            @block.tensor
            def _(pe):
                pe.transpose(ps[:, 0:NT], order.count[:, :], c.ident[0:NT, 0:NT]).then_inc(s_t, 1)

            @block.vector
            def _(dve):
                dve.wait_ge(s_t, 1)
                dve.tensor_copy(c.degree[:, :], ps[:, 0:NT]).then_inc(s_c, 1)
                dve.wait_ge(s_c, 1)


def attention_nodes(nc, c, name, heads, table_dram, loops):
    H = heads
    with ExitStack() as ctx:
        s = Scope(nc, ctx, name)
        z = s.sb("z", [P, NT, H])
        m = s.sb("m", [P, NT, H])
        has = s.sb("has", [P, NT])
        weight = s.sb("weight", [P, NT, H])
        s_x, s_v, s_z, s_w, s_end = (s.sem(a) for a in ("x", "v", "z", "w", "end"))
        with nc.Block() as block:
            @block.sync
            def _(sp):
                if loops:
                    sp.dma_start(c.acc[:, :, 0:D], table_dram.rearrange("(t p) d -> p t d", p=P)).then_inc(s_x, 16)

            @block.vector
            def _(dve):
                ch = Chain(dve, s_v)
                g, n = c.att_g[:, :, 0:H], c.att_n[:, :, 0:H]
                hb = has[:, :].unsqueeze(2).to_broadcast([P, NT, H])
                ch.step(dve.tensor_scalar(has[:, :], c.degree[:, :], 1.0, None, ALU.min))
                ch.step(dve.tensor_tensor(m[:, :, :], c.seg_max[:, :, 0:H], hb, ALU.mult))
                ch.step(dve.tensor_scalar(has[:, :], has[:, :], 1.0, BIG, ALU.subtract, ALU.mult))
                ch.step(dve.tensor_tensor(m[:, :, :], m[:, :, :], hb, ALU.add))
                if loops:
                    ch.step(dve.tensor_tensor(m[:, :, :], m[:, :, :], g, ALU.max))
                ch.step(dve.tensor_tensor(m[:, :, :], m[:, :, :], n, ALU.add))
                ch.step(dve.scalar_tensor_tensor(out=c.pair[:, :, H:2 * H], in0=m[:, :, :], scalar=0.2, in1=m[:, :, :],
                                                 op0=ALU.mult, op1=ALU.max))
                ch.step(dve.tensor_copy(c.pair[:, :, 0:H], n))
                if not loops:
                    dve.memset(c.acc[:, :, 0:D + H], 0.0).then_inc(s_end, 1)
                    dve.wait_ge(s_end, 1)
                    return
                ch.step(dve.tensor_tensor(z[:, :, :], g, n, ALU.add))
                ch.step(dve.scalar_tensor_tensor(out=z[:, :, :], in0=z[:, :, :], scalar=0.2, in1=z[:, :, :],
                                                 op0=ALU.mult, op1=ALU.max))
                dve.tensor_tensor(z[:, :, :], z[:, :, :], c.pair[:, :, H:2 * H], ALU.subtract).then_inc(s_z, 1)
                dve.wait_ge(s_w, 1)
                dve.wait_ge(s_x, 16)
                ch.step(dve.tensor_copy(c.acc[:, :, D:D + H], weight[:, :, :]))
                for t in range(0, NT, 7):
                    acc = c.acc[:, t:t + 7, 0:D].rearrange("p t (h d) -> p t h d", h=H)
                    dve.tensor_tensor(acc, acc, weight[:, t:t + 7, :].unsqueeze(3).to_broadcast([P, 7, H, D // H]),
                                      ALU.mult).then_inc(s_end, 1)
                dve.wait_ge(s_end, NT // 7)

            @block.scalar
            def _(act):
                if loops:
                    act.wait_ge(s_z, 1)
                    act.activation(weight[:, :, :], z[:, :, :], ACT.Exp).then_inc(s_w, 1)


def tile_registers(nc, eng, order, g, q):
    word = eng.value_load(order.tile_of[0:1, bass.ds(g * (U // PACK) + q, 1)], min_val=0, max_val=(1 << 24) - 1)
    return [nc.s_assert_within(eng.snap((word >> (PBITS * k)) & ((1 << PBITS) - 1)), 0, NT - 1,
                               skip_runtime_bounds_check_because="each field is a node tile by its making")
            for k in range(PACK)]


def stage_indices(sp, order_idx, idx, s_idx, s_gat, more=None):
    def body(g, j):
        wait(sp, s_gat[j % 2], halves(g, j, 16 * U, -1) if started(g, 4) else 0)
        sp.dma_start(idx[:, j, :], order_idx[:, bass.ds(g * U, U)]).then_inc(s_idx[j], 16)
        if more is not None:
            more(g, j)
    groups4(sp, SG, body)


def gather_rows(pool, table_dram, idx, rows, s_idx, s_gat, s_agg, s_passed):
    def body(g, j):
        pool.wait_ge(s_idx[j], quarters(g, j, 16, 1))
        for u in range(U):
            wait(pool, s_agg, g * U + u - 2 * U + 1 if started(g, 2) else 0)
            hold(pool, s_passed)
            pool.indirect_dma_start(rows[:, j % 2, u, 0:D], None, table_dram,
                                    bass.IndirectOffsetOnAxis(ap=idx[:, j, u:u + 1], axis=0)).then_inc(s_gat[j % 2], 16)
    groups4(pool, SG, body)


def gather_sum(nc, c, name, order, gather_idx, table_dram, norm=None):
    BANKS = 8
    with ExitStack() as ctx:
        s = Scope(nc, ctx, name)
        idx = s.sb("idx", [P, 4, U], U32)
        rows = s.sb("rows", [P, 2, U, D])
        sel = s.sb("sel", [P, 2, U, P])
        ps = s.psum("ps", [P, BANKS, 512])
        s_idx = [s.sem(f"idx{k}") for k in range(4)]
        s_gat = [s.sem(f"gat{k}") for k in range(2)]
        s_sel, s_agg, s_acc, s_passed = (s.sem(x) for x in ("sel", "agg", "acc", "passed"))
        with nc.Block() as block:
            @block.sync
            def _(sp):
                stage_indices(sp, gather_idx, idx, s_idx, s_gat)

            @block.gpsimd
            def _(pool):
                gather_rows(pool, table_dram, idx, rows, s_idx, s_gat, s_agg, s_passed)

            @block.vector
            def _(dve):
                def select(g, j):
                    wait(dve, s_agg, (g - 1) * U if started(g, 2) else 0)
                    if norm is None:
                        row = order.row[:, bass.ds(g * U, U)]
                        dve.tensor_tensor(sel[:, j % 2, :, :], c.iota[:, :].unsqueeze(1).to_broadcast([P, U, P]),
                                          row.unsqueeze(2).to_broadcast([P, U, P]), ALU.is_equal).then_inc(s_sel, 1)
                    else:
                        for u in range(U):
                            last = dve.tensor_scalar(sel[:, j % 2, u, :], c.iota[:, :],
                                                     order.row[:, bass.ds(g * U + u, 1)], norm[:, bass.ds(g * U + u, 1)],
                                                     ALU.is_equal, ALU.mult)
                        last.then_inc(s_sel, 1)

                def add(g):
                    for u in range(U):
                        if u % PACK == 0:
                            regs = tile_registers(nc, dve, order, g, u // PACK)
                        t = g * U + u
                        dve.wait_ge(s_agg, t + 1)
                        wait(dve, s_acc, t)
                        acc = c.acc[:, bass.ds(regs[u % PACK], 1), 0:D].rearrange("p a d -> p (a d)")
                        dve.tensor_tensor(acc, acc, ps[:, u % BANKS, 0:D], ALU.add).then_inc(s_acc, 1)

                def body(g, j):
                    select(g, j)
                    if started(g, 1):
                        add(g - 1)
                groups4(dve, SG, body)
                add(SG - 1)
                dve.wait_ge(s_acc, ST)

            @block.tensor
            def _(pe):
                def body(g, j):
                    pe.wait_ge(s_sel, g + 1)
                    pe.wait_ge(s_gat[j % 2], halves(g, j, 16 * U, 1))
                    for u in range(U):
                        wait(pe, s_acc, (g - 1) * U + u + 1 if started(g, 1) else 0)
                        pe.matmul(ps[:, u % BANKS, 0:D], sel[:, j % 2, u, :], rows[:, j % 2, u, :],
                                  start=True, stop=True).then_inc(s_agg, 1)
                groups4(pe, SG, body)


def gather_sum_attention(nc, c, name, order, gather_idx, table_dram, heads, gathered):
    H = heads
    W = D + H
    BANK0, BANKS = 3, 4
    with ExitStack() as ctx:
        s = Scope(nc, ctx, name)
        idx = s.sb("idx", [P, 4, U], U32)
        rows = s.sb("rows", [P, 2, U, W])
        sel = s.sb("sel", [P, 4, U, P])
        sel_t = s.sb("sel_t", [P, U, P])
        own = s.sb("own", [P, 4, U, 2 * H])
        z = s.sb("z", [P, U, H])
        y = s.sb("y", [P, U, H])
        ps = s.psum("ps", [P, 8, 512])
        tr = ps[:, 0:2, :].rearrange("p b (u e) -> p (b u) e", u=4)
        look = ps[:, 2, 0:U * 2 * H].rearrange("p (u h) -> p u h", u=U)
        s_idx = [s.sem(f"idx{k}") for k in range(4)]
        s_gat = [s.sem(f"gat{k}") for k in range(2)]
        s_own = [s.sem(f"own{k}") for k in range(4)]
        s_far, s_sel, s_tr, s_st, s_look = (s.sem(x) for x in ("far", "sel", "tr", "st", "look"))
        s_z, s_w, s_msg, s_v = (s.sem(x) for x in ("z", "w", "msg", "v"))
        s_agg, s_acc, s_passed = (s.sem(x) for x in ("agg", "acc", "passed"))
        with nc.Block() as block:
            @block.sync
            def _(sp):
                def stage_pairs(g, j):
                    wait(sp, s_look, g - 3)
                    for q in range(U // PACK):
                        for u, tile in enumerate(tile_registers(nc, sp, order, g, q), q * PACK):
                            sp.dma_start(own[:, j, u, :], c.pair[:, bass.ds(tile, 1), :].squeeze(1)).then_inc(s_own[j], 16)
                stage_indices(sp, gather_idx, idx, s_idx, s_gat, stage_pairs)

            @block.gpsimd
            def _(pool):
                gather_rows(pool, table_dram, idx, rows, s_idx, s_gat, s_agg, s_passed)

            @block.scalar
            def _(act):
                def select(g, j):
                    wait(act, s_agg, (g - 3) * U if started(g, 4) else 0)
                    for u in range(U):
                        far = act.activation(sel[:, j, u, :], c.iota[:, :], ACT.Abs,
                                             bias=order.row[:, bass.ds(g * U + u, 1)], scale=-1.0)
                    far.then_inc(s_far, 1)
                    act.wait_ge(s_far, g + 1)
                    act.activation(sel[:, j, :, :], sel[:, j, :, :], ACT.Relu, bias=c.ones[:, 0:1], scale=-1.0) \
                        .then_inc(s_sel, 1)

                def copy_turned(g):
                    act.wait_ge(s_tr, g + 1)
                    wait(act, s_look, g)
                    act.copy(sel_t[:, :, :], tr[:, :, :]).then_inc(s_st, 1)

                def weights(g, j):
                    act.wait_ge(s_z, g + 1)
                    wait(act, s_agg, (g - 1) * U if started(g, 2) else 0)
                    act.activation(rows[:, j % 2, :, D:W], y[:, :, :], ACT.Exp).then_inc(s_w, 1)

                def body(g, j):
                    if started(g, 2):
                        copy_turned(g - 2)
                    select(g, j)
                    if started(g, 2):
                        weights(g - 2, j)
                act.wait_ge(c.ready, 5)
                groups4(act, SG, body)
                for g in (SG - 2, SG - 1):
                    copy_turned(g)
                    weights(g, g % 2)

            @block.tensor
            def _(pe):
                def turn(g, j):
                    pe.wait_ge(s_sel, g + 1)
                    wait(pe, s_st, g)
                    pe.wait_ge(c.ready, 5)
                    for u in range(U):
                        mm = pe.transpose(tr[:, u, :], sel[:, j, u, :], c.ident[:, :])
                    mm.then_inc(s_tr, 1)

                def lookup(g, j):
                    pe.wait_ge(s_st, g + 1)
                    pe.wait_ge(s_own[j], quarters(g, j, 16 * U, 1))
                    wait(pe, s_z, g)
                    for u in range(U):
                        mm = pe.matmul(look[:, u, :], sel_t[:, u, :], own[:, j, u, :], start=True, stop=True)
                    mm.then_inc(s_look, 1)

                def sums(g, j, tiles):
                    for u in tiles:
                        t = g * U + u
                        pe.wait_ge(s_msg, t + 1)
                        wait(pe, s_acc, t - BANKS + 1 if not (isinstance(t, int) and t < BANKS) else 0)
                        pe.matmul(ps[:, BANK0 + u % BANKS, 0:W], sel[:, j, u, :], rows[:, j % 2, u, 0:W],
                                  start=True, stop=True).then_inc(s_agg, 1)

                def body(g, j):
                    turn(g, j)
                    if started(g, 1):
                        sums(g - 1, (j - 1) % 4, range(0, 3))
                    lookup(g, j)
                    if started(g, 1):
                        sums(g - 1, (j - 1) % 4, range(3, U))
                groups4(pe, SG, body)
                sums(SG - 1, 3, range(U))

            @block.vector
            def _(dve):
                def weigh(g, step):
                    if step == 0:
                        dve.wait_ge(s_look, g + 1)
                        dve.tensor_tensor(z[:, :, :], gathered[:, bass.ds(g * U, U), 0:H], look[:, :, 0:H], ALU.add) \
                            .then_inc(s_v, 1)
                        return
                    dve.wait_ge(s_v, g * 3 + step)
                    if step == 1:
                        dve.scalar_tensor_tensor(out=y[:, :, :], in0=z[:, :, :], scalar=0.2, in1=z[:, :, :],
                                                 op0=ALU.mult, op1=ALU.max).then_inc(s_v, 1)
                    elif step == 2:
                        dve.tensor_tensor(z[:, :, :], y[:, :, :], look[:, :, H:2 * H], ALU.subtract).then_inc(s_v, 1)
                    else:
                        dve.tensor_scalar(y[:, :, :], z[:, :, :], 0.0, None, ALU.min).then_inc(s_z, 1)

                def multiply(j, u):
                    r = rows[:, j % 2, u, 0:D].rearrange("p (h d) -> p h d", h=H)
                    dve.tensor_tensor(r, r, rows[:, j % 2, u, D:W].unsqueeze(2).to_broadcast([P, H, D // H]),
                                      ALU.mult).then_inc(s_msg, 1)

                def add(g, u, tile):
                    t = g * U + u
                    dve.wait_ge(s_agg, t + 1)
                    wait(dve, s_acc, t)
                    acc = c.acc[:, bass.ds(tile, 1), 0:W].rearrange("p a d -> p (a d)")
                    dve.tensor_tensor(acc, acc, ps[:, BANK0 + u % BANKS, 0:W], ALU.add).then_inc(s_acc, 1)

                def group(g, j, following=None):
                    dve.wait_ge(s_w, g + 1)
                    dve.wait_ge(s_gat[j % 2], halves(g, j, 16 * U, 1))
                    for u in range(U):
                        multiply(j, u)
                        if u % PACK == 0 and (u or started(g, 1)):
                            tiles = tile_registers(nc, dve, order, g if u else g - 1, 0 if u else 1)
                        if u >= PACK:
                            add(g, u - PACK, tiles[u - PACK])
                        elif started(g, 1):
                            add(g - 1, u + PACK, tiles[u])
                        if u >= U - 4 and following is not None:
                            weigh(following, u - (U - 4))

                def body(g, j):
                    if started(g, 1):
                        group(g - 1, j - 1, following=g)
                    else:
                        for step in range(4):
                            weigh(g, step)
                groups4(dve, SG, body)
                group(SG - 1, 3)
                for u, tile in enumerate(tile_registers(nc, dve, order, SG - 1, 1), PACK):
                    add(SG - 1, u, tile)
                dve.wait_ge(s_acc, ST)


def softmax_mean(nc, c, name, heads, bias_dram):
    H = heads
    with ExitStack() as ctx:
        s = Scope(nc, ctx, name)
        bias = s.sb("bias", [P, D])
        den = s.sb("den", [P, NT, H])
        s_b, s_v = s.sem("b"), s.sem("v")
        with nc.Block() as block:
            @block.sync
            def _(sp):
                sp.dma_start(bias[:, :], bias_dram.partition_broadcast(P)).then_inc(s_b, 16)

            @block.vector
            def _(dve):
                ch = Chain(dve, s_v)
                ch.step(dve.tensor_scalar(den[:, :, :], c.acc[:, :, D:D + H], 1e-16, None, ALU.max))
                ch.step(dve.reciprocal(den[:, :, :], den[:, :, :]))
                a4 = c.acc[:, :, 0:D].rearrange("p t (h d) -> p t h d", h=H)
                ch.step(dve.tensor_tensor(a4, a4, den[:, :, :].unsqueeze(3).to_broadcast([P, NT, H, D // H]), ALU.mult))
                dve.wait_ge(s_b, 16)
                ch.step(dve.tensor_tensor(c.acc[:, :, 0:D], c.acc[:, :, 0:D],
                                          bias[:, :].unsqueeze(1).to_broadcast([P, NT, D]), ALU.add))


def batch_norm_add(nc, c, name, gamma_dram, beta_dram):
    with ExitStack() as ctx:
        s = Scope(nc, ctx, name)
        gamma = s.sb("gamma", [P, D])
        beta = s.sb("beta", [P, D])
        mean = s.sb("mean", [P, D])
        std = s.sb("std", [P, D])
        eps = s.sb("eps", [P, 1])
        sq = s.sb("sq", [P, 2, D])
        ps = s.psum("ps", [P, 2, 512])
        s_b, s_v, s_sum, s_dev, s_sq, s_sq_mm, s_var, s_std = (
            s.sem(x) for x in ("b", "v", "sum", "dev", "sq", "sq_mm", "var", "std"))
        FULL = NT - 1

        with nc.Block() as block:
            @block.sync
            def _(sp):
                sp.dma_start(gamma[:, :], gamma_dram.partition_broadcast(P)).then_inc(s_b, 16)
                sp.dma_start(beta[:, :], beta_dram.partition_broadcast(P)).then_inc(s_b, 16)

            @block.tensor
            def _(pe):
                pe.matmul(ps[:, 0, 0:D], c.ones[0:LAST, :], c.acc[0:LAST, NT - 1, 0:D], start=True, stop=False,
                          skip_group_check=True)
                loop(pe, FULL, lambda i: pe.matmul(
                    ps[:, 0, 0:D], c.ones[:, :], c.acc[:, bass.ds(i, 1), 0:D].rearrange("p a d -> p (a d)"),
                    start=False, stop=False, skip_group_check=True).then_inc(s_sum, 1))

                def squares(j, k):
                    pe.wait_ge(s_sq, j + 1)
                    M = LAST if isinstance(j, int) and j == NT - 1 else P
                    pe.matmul(ps[:, 1, 0:D], c.ones[0:M, :], sq[0:M, k, :], start=isinstance(j, int) and j == 0,
                              stop=False, skip_group_check=True).then_inc(s_sq_mm, 1)
                node_tiles(pe, squares)

            @block.scalar
            def _(act):
                act.wait_ge(s_dev, 1)

                def squares(j, k):
                    wait(act, s_sq_mm, j - 1)
                    act.wait_ge(s_dev, 1)
                    act.activation(sq[:, k, :], c.acc[:, bass.ds(j, 1), 0:D].rearrange("p a d -> p (a d)"),
                                   ACT.Square).then_inc(s_sq, 1)
                node_tiles(act, squares)
                act.wait_ge(s_var, 1)
                act.activation(std[:, :], std[:, :], ACT.Sqrt, bias=eps[:, 0:1]).then_inc(s_std, 1)

            @block.vector
            def _(dve):
                ch = Chain(dve, s_v)
                acc = c.acc[:, :, 0:D]

                def rows(ap):
                    return ap[:, :].unsqueeze(1).to_broadcast([P, NT, D])
                ch.step(dve.memset(eps[:, :], EPS))
                dve.wait_ge(s_sum, FULL)
                ch.step(dve.tensor_scalar(mean[:, :], ps[:, 0, 0:D], 1.0 / N, None, ALU.mult))
                dve.tensor_tensor(acc, acc, rows(mean), ALU.subtract).then_inc(s_dev, 1)
                dve.wait_ge(s_sq_mm, NT)
                dve.tensor_scalar(std[:, :], ps[:, 1, 0:D], 1.0 / N, None, ALU.mult).then_inc(s_var, 1)
                dve.wait_ge(s_std, 1)
                dve.wait_ge(s_b, 32)
                ch.step(dve.reciprocal(std[:, :], std[:, :]))
                ch.step(dve.tensor_tensor(std[:, :], std[:, :], gamma[:, :], ALU.mult))
                dve.wait_ge(s_dev, 1)
                ch.step(dve.tensor_tensor(acc, acc, rows(std), ALU.mult))
                ch.step(dve.tensor_tensor(acc, acc, rows(beta), ALU.add))
                ch.step(dve.tensor_tensor(c.x[:, :, :], c.x[:, :, :], acc, ALU.add))


def add_nodes(nc, c, name, relu):
    with ExitStack() as ctx:
        s = Scope(nc, ctx, name)
        s_v = s.sem("v")
        with nc.Block() as block:
            @block.vector
            def _(dve):
                ch = Chain(dve, s_v)
                if relu:
                    ch.step(dve.scalar_tensor_tensor(out=c.x[:, :, :], in0=c.acc[:, :, 0:D], scalar=0.0, in1=c.x[:, :, :],
                                                     op0=ALU.max, op1=ALU.add))
                else:
                    ch.step(dve.tensor_tensor(c.x[:, :, :], c.x[:, :, :], c.acc[:, :, 0:D], ALU.add))


def start_acc(nc, c, name, table_dram=None):
    with ExitStack() as ctx:
        s = Scope(nc, ctx, name)
        s_v = s.sem("v")
        with nc.Block() as block:
            if table_dram is None:
                @block.vector
                def _(dve):
                    dve.memset(c.acc[:, :, 0:D], 0.0).then_inc(s_v, 16)
                    dve.wait_ge(s_v, 16)
            else:
                @block.sync
                def _(sp):
                    sp.dma_start(c.acc[:, :, 0:D], table_dram.rearrange("(t p) d -> p t d", p=P)).then_inc(s_v, 16)
                    sp.wait_ge(s_v, 16)


def relation_tables(nc, c, name, w_dram, table_dram):
    PAIRS = RELS // 2
    RING = 5
    with ExitStack() as ctx:
        s = Scope(nc, ctx, name)
        h = s.sb("h", [P, 2, D])
        h_t = s.sb("h_t", [P, 2, 2, P])
        w = s.sb("w", [P, 2, RELS * D])
        stage = s.sb("stage", [P, 2, RELS * D])
        ps = s.psum("ps", [P, 8, 512])
        s_w, s_h, s_tr, s_ht, s_mm = (s.sem(x) for x in ("w", "h", "tr", "ht", "mm"))
        s_even, s_odd = s.sem("even"), s.sem("odd")
        s_out = [s.sem(f"out{k}") for k in range(2)]
        with nc.Block() as block:
            @block.sync
            def _(sp):
                for half in range(2):
                    sp.dma_start(w[:, half, :].rearrange("p (r n) -> p r n", r=RELS),
                                 w_dram[:, half * P:(half + 1) * P, :].rearrange("r p n -> p r n")).then_inc(s_w, 16)

                def body(j, k):
                    sp.wait_ge(s_even, (j + 1) * (PAIRS // 2))
                    sp.wait_ge(s_odd, (j + 1) * (PAIRS // 2))
                    sp.dma_start(table_dram[bass.ds(j * P, P), :], stage[:, k, :]).then_inc(s_out[k], 16)
                node_tiles(sp, body)
                sp.wait_ge(s_out[0], 16 * (NT - NT // 2))
                sp.wait_ge(s_out[1], 16 * (NT // 2))

            def copies(eng, copy, parity, sem, j, k):
                wait(eng, s_out[k], halves(j, k, 16))
                for m in range(parity, PAIRS, 2):
                    eng.wait_ge(s_mm, j * PAIRS + m + 1)
                    copy(stage[:, k, m * 512:(m + 1) * 512], ps[:, 2 + m % RING, :]).then_inc(sem, 1)

            @block.scalar
            def _(act):
                def hidden(j, k):
                    wait(act, s_tr, j - 1)
                    act.wait_ge(c.ready, 5)
                    act.activation(h[:, k, :], c.x[:, bass.ds(j, 1), :].rearrange("p a b -> p (a b)"), ACT.Relu,
                                   bias=c.shift[:, bass.ds(j, 1)], scale=c.rstd[:, bass.ds(j, 1)]).then_inc(s_h, 1)

                def body(j, k):
                    if not isinstance(j, int):
                        hidden(j + 1, 1 - k)
                    elif j + 1 < NT:
                        hidden(j + 1, 1 - k)
                    copies(act, act.copy, 0, s_even, j, k)
                hidden(0, 0)
                node_tiles(act, body)

            @block.vector
            def _(dve):
                def turned(j, k):
                    dve.wait_ge(s_tr, j + 1)
                    wait(dve, s_mm, (j - 1) * PAIRS)
                    dve.tensor_copy(h_t[:, k, :, :], ps[:, k, 0:D].rearrange("p (a b) -> p a b", a=2)).then_inc(s_ht, 1)

                def body(j, k):
                    if not isinstance(j, int) or j + 1 < NT:
                        turned(j + 1, 1 - k)
                    copies(dve, dve.tensor_copy, 1, s_odd, j, k)
                turned(0, 0)
                node_tiles(dve, body)

            @block.tensor
            def _(pe):
                def turn(j, k):
                    pe.wait_ge(s_h, j + 1)
                    wait(pe, s_ht, j - 1)
                    pe.wait_ge(c.ready, 5)
                    for half in range(2):
                        mm = pe.transpose(ps[:, k, half * P:(half + 1) * P], h[:, k, half * P:(half + 1) * P], c.ident[:, :])
                    mm.then_inc(s_tr, 1)

                def body(j, k):
                    if not isinstance(j, int) or j + 1 < NT:
                        turn(j + 1, 1 - k)
                    pe.wait_ge(s_ht, j + 1)
                    for m in range(PAIRS):
                        before = m - RING
                        at = j if before >= 0 else j - 1
                        before %= PAIRS
                        wait(pe, s_odd if before % 2 else s_even,
                             at * (PAIRS // 2) + before // 2 + 1 if started(at, 0) and not (isinstance(at, int) and at < 0) else 0)
                        for half in range(2):
                            mm = pe.matmul(ps[:, 2 + m % RING, :], h_t[:, k, half, :], w[:, half, m * 512:(m + 1) * 512],
                                           start=half == 0, stop=half == 1)
                        mm.then_inc(s_mm, 1)
                pe.wait_ge(s_w, 32)
                turn(0, 0)
                node_tiles(pe, body)


def inverse_degrees(nc, c, name):
    with ExitStack() as ctx:
        s = Scope(nc, ctx, name)
        s_a, s_v = s.sem("a"), s.sem("v")
        with nc.Block() as block:
            @block.scalar
            def _(act):
                act.activation(c.dinv[:, :], c.degree[:, :], ACT.Sqrt, bias=c.ones[:, 0:1]).then_inc(s_a, 1)

            @block.vector
            def _(dve):
                dve.wait_ge(s_a, 1)
                dve.reciprocal(c.dinv[:, :], c.dinv[:, :]).then_inc(s_v, 1)
                dve.wait_ge(s_v, 1)


def finish(nc, c, name, bias_dram, out_dram):
    PARTS = 7
    with ExitStack() as ctx:
        s = Scope(nc, ctx, name, last=True)
        bias = s.sb("bias", [P, D])
        s_b, s_v, s_part, s_out = s.sem("b"), s.sem("v"), s.sem("part"), s.sem("out")
        with nc.Block() as block:
            @block.sync
            def _(sp):
                sp.dma_start(bias[:, :], bias_dram.partition_broadcast(P)).then_inc(s_b, 16)
                for i, t in enumerate(range(0, NT, PARTS)):
                    sp.wait_ge(s_part, i + 1)
                    full = min(t + PARTS, NT - 1)
                    sp.dma_start(out_dram[t * P:full * P, :].rearrange("(t p) d -> p t d", p=P), c.x[:, t:full, :]) \
                        .then_inc(s_out, 16)
                sp.dma_start(out_dram[(NT - 1) * P:N, :], c.x[0:LAST, NT - 1, :]).then_inc(s_out, 16)
                sp.wait_ge(s_out, 16 * (NT // PARTS + 1))

            @block.vector
            def _(dve):
                ch = Chain(dve, s_v)
                dve.wait_ge(s_b, 16)
                for t in range(0, NT, PARTS):
                    acc = c.acc[:, t:t + PARTS, 0:D]
                    x = c.x[:, t:t + PARTS, :]
                    ch.step(dve.tensor_tensor(acc, acc, c.dinv[:, t:t + PARTS].unsqueeze(2).to_broadcast([P, PARTS, D]),
                                              ALU.mult))
                    ch.step(dve.tensor_tensor(acc, acc, bias[:, :].unsqueeze(1).to_broadcast([P, PARTS, D]), ALU.add))
                    dve.scalar_tensor_tensor(out=x, in0=acc, scalar=0.0, in1=x, op0=ALU.max, op1=ALU.add) \
                        .then_inc(s_part, 1)


def gnn_kernel(nc, a, out_dram):
    def dram(name, shape):
        return nc.dram_tensor(name, shape, F32, kind="Internal").ap()

    slots_by_dst = dram("slots_by_dst", (P, ST, 4))
    slots_by_src = dram("slots_by_src", (P, ST, 2))
    rows0, rows1, rows3 = (dram(f"rows{i}", (NPAD, D)) for i in (0, 1, 3))
    rows2 = dram("rows2", (NPAD, RELS * D))
    with ExitStack() as ctx:
        c = Scope(nc, ctx, "c", last=True)
        make_constants(nc, c)
        by_dst = Order(c, "by_dst", (("src", U32), ("src_rel", U32), ("norm", F32), ("dst", F32)))
        by_dst.key = by_dst.words[3]
        by_src = Order(c, "by_src", (("dst", U32), ("src", F32)))
        by_src.key = by_src.words[1]
        c.x = c.sb("x", [P, NT, D])
        c.rstd = c.sb("rstd", [P, NT])
        c.shift = c.sb("shift", [P, NT])
        c.degree = c.sb("degree", [P, NT])
        c.dinv = c.sb("dinv", [P, NT])
        load_nodes(nc, c, a["x"])
        sort_edges(nc, c, "sort_dst", a["dst"], dst_fields(a["src"], a["edge_type_20"], a["edge_weight1"]), 4,
                   slots_by_dst, by_dst)
        sort_edges(nc, c, "sort_src", a["src"], src_fields(a["dst"]), 2, slots_by_src, by_src)

        for layer, heads, order, rows in ((0, 8, by_dst, rows0), (1, 4, by_src, rows1)):
            with ExitStack() as layer_ctx:
                s = Scope(nc, layer_ctx, f"layer{layer}")
                c.att_g = s.sb("att_g", [P, NT, heads])
                c.att_n = s.sb("att_n", [P, NT, heads])
                c.seg_max = s.sb("seg_max", [P, NT, heads])
                c.pair = s.sb("pair", [P, NT, 2 * heads])
                gathered = s.sb("gathered", [P, ST, heads])
                small = dram(f"small{layer}", (NPAD, heads))
                layer_norm_stats(nc, c, f"ln{layer}")
                if layer == 0:
                    att = [a[n].rearrange("h d -> (h d)") for n in ("L0_gnn_att_src", "L0_gnn_att_dst")]
                    project(nc, c, "proj0", a["L0_gnn_W"], rows, att, heads, small, add_h=True)
                else:
                    att = [a[n].rearrange("a h d -> (a h d)") for n in ("L1_gnn_att_dst", "L1_gnn_att_src")]
                    project(nc, c, "proj1", a["L1_gnn_weight"], rows, att, heads, small, w_rearranged=True)
                segment_max(nc, c, f"max{layer}", order, order.words[0], heads, small, gathered,
                            dram(f"ends{layer}", (P, 3)), dram(f"carry{layer}", (P, 2)),
                            dram(f"maxima{layer}", (P * ST, heads)))
                count_columns(nc, c, f"count{layer}", order)
                c.acc = s.sb("acc", [P, NT, D + heads])
                attention_nodes(nc, c, f"nodes{layer}", heads, rows, loops=layer == 0)
                gather_sum_attention(nc, c, f"sum{layer}", order, order.words[0], rows, heads, gathered)
                softmax_mean(nc, c, f"mean{layer}", heads, a[f"L{layer}_gnn_bias"])
                if layer == 0:
                    batch_norm_add(nc, c, "bn0", a["L0_gnn_gamma"], a["L0_gnn_beta"])
                else:
                    add_nodes(nc, c, "add1", relu=False)

        layer_norm_stats(nc, c, "ln2")
        relation_tables(nc, c, "proj2", a["L2_gnn_weight"], rows2)
        c.acc = c.sb("acc", [P, NT, D])
        start_acc(nc, c, "start2")
        gather_sum(nc, c, "sum2", by_dst, by_dst.words[1], rows2.rearrange("n (r d) -> (n r) d", r=RELS),
                   norm=by_dst.words[2])
        add_nodes(nc, c, "add2", relu=True)

        layer_norm_stats(nc, c, "ln3")
        count_columns(nc, c, "count3", by_dst)
        inverse_degrees(nc, c, "deg3")
        project(nc, c, "proj3", a["L3_gnn_weight"], rows3, scale_rows=c.dinv,
                affine=[a[f"L3_gnn_{n}"] for n in ("gamma", "beta", "running_mean", "running_var")])
        start_acc(nc, c, "start3", rows3)
        gather_sum(nc, c, "sum3", by_dst, by_dst.words[0], rows3)
        finish(nc, c, "finish", a["L3_gnn_bias"], out_dram)


_INS = ["x", "src", "dst", "edge_type_20", "edge_weight1",
        "L0_gnn_W", "L0_gnn_att_src", "L0_gnn_att_dst", "L0_gnn_bias", "L0_gnn_gamma", "L0_gnn_beta",
        "L1_gnn_weight", "L1_gnn_att_src", "L1_gnn_att_dst", "L1_gnn_bias", "L2_gnn_weight",
        "L3_gnn_weight", "L3_gnn_bias", "L3_gnn_gamma", "L3_gnn_beta", "L3_gnn_running_mean", "L3_gnn_running_var"]


def kernel(**inputs):
    import concourse.bacc as bacc
    from concourse.bass_utils import run_bass_kernel_spmd

    nc = bacc.Bacc("TRN2", target_bir_lowering=False, num_devices=1)
    arrays, aps = {}, {}
    for name in _INS:
        array = np.ascontiguousarray(inputs[name])
        arrays[f"in_{name}"] = array
        aps[name] = nc.dram_tensor(f"in_{name}", array.shape, mybir.dt.from_np(array.dtype), kind="ExternalInput").ap()
    out = nc.dram_tensor("out_0", (N, D), F32, kind="ExternalOutput").ap()
    gnn_kernel(nc, aps, out)
    result = run_bass_kernel_spmd(nc, [arrays], core_ids=[0])
    return result.results[0]["out_0"]
```

```python
from contextlib import ExitStack

import numpy as np

import concourse.bass as bass
from concourse import mybir
from concourse.alu_op_type import AluOpType as ALU

ACT = mybir.ActivationFunctionType
AX = mybir.AxisListType
F32 = mybir.dt.float32
I32 = mybir.dt.int32
U32 = mybir.dt.uint32
F16 = mybir.dt.float16

P = 128
N = 6250
D = 256
E = 100000
RELS = 20
NT = -(-N // P)
NPAD = NT * P
LAST = N - (NT - 1) * P
EP = 125
EC = E // EP
U = 8
EG = EC // U
ST = -(-((E + NT * (P - 1)) // P) // 16) * 16
SG = ST // U
PACK, PBITS = 4, 6
BIG = 1e30
EPS = 1e-5
assert EP * EC == E and EC % (4 * U) == 0 and ST % (4 * U) == 0 and U == 2 * PACK and NT < 1 << PBITS


def wait(eng, sem, value):
    if not (isinstance(value, int) and value <= 0):
        eng.wait_ge(sem, value)


def hold(eng, passed):
    eng.sem_inc(passed, 1)


def loop(eng, count, body, peel=1):
    for i in range(peel):
        body(i)
    with eng.Fori(peel, count) as i:
        body(i)


class Scope:

    def __init__(self, nc, ctx, name, last=False):
        self.nc, self.ctx, self.name, self.sems = nc, ctx, name, []
        if not last:
            ctx.callback(self.free_sems)

    def free_sems(self):
        if self.sems:
            self.nc.clear_and_free_semaphores(self.sems)
            self.nc.all_engine_barrier()

    def sb(self, name, shape, dt=F32):
        return self.ctx.enter_context(self.nc.sbuf_tensor(f"{self.name}_{name}", shape, dt))

    def psum(self, name, shape, dt=F32):
        return self.ctx.enter_context(self.nc.psum_tensor(f"{self.name}_{name}", shape, dt))

    def sem(self, name):
        self.sems.append(self.nc.alloc_semaphore(f"{self.name}_{name}"))
        return self.sems[-1]


def make_constants(nc, c):
    c.ident = c.sb("ident", [P, P])
    c.ones = c.sb("ones", [P, P])
    c.iota = c.sb("iota", [P, P])
    c.before = c.sb("before", [P, P])
    c.ident16 = c.sb("ident16", [P, P], F16)
    with ExitStack() as ctx:
        s = Scope(nc, ctx, "const")
        iota_i = s.sb("iota_i", [P, P], I32)
        filled = c.sem("filled")
        ready = c.ready = c.sem("ready")
        with nc.Block() as block:
            @block.gpsimd
            def _(pool):
                pool.memset(c.ident[:, :], 0.0).then_inc(filled, 1)
                pool.memset(c.ones[:, :], 1.0).then_inc(filled, 1)
                pool.memset(c.before[:, :], 1.0).then_inc(filled, 1)
                pool.iota(iota_i[:, :], pattern=[[1, P]], base=0, channel_multiplier=0).then_inc(ready, 1)
                pool.wait_ge(filled, 3)
                pool.affine_select(out=c.ident[:, :], in_=c.ident[:, :], compare_op=ALU.not_equal, fill=1.0,
                                   base=0, pattern=[[-1, P]], channel_multiplier=1).then_inc(ready, 1)
                pool.affine_select(out=c.before[:, :], in_=c.before[:, :], compare_op=ALU.is_gt, fill=0.0,
                                   base=0, pattern=[[1, P]], channel_multiplier=-1).then_inc(ready, 1)

            @block.vector
            def _(dve):
                dve.wait_ge(ready, 1)
                dve.tensor_copy(c.iota[:, :], iota_i[:, :]).then_inc(ready, 1)
                dve.wait_ge(ready, 4)
                dve.tensor_copy(c.ident16[:, :], c.ident[:, :]).then_inc(ready, 1)
                dve.wait_ge(ready, 5)


def sort_edges(nc, c, name, key_dram, fields, words, slots_dram, out):
    with ExitStack() as ctx:
        s = Scope(nc, ctx, name)
        key = s.sb("key", [EP, EC], I32)
        digit = s.sb("digit", [EP, EC], I32)
        hi = s.sb("hi", [EP, EC], F16)
        lo = s.sb("lo", [EP, EC], F16)
        iotas = s.sb("iotas", [EP, P, U], F16)
        pay = s.sb("pay", [EP, EC, words])
        slots = s.sb("slots", [P, ST, words])
        out.tile_f = s.sb("tile_f", [P, ST])
        hot_hi = s.sb("hot_hi", [EP, 4, NT, U], F16)
        hot_lo = s.sb("hot_lo", [EP, 4, P, U], F16)
        ps = s.psum("ps", [P, 8, 512])
        load_fields, emit_fields = fields(s)

        s_load, s_fill, s_init = s.sem("load"), s.sem("fill"), s.sem("init")
        s_prep = s.sem("prep")
        s_hot, s_counted = s.sem("hot"), s.sem("counted")
        s_base, s_mm = s.sem("base"), s.sem("base_mm")
        tiles_f = s.sb("tiles_f", [NT, 1])
        tiles_i = s.sb("tiles_i", [NT, 1], I32)
        total = s.sb("total", [NT, 1])
        base = s.sb("base", [NT, 1])
        first = s.sb("first", [NT, P])
        after = s.sb("after", [NT, P])
        reached = s.sb("reached", [NT, ST])
        iota_t = s.sb("iota_t", [NT, ST], I32)
        iota_tf = s.sb("iota_tf", [NT, ST])
        s_iota = s.sem("iota")
        hist = ps[0:NT, 0, 0:P]
        HALF = ST // 2
        packed = s.sb("packed", [1, ST // PACK])
        nload = load_fields(None)
        with nc.Block() as block:
            @block.sync
            def _(sp):
                sp.dma_start(key[:, :], key_dram.rearrange("(p c) -> p c", p=EP)).then_inc(s_load, 16)
                load_fields(sp, s_load)
                sp.wait_ge(s_fill, 2)
                sp.dma_start(slots_dram, slots[:, :, :]).then_inc(s_init, 16)
                sp.wait_ge(s_init, 16)

            @block.gpsimd
            def _(pool):
                pool.iota(iota_t[:, :], pattern=[[1, ST]], base=0, channel_multiplier=0).then_inc(s_iota, 1)
                pool.memset(slots[:, :, 0:words - 1], 0.0).then_inc(s_fill, 1)
                pool.memset(slots[:, :, words - 1:words], -1.0).then_inc(s_fill, 1)

            @block.vector
            def _(dve):
                done = [0]

                def link(ins):
                    done[0] += 1
                    ins.then_inc(s_prep, 1)
                    dve.wait_ge(s_prep, done[0])

                link(dve.tensor_copy(iotas[:, :, :], c.iota[0:EP, :].unsqueeze(2).to_broadcast([EP, P, U])))
                dve.wait_ge(s_load, 16 * (1 + nload))
                link(dve.tensor_scalar(digit[:, :], key[:, :], 7, None, ALU.arith_shift_right))
                link(dve.tensor_copy(hi[:, :], digit[:, :]))
                link(dve.tensor_scalar(digit[:, :], key[:, :], P - 1, None, ALU.bitwise_and))
                link(dve.tensor_copy(lo[:, :], digit[:, :]))
                link(dve.tensor_copy(pay[:, :, words - 1], key[:, :]))
                emit_fields(dve, link, pay)

                def hot(i):
                    for j in range(4):
                        g = i * 4 + j
                        wait(dve, s_counted, g - 3)
                        one_hot(dve, iotas, s_hot, hi, lo, hot_hi, hot_lo, g, j)

                loop(dve, EG // 4, hot)
                dve.wait_ge(s_counted, EG)

                def link(ins):
                    done[0] += 1
                    ins.then_inc(s_prep, 1)
                    dve.wait_ge(s_prep, done[0])

                link(dve.tensor_copy(out.count[:, :], hist))
                link(dve.tensor_reduce(total[:, :], out.count[:, :], AX.X, ALU.add))
                link(dve.tensor_scalar(tiles_f[:, :], total[:, :], float(P - 1), None, ALU.add))
                link(dve.tensor_copy(tiles_i[:, :], tiles_f[:, :]))
                link(dve.tensor_scalar(tiles_i[:, :], tiles_i[:, :], 7, None, ALU.arith_shift_right))
                dve.tensor_copy(tiles_f[:, :], tiles_i[:, :]).then_inc(s_base, 1)
                dve.wait_ge(s_mm, 1)
                link(dve.tensor_copy(base[:, :], ps[0:NT, 1, 0:1]))
                link(dve.tensor_tensor_scan(after[:, :], c.ones[0:NT, :], out.count[:, :], 0.0, ALU.mult, ALU.add))
                link(dve.tensor_tensor(first[:, :], after[:, :], out.count[:, :], ALU.subtract))
                link(dve.scalar_tensor_tensor(out=out.start[:, :], in0=base[:, :].to_broadcast([NT, P]), scalar=float(P),
                                              in1=first[:, :], op0=ALU.mult, op1=ALU.add))
                dve.wait_ge(s_iota, 1)
                link(dve.tensor_copy(iota_tf[:, :], iota_t[:, :]))
                dve.tensor_scalar(reached[:, :], iota_tf[:, :], base[:, 0:1], None, ALU.is_ge).then_inc(s_base, 1)
                dve.wait_ge(s_mm, 2)
                for h in range(2):
                    last = dve.tensor_scalar(out.tile_f[:, h * HALF:(h + 1) * HALF], ps[:, 2 + h, 0:HALF], -1.0, None,
                                             ALU.add)
                    link(last)
                nt4 = out.tile_f[0:1, :].rearrange("p (q k) -> p q k", k=PACK)
                link(dve.tensor_copy(packed[:, :], nt4[:, :, PACK - 1]))
                for k in reversed(range(PACK - 1)):
                    link(dve.scalar_tensor_tensor(out=packed[:, :], in0=packed[:, :], scalar=float(1 << PBITS),
                                                  in1=nt4[:, :, k], op0=ALU.mult, op1=ALU.add))
                link(dve.tensor_copy(out.tile_of[:, :], packed[:, :]))

            @block.tensor
            def _(pe):
                def count(i):
                    for j in range(4):
                        g = i * 4 + j
                        pe.wait_ge(s_hot, g * 2 + 2)
                        for u in range(U):
                            mm = pe.matmul(hist, hot_hi[:, j, :, u], hot_lo[:, j, :, u],
                                           start=isinstance(i, int) and g == 0 and u == 0, stop=False,
                                           skip_group_check=True)
                        mm.then_inc(s_counted, 1)

                loop(pe, EG // 4, count)
                pe.wait_ge(s_base, 1)
                pe.matmul(ps[0:NT, 1, 0:1], c.before[0:NT, 0:NT], tiles_f[:, :], start=True, stop=True).then_inc(s_mm, 1)
                pe.wait_ge(s_base, 2)
                for h in range(2):
                    mm = pe.matmul(ps[:, 2 + h, 0:HALF], c.ones[0:NT, :], reached[:, h * HALF:(h + 1) * HALF],
                                   start=True, stop=True)
                mm.then_inc(s_mm, 1)

        assert U * EP <= 2048
        hot_hi_t = s.sb("hot_hi_t", [NT, 2, U, P])
        hot_hi_t16 = s.sb("hot_hi_t16", [NT, 2, U, P], F16)
        same = s.sb("same", [EP, 2, U, P], F16)
        free = s.sb("free", [NT, 2, P])
        earlier = s.sb("earlier", [NT, 2, U, P], F16)
        picked = s.sb("picked", [EP, U, P])
        pos = s.sb("pos", [EP, U])
        pos_i = s.sb("pos_i", [EP, U], I32)
        tile_i = s.sb("slot_tile_i", [EP, U], I32)
        tile_f = s.sb("slot_tile_f", [EP, U])
        row_f = s.sb("row_f", [EP, U])
        idx = s.sb("idx", [EP, 4, U], U32)
        stage = s.sb("stage", [EP, 4, U, words])
        tr = ps[:, 0, :].bitcast(F16).rearrange("p (u e) -> p u e", u=U)
        eq = ps[:, 1:3, :].rearrange("p b (u e) -> p (b u) e", u=4)
        look = ps[:, 3:5, :].rearrange("p b (u e) -> p (b u) e", u=4)
        prefix = ps[0:NT, 5:7, :].rearrange("p b (u e) -> p (b u) e", u=4)
        in_group = ps[0:NT, 7, 0:P]
        s_hot2, s_tr, s_hot_t, s_eq, s_same = (s.sem(x) for x in ("hot2", "tr", "hot_t", "eq", "same"))
        s_pre, s_free, s_early, s_look, s_idx, s_stage = (
            s.sem(x) for x in ("pre", "free", "early", "look", "idx", "stage"))
        s_picked, s_step, s_passed = s.sem("picked"), s.sem("step"), s.sem("passed")
        s_scat = [s.sem(f"scat{k}") for k in range(4)]
        STEPS = 5
        with nc.Block() as block:
            @block.vector
            def _(dve):
                def next_free(g, j):
                    if not started(g, 1):
                        dve.tensor_copy(free[:, 0, :], out.start[:, :]).then_inc(s_free, 1)
                        return
                    dve.wait_ge(s_pre, g)
                    dve.wait_ge(s_free, g)
                    wait(dve, s_look, g - 1)
                    dve.tensor_tensor(free[:, j % 2, :], free[:, (j + 1) % 2, :], in_group, ALU.add).then_inc(s_free, 1)

                def same_key(g, j):
                    wait(dve, s_eq, g + 1)
                    wait(dve, s_look, g - 1)
                    dve.tensor_tensor(same[:, j % 2, :, 0:EP], eq[0:EP, :, 0:EP],
                                      c.before[0:EP, 0:EP].unsqueeze(1).to_broadcast([EP, U, EP]), ALU.mult) \
                        .then_inc(s_same, 1)

                def place(g, j):
                    ch = Chain(dve, s_step, g * STEPS)
                    dve.wait_ge(s_look, g + 1)
                    dve.tensor_tensor(picked[:, :, :], look[0:EP, :, :],
                                      hot_lo[:, j % 4, :, :].rearrange("p n u -> p u n"), ALU.mult) \
                        .then_inc(s_picked, 1)
                    dve.wait_ge(s_picked, g + 1)
                    ch.step(dve.tensor_reduce(pos[:, :], picked[:, :, :], AX.X, ALU.add))
                    ch.step(dve.tensor_copy(pos_i[:, :], pos[:, :]))
                    ch.step(dve.tensor_scalar(tile_i[:, :], pos_i[:, :], 7, None, ALU.arith_shift_right))
                    ch.step(dve.tensor_copy(tile_f[:, :], tile_i[:, :]))
                    ch.step(dve.scalar_tensor_tensor(out=row_f[:, :], in0=tile_f[:, :], scalar=-float(P),
                                                     in1=pos[:, :], op0=ALU.mult, op1=ALU.add))
                    assert ch.n == STEPS
                    wait(dve, s_scat[j % 4], quarters(g, j % 4, 16 * U))
                    dve.scalar_tensor_tensor(out=idx[:, j % 4, :], in0=row_f[:, :], scalar=float(ST),
                                             in1=tile_f[:, :], op0=ALU.mult, op1=ALU.add).then_inc(s_idx, 1)

                def body(i):
                    for j in range(4):
                        g = i * 4 + j
                        wait(dve, s_look, g - 3)
                        one_hot(dve, iotas, s_hot2, hi, lo, hot_hi, hot_lo, g, j)
                        next_free(g, j)
                        if started(g, 1):
                            same_key(g - 1, j - 1)
                        if started(g, 2):
                            place(g - 2, j - 2)

                loop(dve, EG // 4, body, peel=2)
                same_key(EG - 1, 3)
                place(EG - 2, 2)
                place(EG - 1, 3)

            @block.tensor
            def _(pe):
                def counts(g, j):
                    wait(pe, s_early, g)
                    wait(pe, s_free, g + 1 if started(g, 1) else 0)
                    for u in range(U):
                        for bank in range(2):
                            a, b = max(u + 1, 4 * bank), 4 * bank + 4
                            if a < b:
                                pe.matmul(prefix[:, a:b, :], hot_hi[:, j, :, u],
                                          hot_lo[:, j, :, u].unsqueeze(1).to_broadcast([EP, b - a, P]),
                                          start=u == 0, stop=False, skip_group_check=True)
                        mm = pe.matmul(in_group, hot_hi[:, j, :, u], hot_lo[:, j, :, u], start=u == 0, stop=False,
                                       skip_group_check=True)
                    mm.then_inc(s_pre, 1)

                def lookup(g, j):
                    wait(pe, s_same, g + 1)
                    wait(pe, s_early, g + 1)
                    wait(pe, s_free, g + 1)
                    wait(pe, s_picked, g)
                    for u in range(U):
                        pe.matmul(look[0:EP, u, :], hot_hi_t[:, j % 2, u, 0:EP], free[:, j % 2, :],
                                  start=True, stop=False, skip_group_check=True)
                        if u:
                            pe.matmul(look[0:EP, u, :], hot_hi_t16[:, j % 2, u, 0:EP], earlier[:, j % 2, u, :],
                                      start=False, stop=False, skip_group_check=True)
                        mm = pe.matmul(look[0:EP, u, :], same[:, j % 2, u, 0:EP], hot_lo[:, j % 4, :, u],
                                       start=False, stop=True, skip_group_check=True)
                    mm.then_inc(s_look, 1)

                def body(i):
                    for j in range(4):
                        g = i * 4 + j
                        pe.wait_ge(s_hot2, g * 2 + 2)
                        wait(pe, s_hot_t, g * 2)
                        hold(pe, s_passed)
                        for u in range(U):
                            mm = pe.transpose(tr[0:NT, u, 0:EP], hot_hi[:, j, :, u], c.ident16[0:EP, 0:EP])
                        mm.then_inc(s_tr, 1)
                        counts(g, j)
                        pe.wait_ge(s_hot_t, g * 2 + 2)
                        wait(pe, s_same, g)
                        for u in range(U):
                            mm = pe.matmul(eq[0:EP, u, 0:EP], hot_hi_t16[:, j % 2, u, 0:EP], hot_hi_t16[:, j % 2, u, 0:EP],
                                           start=True, stop=True)
                        mm.then_inc(s_eq, 1)
                        if started(g, 1):
                            lookup(g - 1, j - 1)

                loop(pe, EG // 4, body)
                lookup(EG - 1, 3)

            @block.scalar
            def _(act):
                def body(i):
                    for j in range(4):
                        g = i * 4 + j
                        act.wait_ge(s_tr, g + 1)
                        wait(act, s_look, g - 1)
                        act.copy(hot_hi_t16[:, j % 2, :, 0:EP], tr[0:NT, :, 0:EP]).then_inc(s_hot_t, 1)
                        act.copy(hot_hi_t[:, j % 2, :, 0:EP], tr[0:NT, :, 0:EP]).then_inc(s_hot_t, 1)
                        act.wait_ge(s_pre, g + 1)
                        act.copy(earlier[:, j % 2, 1:U, :], prefix[:, 1:U, :]).then_inc(s_early, 1)
                        wait(act, s_scat[j], quarters(g, j, 16 * U))
                        act.copy(stage[:, j, :, :], pay[:, bass.ds(g * U, U), :]) \
                            .then_inc(s_stage, 1)

                loop(act, EG // 4, body)

            @block.gpsimd
            def _(pool):
                def body(i):
                    for j in range(4):
                        g = i * 4 + j
                        pool.wait_ge(s_idx, g + 1)
                        pool.wait_ge(s_stage, g + 1)
                        hold(pool, s_passed)
                        for u in range(U):
                            pool.indirect_dma_start(
                                slots_dram.rearrange("e t w -> (e t) w"),
                                bass.IndirectOffsetOnAxis(ap=idx[:, j, u:u + 1], axis=0),
                                stage[:, j, u, :], None).then_inc(s_scat[j], 16)

                loop(pool, EG // 4, body)
                for k in range(4):
                    pool.wait_ge(s_scat[k], EG // 4 * 16 * U)

        s_back, s_split = s.sem("back"), s.sem("split")
        with nc.Block() as block:
            @block.sync
            def _(sp):
                sp.dma_start(slots[:, :, :], slots_dram).then_inc(s_back, 16)

            @block.vector
            def _(dve):
                dve.wait_ge(s_back, 16)
                for w, array in enumerate(out.words):
                    dve.tensor_copy(array[:, :], slots[:, :, w]).then_inc(s_split, 1)
                dve.scalar_tensor_tensor(out=out.row[:, :], in0=out.tile_f[:, :], scalar=-float(P),
                                         in1=slots[:, :, words - 1], op0=ALU.mult, op1=ALU.add).then_inc(s_split, 1)


def halves(g, j, each, more=0):
    return (g - (j & 1) + 2 * more) * (each // 2)


def one_hot(dve, iotas, s_hot, hi, lo, hot_hi, hot_lo, g, j):
    for digit, hot, n in ((hi, hot_hi, NT), (lo, hot_lo, P)):
        dve.tensor_tensor(hot[:, j, :, :], iotas[:, 0:n, :],
                          digit[:, bass.ds(g * U, U)].unsqueeze(1).to_broadcast([EP, n, U]), ALU.is_equal) \
            .then_inc(s_hot, 1)


class Order:

    def __init__(self, c, name, words):
        self.words = [c.sb(f"{name}_{w}", [P, ST], dt) for w, dt in words]
        self.row = c.sb(f"{name}_row", [P, ST])
        self.start = c.sb(f"{name}_start", [NT, P])
        self.count = c.sb(f"{name}_count", [NT, P])
        self.tile_of = c.sb(f"{name}_tile_of", [1, ST // PACK], I32)


def dst_fields(src_dram, type_dram, norm_dram):
    def fields(s):
        src = s.sb("src", [EP, EC], I32)
        rel = s.sb("rel", [EP, EC], I32)
        norm = s.sb("norm", [EP, EC])

        def load(sp, sem=None):
            if sp is not None:
                sp.dma_start(src[:, :], src_dram.rearrange("(p c) -> p c", p=EP)).then_inc(sem, 16)
                sp.dma_start(rel[:, :], type_dram.rearrange("(p c) -> p c", p=EP)).then_inc(sem, 16)
                sp.dma_start(norm[:, :], norm_dram.rearrange("(p c) w -> p (c w)", p=EP)).then_inc(sem, 16)
            return 3

        def emit(dve, link, pay):
            link(dve.tensor_copy(pay[:, :, 0], src[:, :]))
            link(dve.scalar_tensor_tensor(out=pay[:, :, 1], in0=src[:, :],
                                          scalar=float(RELS), in1=rel[:, :], op0=ALU.mult, op1=ALU.add))
            link(dve.tensor_copy(pay[:, :, 2], norm[:, :]))
        return load, emit
    return fields


def src_fields(dst_dram):
    def fields(s):
        dst = s.sb("dst", [EP, EC], I32)

        def load(sp, sem=None):
            if sp is not None:
                sp.dma_start(dst[:, :], dst_dram.rearrange("(p c) -> p c", p=EP)).then_inc(sem, 16)
            return 1

        def emit(dve, link, pay):
            link(dve.tensor_copy(pay[:, :, 0], dst[:, :]))
        return load, emit
    return fields


def node_tiles(eng, body):
    def pair(i):
        body(2 * i, 0)
        body(2 * i + 1, 1)
    loop(eng, NT // 2, pair, peel=2)
    if NT % 2:
        body(NT - 1, 0)


def groups4(eng, count, body):
    def four(i):
        for j in range(4):
            body(i * 4 + j, j)
    loop(eng, count // 4, four)


def started(g, lag):
    return not (isinstance(g, int) and g < lag)


class Chain:

    def __init__(self, eng, sem, base=0):
        self.eng, self.sem, self.base, self.n = eng, sem, base, 0

    def step(self, ins):
        self.n += 1
        ins.then_inc(self.sem, 1)
        self.eng.wait_ge(self.sem, self.base + self.n)


def load_nodes(nc, c, x_dram):
    s_zero, s_x = c.sem("x_zero"), c.sem("x")
    with nc.Block() as block:
        @block.gpsimd
        def _(pool):
            pool.memset(c.x[:, NT - 1, :], 0.0).then_inc(s_zero, 1)

        @block.sync
        def _(sp):
            sp.dma_start(c.x[:, 0:NT - 1, :], x_dram[0:(NT - 1) * P, :].rearrange("(t p) d -> p t d", p=P)).then_inc(s_x, 16)
            sp.wait_ge(s_zero, 1)
            sp.dma_start(c.x[0:LAST, NT - 1, :], x_dram[(NT - 1) * P:N, :]).then_inc(s_x, 16)
            sp.wait_ge(s_x, 32)


def layer_norm_stats(nc, c, name):
    with ExitStack() as ctx:
        s = Scope(nc, ctx, name)
        st = s.sb("stats", [P, NT, 6])
        mean = s.sb("mean", [P, NT])
        gap = s.sb("gap", [P, NT])
        var = s.sb("var", [P, NT])
        eps = s.sb("eps", [P, 1])
        std = s.sb("std", [P, NT])
        s_bn, s_step, s_var, s_std, s_end = (s.sem(x) for x in ("bn", "step", "var", "std", "end"))
        with nc.Block() as block:
            @block.vector
            def _(dve):
                dve.memset(eps[:, :], EPS).then_inc(s_bn, 1)

                def statistics(i):
                    for k in range(7):
                        dve.bn_stats(st[:, bass.ds(i * 7 + k, 1), :].rearrange("p a b -> p (a b)"),
                                     c.x[:, bass.ds(i * 7 + k, 1), :].rearrange("p a b -> p (a b)")).then_inc(s_bn, 1)
                assert NT % 7 == 0
                loop(dve, NT // 7, statistics)
                dve.wait_ge(s_bn, NT + 1)
                ch = Chain(dve, s_step)
                ch.step(dve.tensor_tensor(mean[:, :], st[:, :, 1], st[:, :, 4], ALU.add))
                ch.step(dve.tensor_tensor(gap[:, :], st[:, :, 1], st[:, :, 4], ALU.subtract))
                ch.step(dve.tensor_tensor(var[:, :], st[:, :, 2], st[:, :, 5], ALU.add))
                ch.step(dve.tensor_scalar(mean[:, :], mean[:, :], 0.5, None, ALU.mult))
                ch.step(dve.tensor_tensor(gap[:, :], gap[:, :], gap[:, :], ALU.mult))
                ch.step(dve.tensor_scalar(gap[:, :], gap[:, :], 0.25, None, ALU.mult))
                dve.scalar_tensor_tensor(out=var[:, :], in0=var[:, :], scalar=1.0 / D, in1=gap[:, :],
                                         op0=ALU.mult, op1=ALU.add).then_inc(s_var, 1)
                dve.wait_ge(s_std, 1)
                ch.step(dve.reciprocal(c.rstd[:, :], std[:, :]))
                dve.scalar_tensor_tensor(out=c.shift[:, :], in0=mean[:, :], scalar=-1.0, in1=c.rstd[:, :],
                                         op0=ALU.mult, op1=ALU.mult).then_inc(s_end, 1)

            @block.scalar
            def _(act):
                act.wait_ge(s_bn, 1)
                act.wait_ge(s_var, 1)
                act.activation(std[:, :], var[:, :], ACT.Sqrt, bias=eps[:, 0:1]).then_inc(s_std, 1)


def hidden_rows(act, c, h, j, k):
    return act.activation(h[:, k, :], c.x[:, bass.ds(j, 1), :].rearrange("p a b -> p (a b)"), ACT.Relu,
                          bias=c.shift[:, bass.ds(j, 1)], scale=c.rstd[:, bass.ds(j, 1)])


def attention_scalars(nc, c, name, w, w_loads, att_drams, heads, small_dram):
    H = heads
    with ExitStack() as ctx:
        s = Scope(nc, ctx, name)
        h = s.sb("h", [P, 2, D])
        h_t = s.sb("h_t", [P, 2, 2, P])
        vec = s.sb("vec", [P, 2, D])
        prod = s.sb("prod", [P, 2, 2, D])
        fold = s.sb("fold", [P, 2, 2 * H])
        ps = s.psum("ps", [P, 4, 512])
        s_w, s_prod, s_fold, s_small = (s.sem(x) for x in ("w", "prod", "fold", "small"))
        s_h, s_tr, s_ht, s_mm, s_att = (s.sem(x) for x in ("h", "tr", "ht", "mm", "att"))
        with nc.Block() as block:
            @block.sync
            def _(sp):
                for to, of in w_loads:
                    sp.dma_start(to, of).then_inc(s_w, 16)
                for i in range(2):
                    sp.dma_start(vec[:, i, :], att_drams[i].partition_broadcast(P)).then_inc(s_w, 16)
                sp.wait_ge(s_att, NT)
                sp.dma_start(small_dram.rearrange("(t p) h -> p t h", p=P), c.att[:, :, 0:H]).then_inc(s_small, 16)
                sp.wait_ge(s_small, 16)

            @block.scalar
            def _(act):
                def body(j, k):
                    wait(act, s_tr, j - 1)
                    hidden_rows(act, c, h, j, k).then_inc(s_h, 1)
                node_tiles(act, body)

            @block.tensor
            def _(pe):
                def turn(j, k):
                    pe.wait_ge(s_h, j + 1)
                    wait(pe, s_ht, j - 1)
                    pe.wait_ge(c.ready, 5)
                    for half in range(2):
                        mm = pe.transpose(ps[:, k, half * P:(half + 1) * P], h[:, k, half * P:(half + 1) * P], c.ident[:, :])
                    mm.then_inc(s_tr, 1)

                def product(j, k):
                    pe.wait_ge(s_ht, j + 1)
                    wait(pe, s_att, j - 1)
                    for half in range(2):
                        mm = pe.matmul(ps[:, 2 + k, 0:2 * H], h_t[:, k, half, :], fold[:, half, :],
                                       start=half == 0, stop=half == 1)
                    mm.then_inc(s_mm, 1)

                def body(j, k):
                    turn(j, k)
                    if started(j, 1):
                        product(j - 1, 1 - k)
                pe.wait_ge(s_fold, 2)
                node_tiles(pe, body)
                product(NT - 1, (NT - 1) % 2)

            @block.vector
            def _(dve):
                dve.wait_ge(s_w, 16 * (len(w_loads) + 2))
                for i in range(2):
                    dve.tensor_tensor(prod[:, i, :, :], w[:, :, :], vec[:, i, :].unsqueeze(1).to_broadcast([P, 2, D]),
                                      ALU.mult).then_inc(s_prod, 1)
                for i in range(2):
                    dve.wait_ge(s_prod, i + 1)
                    dve.tensor_reduce(fold[:, :, i * H:(i + 1) * H],
                                      prod[:, i, :, :].rearrange("p k (h d) -> p k h d", h=H), AX.X, ALU.add) \
                        .then_inc(s_fold, 1)

                def turned(j, k):
                    dve.wait_ge(s_tr, j + 1)
                    wait(dve, s_mm, j - 1)
                    dve.tensor_copy(h_t[:, k, :, :], ps[:, k, 0:D].rearrange("p (a b) -> p a b", a=2)).then_inc(s_ht, 1)

                def keep(j, k):
                    dve.wait_ge(s_mm, j + 1)
                    dve.tensor_copy(c.att[:, bass.ds(j, 1), :].squeeze(1), ps[:, 2 + k, 0:2 * H]).then_inc(s_att, 1)

                def body(j, k):
                    turned(j, k)
                    if started(j, 1):
                        keep(j - 1, 1 - k)
                node_tiles(dve, body)
                keep(NT - 1, (NT - 1) % 2)


def project_and_gather(nc, c, name, w, table_dram, add_h, gather_idx, heads, small_dram, gathered, pool_groups):
    H = heads
    IN_BANK = 512 // (NT * H)
    B = 2 * IN_BANK
    PARTS = U // (2 * B)
    FIRST = pool_groups
    LG = SG - FIRST
    assert pool_groups % 4 == 0 and LG % 4 == 0 and U % (2 * B) == 0
    with ExitStack() as ctx:
        s = Scope(nc, ctx, name)
        h = s.sb("h", [P, 2, D])
        h_t = s.sb("h_t", [P, 2, 2, P])
        rows = s.sb("rows", [P, 2, D])
        idx = s.sb("idx", [P, 4, U], U32)
        ring = s.sb("ring", [P, 4, U, H])
        digit = s.sb("digit", [P, ST], U32)
        hi = s.sb("hi", [P, ST], F16)
        lo = s.sb("lo", [P, ST], F16)
        iotas = s.sb("iotas", [P, P, U], F16)
        hot_hi = s.sb("hot_hi", [P, 2, NT, U], F16)
        hot_lo = s.sb("hot_lo", [P, 2, P, U], F16)
        hot_t = s.sb("hot_t", [P, 2, U, P])
        masked = s.sb("masked", [P, U, H, NT])
        ps = s.psum("ps", [P, 6, 512])
        turned_h = ps[:, 0:2, 0:D]
        product = ps[:, 2:4, 0:D]
        look = ps[:, 0:4, :]
        turned_hot = ps[:, 4:6, :].bitcast(F16).rearrange("p k (u e) -> p k u e", u=U)
        s_h, s_tr, s_ht, s_mm, s_x, s_rows = (s.sem(x) for x in ("h", "tr", "ht", "mm", "x", "rows"))
        s_out = [s.sem(f"out{k}") for k in range(2)]
        s_idx = [s.sem(f"idx{k}") for k in range(4)]
        s_gat = [s.sem(f"gat{k}") for k in range(4)]
        s_kept = [s.sem(f"kept{k}") for k in range(4)]
        s_passed, s_prep, s_hot, s_turn = (s.sem(x) for x in ("passed", "prep", "hot", "turn"))
        s_hot_t, s_look, s_mask, s_found = (s.sem(x) for x in ("hot_t", "look", "mask", "found"))
        s_turn_passed = s.sem("turn_passed")
        with nc.Block() as block:
            @block.sync
            def _(sp):
                def keep(g, j):
                    sp.wait_ge(s_gat[j], quarters(g, j, 16 * U, 1))
                    sp.dma_start(gathered[:, bass.ds(g * U, U), :], ring[:, j, :, :]).then_inc(s_kept[j], 16)

                def body(g, j):
                    sp.dma_start(idx[:, j, :], gather_idx[:, bass.ds(g * U, U)]).then_inc(s_idx[j], 16)
                    if started(g, 2):
                        keep(g - 2, (j - 2) % 4)
                groups4(sp, pool_groups, body)
                keep(pool_groups - 2, 2)
                keep(pool_groups - 1, 3)
                for j in range(4):
                    sp.wait_ge(s_kept[j], 16 * (pool_groups // 4))

            @block.gpsimd
            def _(pool):
                def body(g, j):
                    pool.wait_ge(s_idx[j], quarters(g, j, 16, 1))
                    wait(pool, s_kept[j], quarters(g, j, 16))
                    hold(pool, s_passed)
                    for u in range(U):
                        pool.indirect_dma_start(ring[:, j, u, :], None, small_dram,
                                                bass.IndirectOffsetOnAxis(ap=idx[:, j, u:u + 1], axis=0)) \
                            .then_inc(s_gat[j], 16)
                groups4(pool, pool_groups, body)

            @block.scalar
            def _(act):
                def store(j, k):
                    act.wait_ge(s_rows, j + 1)
                    act.dma_start(table_dram[bass.ds(j * P, P), :], rows[:, k, :]).then_inc(s_out[k], 16)

                def body(j, k):
                    wait(act, s_tr, j - 1)
                    wait(act, s_x, j - 1 if add_h else 0)
                    hidden_rows(act, c, h, j, k).then_inc(s_h, 1)
                    if started(j, 2):
                        store(j - 2, k)
                node_tiles(act, body)
                store(NT - 2, (NT - 2) % 2)
                store(NT - 1, (NT - 1) % 2)

                def copy_turned(g, j):
                    act.wait_ge(s_turn, g + 1)
                    wait(act, s_look, (g - 1) * (U // B))
                    act.copy(hot_t[:, j % 2, :, :], turned_hot[:, j % 2, :, :]).then_inc(s_hot_t, 1)
                groups4(act, LG, copy_turned)
                act.wait_ge(s_out[0], 16 * (NT - NT // 2))
                act.wait_ge(s_out[1], 16 * (NT // 2))

            @block.tensor
            def _(pe):
                def turn(j, k):
                    pe.wait_ge(s_h, j + 1)
                    wait(pe, s_ht, j - 1)
                    pe.wait_ge(c.ready, 5)
                    for half in range(2):
                        mm = pe.transpose(turned_h[:, k, half * P:(half + 1) * P], h[:, k, half * P:(half + 1) * P],
                                          c.ident[:, :])
                    mm.then_inc(s_tr, 1)

                def multiply(j, k):
                    pe.wait_ge(s_ht, j + 1)
                    wait(pe, s_rows, j - 1)
                    for half in range(2):
                        mm = pe.matmul(product[:, k, :], h_t[:, k, half, :], w[:, half, :], start=half == 0, stop=half == 1)
                    mm.then_inc(s_mm, 1)

                def body(j, k):
                    turn(j, k)
                    if started(j, 1):
                        multiply(j - 1, 1 - k)
                node_tiles(pe, body)
                multiply(NT - 1, (NT - 1) % 2)

                def turn_hot(g, j):
                    pe.wait_ge(s_hot, 2 * g + 2)
                    wait(pe, s_hot_t, g - 1)
                    hold(pe, s_turn_passed)
                    for u in range(U):
                        mm = pe.transpose(turned_hot[:, j % 2, u, :], hot_lo[:, j % 2, :, u], c.ident16[:, :])
                    mm.then_inc(s_turn, 1)

                def lookup(g, j):
                    pe.wait_ge(s_hot_t, g + 1)
                    for b in range(U // B):
                        wait(pe, s_mask, g * (U // B) + b - 1)
                        for i in range(B):
                            to = look[:, b % 2 * 2 + i // IN_BANK, i % IN_BANK * NT * H:(i % IN_BANK + 1) * NT * H]
                            mm = pe.matmul(to.rearrange("p (t h) -> p t h", h=H), hot_t[:, j % 2, b * B + i, :],
                                           c.att[:, :, 0:H], start=True, stop=True)
                        mm.then_inc(s_look, 1)

                def look_body(g, j):
                    if started(g, 1):
                        lookup(g - 1, (j - 1) % 4)
                    turn_hot(g, j)
                groups4(pe, LG, look_body)
                lookup(LG - 1, 3)

            @block.vector
            def _(dve):
                ch = Chain(dve, s_prep)
                for shift, mask, to in ((7, None, hi), (None, P - 1, lo)):
                    if shift is not None:
                        ch.step(dve.tensor_scalar(digit[:, :], gather_idx[:, :], shift, None, ALU.logical_shift_right))
                    else:
                        ch.step(dve.tensor_scalar(digit[:, :], gather_idx[:, :], mask, None, ALU.bitwise_and))
                    ch.step(dve.tensor_copy(to[:, :], digit[:, :]))
                ch.step(dve.tensor_copy(iotas[:, :, :], c.iota[:, :].unsqueeze(2).to_broadcast([P, P, U])))

                def turned(j, k):
                    dve.wait_ge(s_tr, j + 1)
                    wait(dve, s_mm, j - 1)
                    dve.tensor_copy(h_t[:, k, :, :], turned_h[:, k, :].rearrange("p (a b) -> p a b", a=2)).then_inc(s_ht, 1)
                    if add_h:
                        xj = c.x[:, bass.ds(j, 1), :].rearrange("p a b -> p (a b)")
                        dve.tensor_tensor(xj, xj, h[:, k, :], ALU.add).then_inc(s_x, 1)

                def keep(j, k):
                    dve.wait_ge(s_mm, j + 1)
                    wait(dve, s_out[k], halves(j, k, 16))
                    dve.tensor_copy(rows[:, k, :], product[:, k, :]).then_inc(s_rows, 1)

                def body(j, k):
                    turned(j, k)
                    if started(j, 1):
                        keep(j - 1, 1 - k)
                node_tiles(dve, body)
                keep(NT - 1, (NT - 1) % 2)

                def one_hots(g, j):
                    wait(dve, s_turn, g - 1)
                    for digits, hot, n in ((hi, hot_hi, NT), (lo, hot_lo, P)):
                        dve.tensor_tensor(hot[:, j % 2, :, :], iotas[:, 0:n, :],
                                          digits[:, bass.ds((g + FIRST) * U, U)].unsqueeze(1).to_broadcast([P, n, U]),
                                          ALU.is_equal).then_inc(s_hot, 1)

                def find(g, j):
                    dve.wait_ge(s_hot, 2 * g + 2)
                    for part in range(PARTS):
                        wait(dve, s_found, (g - 1) * PARTS + part + 1 if started(g, 1) else 0)
                        for b in range(2 * part, 2 * part + 2):
                            dve.wait_ge(s_look, g * (U // B) + b + 1)
                            for i in range(2):
                                t = b * B + i * IN_BANK
                                ins = dve.tensor_tensor(
                                    masked[:, t:t + IN_BANK, :, :].rearrange("p u h t -> p u t h"),
                                    look[:, b % 2 * 2 + i, 0:IN_BANK * NT * H]
                                    .rearrange("p (u t h) -> p u t h", u=IN_BANK, h=H),
                                    hot_hi[:, j % 2, :, t:t + IN_BANK].rearrange("p t u -> p u t").unsqueeze(3)
                                    .to_broadcast([P, IN_BANK, NT, H]), ALU.mult)
                            ins.then_inc(s_mask, 1)
                        dve.wait_ge(s_mask, g * (U // B) + 2 * part + 2)
                        dve.tensor_reduce(gathered[:, bass.ds((g + FIRST) * U + part * 2 * B, 2 * B), :],
                                          masked[:, part * 2 * B:(part + 1) * 2 * B, :, :], AX.X, ALU.add) \
                            .then_inc(s_found, 1)

                def look_body(g, j):
                    one_hots(g, j)
                    if started(g, 1):
                        find(g - 1, (j - 1) % 4)
                groups4(dve, LG, look_body)
                find(LG - 1, 3)


def project_normed(nc, c, name, w_dram, table_dram, affine, scale_rows):
    with ExitStack() as ctx:
        s = Scope(nc, ctx, name)
        h = s.sb("h", [P, 2, D])
        h_t = s.sb("h_t", [P, 2, 2, P])
        rows = s.sb("rows", [P, 2, D])
        w = s.sb("w", [P, 2, D])
        ps = s.psum("ps", [P, 8, 512])
        s_w, s_h, s_tr, s_ht, s_mm, s_rows = (s.sem(x) for x in ("w", "h", "tr", "ht", "mm", "rows"))
        s_out = [s.sem(f"out{k}") for k in range(2)]
        s_half, s_pre = s.sem("half"), s.sem("pre")
        cols = s.sb("cols", [P, 4, 2])
        eps = s.sb("eps", [P, 1])
        gain = s.sb("gain", [P, 2])
        loads = [(w[:, :, :], w_dram.rearrange("(k p) n -> p k n", p=P))]
        loads += [(cols[:, i, :], a.rearrange("(k p) -> p k", p=P)) for i, a in enumerate(affine)]
        with nc.Block() as block:
            @block.sync
            def _(sp):
                for to, of in loads:
                    sp.dma_start(to, of, allow_slow_non_contiguous=True).then_inc(s_w, 16)

                def body(j, k):
                    sp.wait_ge(s_rows, j + 1)
                    sp.dma_start(table_dram[bass.ds(j * P, P), :], rows[:, k, :]).then_inc(s_out[k], 16)
                node_tiles(sp, body)
                sp.wait_ge(s_out[0], 16 * (NT - NT // 2))
                sp.wait_ge(s_out[1], 16 * (NT // 2))

            @block.scalar
            def _(act):
                act.wait_ge(s_pre, 1)
                act.wait_ge(s_w, 16 * len(loads))
                act.activation(gain[:, :], cols[:, 3, :], ACT.Sqrt, bias=eps[:, 0:1]).then_inc(s_pre, 1)

                def body(j, k):
                    wait(act, s_tr, j - 1)
                    hidden_rows(act, c, h, j, k).then_inc(s_h, 1)
                node_tiles(act, body)

            @block.tensor
            def _(pe):
                pe.wait_ge(s_w, 16 * len(loads))

                def turn(j, k):
                    pe.wait_ge(s_h, j + 1)
                    wait(pe, s_ht, j - 1)
                    pe.wait_ge(c.ready, 5)
                    for half in range(2):
                        mm = pe.transpose(ps[:, k, half * P:(half + 1) * P], h[:, k, half * P:(half + 1) * P], c.ident[:, :])
                    mm.then_inc(s_tr, 1)

                def product(j, k):
                    pe.wait_ge(s_ht, j + 1)
                    wait(pe, s_rows, j - 1)
                    for half in range(2):
                        mm = pe.matmul(ps[:, 2 + k, 0:D], h_t[:, k, half, :], w[:, half, :], start=half == 0, stop=half == 1)
                    mm.then_inc(s_mm, 1)

                def body(j, k):
                    turn(j, k)
                    if started(j, 1):
                        product(j - 1, 1 - k)
                node_tiles(pe, body)
                product(NT - 1, (NT - 1) % 2)

            @block.vector
            def _(dve):
                ch = Chain(dve, s_pre)
                ch.step(dve.memset(eps[:, :], EPS))
                dve.wait_ge(s_w, 16 * len(loads))
                dve.wait_ge(s_pre, 2)
                ch.base = 1
                ch.step(dve.reciprocal(gain[:, :], gain[:, :]))
                ch.step(dve.tensor_tensor(gain[:, :], gain[:, :], cols[:, 0, :], ALU.mult))

                def turned(j, k):
                    dve.wait_ge(s_tr, j + 1)
                    wait(dve, s_mm, j - 1)
                    for half in range(2):
                        ins = dve.tensor_scalar(h_t[:, k, half, :], ps[:, k, half * P:(half + 1) * P],
                                                cols[:, 2, half:half + 1], gain[:, half:half + 1],
                                                ALU.subtract, ALU.mult)
                        ins.then_inc(s_half, 1)
                    for half in range(2):
                        dve.wait_ge(s_half, 2 * j + half + 1)
                        ins = dve.tensor_scalar(h_t[:, k, half, :], h_t[:, k, half, :], cols[:, 1, half:half + 1], None,
                                                ALU.add)
                    ins.then_inc(s_ht, 1)

                def keep(j, k):
                    dve.wait_ge(s_mm, j + 1)
                    wait(dve, s_out[k], halves(j, k, 16))
                    dve.tensor_scalar(rows[:, k, :], ps[:, 2 + k, 0:D], scale_rows[:, bass.ds(j, 1)], None,
                                      ALU.mult).then_inc(s_rows, 1)

                def body(j, k):
                    turned(j, k)
                    if started(j, 1):
                        keep(j - 1, 1 - k)
                node_tiles(dve, body)
                keep(NT - 1, (NT - 1) % 2)


def segment_max(nc, c, name, order, heads, gathered, carry_dram, carry2_dram, rows_dram):
    C = P // heads
    TB = ST // C
    L = TB * P
    with ExitStack() as ctx:
        s = Scope(nc, ctx, name)
        s_max = s.sem("max")
        key_t = s.sb("key_t", [P, TB, P])
        val_t = s.sb("val_t", [P, TB, P])
        new_t = s.sb("new_t", [P, TB, P])
        stage = s.sb("stage", [P, 2, 2, C, heads])
        ps = s.psum("ps", [P, 8, 512])
        s_st, s_tr, s_cp = s.sem("st"), s.sem("tr"), s.sem("cp")
        by_chunk = [order.key[:, :].rearrange("p (c b) -> p b c", c=C).unsqueeze(3).to_broadcast([P, TB, C, heads]),
                    gathered[:, :, 0:heads].rearrange("p (c b) h -> p b c h", c=C)]

        def batches(eng, body):
            loop(eng, TB // 2, lambda i: [body(i * 2 + k, k) for k in range(2)])

        with nc.Block() as block:
            @block.vector
            def _(dve):
                def body(b, k):
                    wait(dve, s_tr, (b - 1) * 2)
                    for i in range(2):
                        dve.tensor_copy(stage[:, k, i, :, :], by_chunk[i][:, bass.ds(b, 1), :, :].squeeze(1)) \
                            .then_inc(s_st, 1)
                batches(dve, body)

            @block.tensor
            def _(pe):
                def body(b, k):
                    pe.wait_ge(s_st, b * 2 + 2)
                    wait(pe, s_cp, (b - 1) * 2)
                    pe.wait_ge(c.ready, 5)
                    for i in range(2):
                        pe.transpose(ps[:, 2 * k + i, 0:P], stage[:, k, i, :, :].rearrange("p c h -> p (c h)"), c.ident[:, :]) \
                            .then_inc(s_tr, 1)
                batches(pe, body)

            @block.scalar
            def _(act):
                def body(b, k):
                    act.wait_ge(s_tr, b * 2 + 2)
                    for i, to in enumerate((key_t, val_t)):
                        act.copy(to[:, bass.ds(b, 1), :].rearrange("p a e -> p (a e)"), ps[:, 2 * k + i, 0:P]).then_inc(s_cp, 1)
                batches(act, body)
                act.wait_ge(s_cp, 2 * TB)

        key_l = key_t[:, :, :].rearrange("p b e -> p (b e)")
        val_l = val_t[:, :, :].rearrange("p b e -> p (b e)")
        new_l = new_t[:, :, :].rearrange("p b e -> p (b e)")
        ends = s.sb("ends", [P, 3])
        ch_in = s.sb("ch_in", [heads, C, 3])
        cont = s.sb("cont", [heads, C])
        whole = s.sb("whole", [heads, C])
        run = s.sb("run", [heads, C])
        carry = s.sb("carry", [heads, C, 2])
        carried = s.sb("carried", [P, 2])
        last_slot = s.sb("last_slot", [NT, P])
        slot_i = s.sb("slot_i", [NT, P], I32)
        tile_i = s.sb("tile_i", [NT, P], I32)
        tile_f = s.sb("tile_f", [NT, P])
        row_f = s.sb("row_f", [NT, P])
        back = s.sb("back", [P, 2, P])
        row_idx = s.sb("row_idx", [P, NT], U32)
        s_v, s_d, s_e, s_f = s.sem("v"), s.sem("d"), s.sem("e"), s.sem("f")
        s_t2, s_c2, s_b2, s_r = s.sem("t2"), s.sem("c2"), s.sem("b2"), s.sem("r")
        s_rows = s.sem("rows")
        back_e = val_t[:, :, :].rearrange("p b e -> p (b e)").rearrange("p (c b h) -> p b c h", c=C, h=heads)
        with nc.Block() as block:
            @block.sync
            def _(sp):
                sp.wait_ge(s_e, 1)
                sp.dma_start(carry_dram, ends[:, :]).then_inc(s_d, 16)
                sp.wait_ge(s_d, 16)
                sp.dma_start(ch_in[:, :, :], carry_dram.rearrange("(c h) k -> h c k", h=heads)).then_inc(s_d, 16)
                sp.wait_ge(s_e, 2)
                sp.dma_start(carry2_dram.rearrange("(c h) k -> h c k", h=heads), carry[:, :, :]).then_inc(s_d, 16)
                sp.wait_ge(s_d, 48)
                sp.dma_start(carried[:, :], carry2_dram).then_inc(s_d, 16)
                sp.wait_ge(s_c2, TB)
                sp.dma_start(rows_dram.rearrange("(e t) h -> e (t h)", e=P), val_l).then_inc(s_rows, 16)
                sp.wait_ge(s_rows, 16)

            @block.vector
            def _(dve):
                ch = Chain(dve, s_v)
                ch.step(dve.tensor_tensor(last_slot[:, :], order.start[:, :], order.count[:, :], ALU.add))
                ch.step(dve.tensor_scalar(last_slot[:, :], last_slot[:, :], -1.0, 0.0, ALU.add, ALU.max))
                ch.step(dve.tensor_copy(slot_i[:, :], last_slot[:, :]))
                ch.step(dve.tensor_scalar(tile_i[:, :], slot_i[:, :], 7, None, ALU.arith_shift_right))
                ch.step(dve.tensor_copy(tile_f[:, :], tile_i[:, :]))
                ch.step(dve.scalar_tensor_tensor(out=row_f[:, :], in0=tile_f[:, :], scalar=-float(P),
                                                 in1=last_slot[:, :], op0=ALU.mult, op1=ALU.add))
                dve.scalar_tensor_tensor(out=row_f[:, :], in0=row_f[:, :], scalar=float(ST),
                                         in1=tile_f[:, :], op0=ALU.mult, op1=ALU.add).then_inc(s_r, 1)
                dve.wait_ge(s_r, 1)
                ch.step(dve.tensor_tensor(new_l[:, 1:L], key_l[:, 1:L], key_l[:, 0:L - 1], ALU.not_equal))
                ch.step(dve.tensor_scalar(new_l[:, 1:L], new_l[:, 1:L], -BIG, None, ALU.mult))
                ch.step(dve.memset(new_l[:, 0:1], 0.0))
                ch.step(dve.tensor_copy(ends[:, 0:1], key_l[:, 0:1]))
                ch.step(dve.tensor_copy(ends[:, 1:2], key_l[:, L - 1:L]))
                ch.step(dve.tensor_tensor_scan(key_l, new_l, val_l, -BIG, ALU.add, ALU.max))
                dve.tensor_copy(ends[:, 2:3], key_l[:, L - 1:L]).then_inc(s_e, 1)
                dve.wait_ge(s_d, 32)
                ch.step(dve.tensor_tensor(cont[:, 1:C], ch_in[:, 1:C, 0], ch_in[:, 0:C - 1, 1], ALU.is_equal))
                ch.step(dve.memset(cont[:, 0:1], 0.0))
                ch.step(dve.tensor_tensor(whole[:, :], ch_in[:, :, 0], ch_in[:, :, 1], ALU.is_equal))
                ch.step(dve.tensor_tensor(whole[:, :], whole[:, :], cont[:, :], ALU.mult))
                ch.step(dve.tensor_scalar(whole[:, :], whole[:, :], 1.0, BIG, ALU.subtract, ALU.mult))
                ch.step(dve.tensor_tensor_scan(run[:, :], whole[:, :], ch_in[:, :, 2], -BIG, ALU.add, ALU.max))
                ch.step(dve.memset(carry[:, 0:1, 0:1], -BIG))
                ch.step(dve.tensor_copy(carry[:, 1:C, 0], run[:, 0:C - 1]))
                dve.tensor_scalar(carry[:, :, 1], cont[:, :], 1.0, BIG, ALU.subtract, ALU.mult).then_inc(s_e, 1)
                dve.wait_ge(s_d, 64)
                ch.step(dve.tensor_copy(new_l[:, 0:1], carried[:, 1:2]))
                dve.tensor_tensor_scan(key_l, new_l, val_l, carried[:, 0:1], ALU.add, ALU.max).then_inc(s_f, 1)
                dve.wait_ge(s_f, 1)

                def body(b, k):
                    wait(dve, s_t2, b - 1)
                    dve.tensor_copy(back[:, k, :], key_t[:, bass.ds(b, 1), :].rearrange("p a e -> p (a e)")).then_inc(s_b2, 1)
                batches(dve, body)
                dve.wait_ge(s_r, 2)
                dve.tensor_copy(row_idx[:, :], ps[:, 4, 0:NT]).then_inc(s_r, 1)
                dve.wait_ge(s_r, 3)

            @block.tensor
            def _(pe):
                pe.wait_ge(s_r, 1)
                pe.transpose(ps[:, 4, 0:NT], row_f[:, :], c.ident[0:NT, 0:NT]).then_inc(s_r, 1)

                def body(b, k):
                    pe.wait_ge(s_b2, b + 1)
                    wait(pe, s_c2, b - 1)
                    pe.wait_ge(c.ready, 5)
                    pe.transpose(ps[:, k, 0:P], back[:, k, :], c.ident[:, :]).then_inc(s_t2, 1)
                batches(pe, body)

            @block.scalar
            def _(act):
                act.wait_ge(s_f, 1)

                def body(b, k):
                    act.wait_ge(s_t2, b + 1)
                    act.copy(back_e[:, bass.ds(b, 1), :, :].squeeze(1),
                             ps[:, k, 0:P].rearrange("p (c h) -> p c h", c=C)).then_inc(s_c2, 1)
                batches(act, body)

        with nc.Block() as block:
            @block.gpsimd
            def _(pool):
                for t in range(NT):
                    pool.indirect_dma_start(c.seg_max[:, t, 0:heads], None, rows_dram,
                                            bass.IndirectOffsetOnAxis(ap=row_idx[:, t:t + 1], axis=0)).then_inc(s_max, 16)
                pool.wait_ge(s_max, 16 * NT)


def quarters(g, j, each, more=0):
    return (g - j + 4 * more) * (each // 4)


def count_columns(nc, c, name, order):
    with ExitStack() as ctx:
        s = Scope(nc, ctx, name)
        ps = s.psum("ps", [P, 512])
        s_t, s_c = s.sem("t"), s.sem("c")
        with nc.Block() as block:
            @block.tensor
            def _(pe):
                pe.transpose(ps[:, 0:NT], order.count[:, :], c.ident[0:NT, 0:NT]).then_inc(s_t, 1)

            @block.vector
            def _(dve):
                dve.wait_ge(s_t, 1)
                dve.tensor_copy(c.degree[:, :], ps[:, 0:NT]).then_inc(s_c, 1)
                dve.wait_ge(s_c, 1)


def attention_nodes(nc, c, name, heads, table_dram, loops):
    H = heads
    with ExitStack() as ctx:
        s = Scope(nc, ctx, name)
        z = s.sb("z", [P, NT, H])
        m = s.sb("m", [P, NT, H])
        has = s.sb("has", [P, NT])
        weight = s.sb("weight", [P, NT, H])
        s_x, s_v, s_z, s_w, s_end = (s.sem(a) for a in ("x", "v", "z", "w", "end"))
        with nc.Block() as block:
            @block.sync
            def _(sp):
                if loops:
                    sp.dma_start(c.acc[:, :, 0:D], table_dram.rearrange("(t p) d -> p t d", p=P)).then_inc(s_x, 16)

            @block.vector
            def _(dve):
                ch = Chain(dve, s_v)
                g, n = c.att[:, :, 0:H], c.att[:, :, H:2 * H]
                hb = has[:, :].unsqueeze(2).to_broadcast([P, NT, H])
                ch.step(dve.tensor_scalar(has[:, :], c.degree[:, :], 1.0, None, ALU.min))
                ch.step(dve.tensor_tensor(m[:, :, :], c.seg_max[:, :, 0:H], hb, ALU.mult))
                ch.step(dve.tensor_scalar(has[:, :], has[:, :], 1.0, BIG, ALU.subtract, ALU.mult))
                ch.step(dve.tensor_tensor(m[:, :, :], m[:, :, :], hb, ALU.add))
                if loops:
                    ch.step(dve.tensor_tensor(m[:, :, :], m[:, :, :], g, ALU.max))
                ch.step(dve.tensor_tensor(m[:, :, :], m[:, :, :], n, ALU.add))
                ch.step(dve.scalar_tensor_tensor(out=c.pair[:, :, H:2 * H], in0=m[:, :, :], scalar=0.2, in1=m[:, :, :],
                                                 op0=ALU.mult, op1=ALU.max))
                ch.step(dve.tensor_copy(c.pair[:, :, 0:H], n))
                if not loops:
                    dve.memset(c.acc[:, :, 0:D + H], 0.0).then_inc(s_end, 1)
                    dve.wait_ge(s_end, 1)
                    return
                ch.step(dve.tensor_tensor(z[:, :, :], g, n, ALU.add))
                ch.step(dve.scalar_tensor_tensor(out=z[:, :, :], in0=z[:, :, :], scalar=0.2, in1=z[:, :, :],
                                                 op0=ALU.mult, op1=ALU.max))
                dve.tensor_tensor(z[:, :, :], z[:, :, :], c.pair[:, :, H:2 * H], ALU.subtract).then_inc(s_z, 1)
                dve.wait_ge(s_w, 1)
                dve.wait_ge(s_x, 16)
                ch.step(dve.tensor_copy(c.acc[:, :, D:D + H], weight[:, :, :]))
                for t in range(0, NT, 7):
                    acc = c.acc[:, t:t + 7, 0:D].rearrange("p t (h d) -> p t h d", h=H)
                    dve.tensor_tensor(acc, acc, weight[:, t:t + 7, :].unsqueeze(3).to_broadcast([P, 7, H, D // H]),
                                      ALU.mult).then_inc(s_end, 1)
                dve.wait_ge(s_end, NT // 7)

            @block.scalar
            def _(act):
                if loops:
                    act.wait_ge(s_z, 1)
                    act.activation(weight[:, :, :], z[:, :, :], ACT.Exp).then_inc(s_w, 1)


def tile_registers(nc, eng, order, g, q):
    word = eng.value_load(order.tile_of[0:1, bass.ds(g * (U // PACK) + q, 1)], min_val=0, max_val=(1 << 24) - 1)
    return [nc.s_assert_within(eng.snap((word >> (PBITS * k)) & ((1 << PBITS) - 1)), 0, NT - 1,
                               skip_runtime_bounds_check_because="each field is a node tile by its making")
            for k in range(PACK)]


def stage_indices(sp, order_idx, idx, s_idx, s_gat, more=None):
    def body(g, j):
        wait(sp, s_gat[j % 2], halves(g, j, 16 * U, -1) if started(g, 4) else 0)
        sp.dma_start(idx[:, j, :], order_idx[:, bass.ds(g * U, U)]).then_inc(s_idx[j], 16)
        if more is not None:
            more(g, j)
    groups4(sp, SG, body)


def gather_rows(pool, table_dram, idx, rows, s_idx, s_gat, s_agg, s_passed):
    def body(g, j):
        pool.wait_ge(s_idx[j], quarters(g, j, 16, 1))
        for u in range(U):
            wait(pool, s_agg, g * U + u - 2 * U + 1 if started(g, 2) else 0)
            hold(pool, s_passed)
            pool.indirect_dma_start(rows[:, j % 2, u, 0:D], None, table_dram,
                                    bass.IndirectOffsetOnAxis(ap=idx[:, j, u:u + 1], axis=0)).then_inc(s_gat[j % 2], 16)
    groups4(pool, SG, body)


def gather_sum(nc, c, name, order, gather_idx, table_dram, norm=None):
    BANKS = 8
    with ExitStack() as ctx:
        s = Scope(nc, ctx, name)
        idx = s.sb("idx", [P, 4, U], U32)
        rows = s.sb("rows", [P, 2, U, D])
        sel = s.sb("sel", [P, 2, U, P])
        ps = s.psum("ps", [P, BANKS, 512])
        s_idx = [s.sem(f"idx{k}") for k in range(4)]
        s_gat = [s.sem(f"gat{k}") for k in range(2)]
        s_sel, s_agg, s_acc, s_passed = (s.sem(x) for x in ("sel", "agg", "acc", "passed"))
        with nc.Block() as block:
            @block.sync
            def _(sp):
                stage_indices(sp, gather_idx, idx, s_idx, s_gat)

            @block.gpsimd
            def _(pool):
                gather_rows(pool, table_dram, idx, rows, s_idx, s_gat, s_agg, s_passed)

            @block.vector
            def _(dve):
                def select(g, j):
                    wait(dve, s_agg, (g - 1) * U if started(g, 2) else 0)
                    if norm is None:
                        row = order.row[:, bass.ds(g * U, U)]
                        dve.tensor_tensor(sel[:, j % 2, :, :], c.iota[:, :].unsqueeze(1).to_broadcast([P, U, P]),
                                          row.unsqueeze(2).to_broadcast([P, U, P]), ALU.is_equal).then_inc(s_sel, U)

                def select_tile(g, j, u):
                    if norm is not None:
                        dve.tensor_scalar(sel[:, j % 2, u, :], c.iota[:, :],
                                          order.row[:, bass.ds(g * U + u, 1)], norm[:, bass.ds(g * U + u, 1)],
                                          ALU.is_equal, ALU.mult).then_inc(s_sel, 1)

                def add(g, u, tile):
                    t = g * U + u
                    dve.wait_ge(s_agg, t + 1)
                    wait(dve, s_acc, t)
                    acc = c.acc[:, bass.ds(tile, 1), 0:D].rearrange("p a d -> p (a d)")
                    dve.tensor_tensor(acc, acc, ps[:, u % BANKS, 0:D], ALU.add).then_inc(s_acc, 1)

                def body(g, j):
                    select(g, j)
                    for u in range(U):
                        select_tile(g, j, u)
                        if started(g, 1):
                            if u % PACK == 0:
                                tiles = tile_registers(nc, dve, order, g - 1, u // PACK)
                            add(g - 1, u, tiles[u % PACK])
                groups4(dve, SG, body)
                for u in range(U):
                    if u % PACK == 0:
                        tiles = tile_registers(nc, dve, order, SG - 1, u // PACK)
                    add(SG - 1, u, tiles[u % PACK])
                dve.wait_ge(s_acc, ST)

            @block.tensor
            def _(pe):
                def body(g, j):
                    pe.wait_ge(s_gat[j % 2], halves(g, j, 16 * U, 1))
                    for u in range(U):
                        pe.wait_ge(s_sel, g * U + u + 1)
                        wait(pe, s_acc, (g - 1) * U + u + 1 if started(g, 1) else 0)
                        pe.matmul(ps[:, u % BANKS, 0:D], sel[:, j % 2, u, :], rows[:, j % 2, u, :],
                                  start=True, stop=True).then_inc(s_agg, 1)
                groups4(pe, SG, body)


def gather_sum_attention(nc, c, name, order, gather_idx, table_dram, heads, gathered):
    H = heads
    W = D + H
    BANK0, BANKS = 3, 4
    with ExitStack() as ctx:
        s = Scope(nc, ctx, name)
        idx = s.sb("idx", [P, 4, U], U32)
        rows = s.sb("rows", [P, 2, U, W])
        sel = s.sb("sel", [P, 4, U, P])
        sel_t = s.sb("sel_t", [P, U, P])
        own = s.sb("own", [P, 4, U, 2 * H])
        z = s.sb("z", [P, U, H])
        y = s.sb("y", [P, U, H])
        ps = s.psum("ps", [P, 8, 512])
        tr = ps[:, 0:2, :].rearrange("p b (u e) -> p (b u) e", u=4)
        look = ps[:, 2, 0:U * 2 * H].rearrange("p (u h) -> p u h", u=U)
        s_idx = [s.sem(f"idx{k}") for k in range(4)]
        s_gat = [s.sem(f"gat{k}") for k in range(2)]
        s_own = [s.sem(f"own{k}") for k in range(4)]
        s_far, s_sel, s_tr, s_st, s_look, s_pairs = (s.sem(x) for x in ("far", "sel", "tr", "st", "look", "pairs"))
        s_z, s_w, s_msg, s_v = (s.sem(x) for x in ("z", "w", "msg", "v"))
        s_agg, s_acc, s_passed = (s.sem(x) for x in ("agg", "acc", "passed"))
        with nc.Block() as block:
            @block.sync
            def _(sp):
                def stage_pairs(g, j):
                    wait(sp, s_look, g - 3)
                    for u, tile in enumerate(tile_registers(nc, sp, order, g, 0)):
                        sp.dma_start(own[:, j, u, :], c.pair[:, bass.ds(tile, 1), :].squeeze(1)).then_inc(s_own[j], 16)
                stage_indices(sp, gather_idx, idx, s_idx, s_gat, stage_pairs)

            @block.gpsimd
            def _(pool):
                gather_rows(pool, table_dram, idx, rows, s_idx, s_gat, s_agg, s_passed)

            @block.scalar
            def _(act):
                def select(g, j):
                    wait(act, s_agg, (g - 3) * U if started(g, 4) else 0)
                    for u in range(U):
                        far = act.activation(sel[:, j, u, :], c.iota[:, :], ACT.Abs,
                                             bias=order.row[:, bass.ds(g * U + u, 1)], scale=-1.0)
                    far.then_inc(s_far, 1)
                    act.wait_ge(s_far, g + 1)
                    act.activation(sel[:, j, :, :], sel[:, j, :, :], ACT.Relu, bias=c.ones[:, 0:1], scale=-1.0) \
                        .then_inc(s_sel, 1)

                def copy_pairs(g, j):
                    wait(act, s_look, g - 3)
                    for u, tile in enumerate(tile_registers(nc, act, order, g, 1), PACK):
                        act.copy(own[:, j, u, :], c.pair[:, bass.ds(tile, 1), :].squeeze(1)).then_inc(s_pairs, 1)

                def copy_turned(g):
                    act.wait_ge(s_tr, g + 1)
                    wait(act, s_look, g)
                    act.copy(sel_t[:, :, :], tr[:, :, :]).then_inc(s_st, 1)

                def weights(g, j):
                    act.wait_ge(s_z, g + 1)
                    wait(act, s_agg, (g - 1) * U if started(g, 2) else 0)
                    act.activation(rows[:, j % 2, :, D:W], y[:, :, :], ACT.Exp).then_inc(s_w, 1)

                def body(g, j):
                    if started(g, 2):
                        copy_turned(g - 2)
                    select(g, j)
                    copy_pairs(g, j)
                    if started(g, 2):
                        weights(g - 2, j)
                act.wait_ge(c.ready, 5)
                groups4(act, SG, body)
                for g in (SG - 2, SG - 1):
                    copy_turned(g)
                    weights(g, g % 2)

            @block.tensor
            def _(pe):
                def turn(g, j):
                    pe.wait_ge(s_sel, g + 1)
                    wait(pe, s_st, g)
                    pe.wait_ge(c.ready, 5)
                    for u in range(U):
                        mm = pe.transpose(tr[:, u, :], sel[:, j, u, :], c.ident[:, :])
                    mm.then_inc(s_tr, 1)

                def lookup(g, j):
                    pe.wait_ge(s_st, g + 1)
                    pe.wait_ge(s_own[j], quarters(g, j, 16 * PACK, 1))
                    pe.wait_ge(s_pairs, (g + 1) * (U - PACK))
                    wait(pe, s_z, g)
                    for u in range(U):
                        mm = pe.matmul(look[:, u, :], sel_t[:, u, :], own[:, j, u, :], start=True, stop=True)
                    mm.then_inc(s_look, 1)

                def sums(g, j, tiles):
                    for u in tiles:
                        t = g * U + u
                        pe.wait_ge(s_msg, t + 1)
                        wait(pe, s_acc, t - BANKS + 1 if not (isinstance(t, int) and t < BANKS) else 0)
                        pe.matmul(ps[:, BANK0 + u % BANKS, 0:W], sel[:, j, u, :], rows[:, j % 2, u, 0:W],
                                  start=True, stop=True).then_inc(s_agg, 1)

                def body(g, j):
                    if started(g, 1):
                        lookup(g - 1, (j - 1) % 4)
                    if started(g, 2):
                        sums(g - 2, (j - 2) % 4, range(0, 5))
                    turn(g, j)
                    if started(g, 2):
                        sums(g - 2, (j - 2) % 4, range(5, U))
                groups4(pe, SG, body)
                lookup(SG - 1, 3)
                sums(SG - 2, 2, range(U))
                sums(SG - 1, 3, range(U))

            @block.vector
            def _(dve):
                def weigh(g, step):
                    if step == 0:
                        dve.wait_ge(s_look, g + 1)
                        dve.tensor_tensor(z[:, :, :], gathered[:, bass.ds(g * U, U), 0:H], look[:, :, 0:H], ALU.add) \
                            .then_inc(s_v, 1)
                        return
                    dve.wait_ge(s_v, g * 3 + step)
                    if step == 1:
                        dve.scalar_tensor_tensor(out=y[:, :, :], in0=z[:, :, :], scalar=0.2, in1=z[:, :, :],
                                                 op0=ALU.mult, op1=ALU.max).then_inc(s_v, 1)
                    elif step == 2:
                        dve.tensor_tensor(z[:, :, :], y[:, :, :], look[:, :, H:2 * H], ALU.subtract).then_inc(s_v, 1)
                    else:
                        dve.tensor_scalar(y[:, :, :], z[:, :, :], 0.0, None, ALU.min).then_inc(s_z, 1)

                def multiply(j, u):
                    r = rows[:, j % 2, u, 0:D].rearrange("p (h d) -> p h d", h=H)
                    dve.tensor_tensor(r, r, rows[:, j % 2, u, D:W].unsqueeze(2).to_broadcast([P, H, D // H]),
                                      ALU.mult).then_inc(s_msg, 1)

                def add(g, u, tile):
                    t = g * U + u
                    dve.wait_ge(s_agg, t + 1)
                    wait(dve, s_acc, t)
                    acc = c.acc[:, bass.ds(tile, 1), 0:W].rearrange("p a d -> p (a d)")
                    dve.tensor_tensor(acc, acc, ps[:, BANK0 + u % BANKS, 0:W], ALU.add).then_inc(s_acc, 1)

                def group(g, j, following=None):
                    dve.wait_ge(s_w, g + 1)
                    dve.wait_ge(s_gat[j % 2], halves(g, j, 16 * U, 1))
                    for u in range(U):
                        multiply(j, u)
                        if u % PACK == 0 and (u or started(g, 1)):
                            tiles = tile_registers(nc, dve, order, g if u else g - 1, 0 if u else 1)
                        if u >= PACK:
                            add(g, u - PACK, tiles[u - PACK])
                        elif started(g, 1):
                            add(g - 1, u + PACK, tiles[u])
                        if 3 <= u < 7 and following is not None:
                            weigh(following, u - 3)

                def body(g, j):
                    if started(g, 1):
                        group(g - 1, j - 1, following=g)
                    else:
                        for step in range(4):
                            weigh(g, step)
                groups4(dve, SG, body)
                group(SG - 1, 3)
                for u, tile in enumerate(tile_registers(nc, dve, order, SG - 1, 1), PACK):
                    add(SG - 1, u, tile)
                dve.wait_ge(s_acc, ST)


def softmax_mean(nc, c, name, heads, bias_dram):
    H = heads
    with ExitStack() as ctx:
        s = Scope(nc, ctx, name)
        bias = s.sb("bias", [P, D])
        den = s.sb("den", [P, NT, H])
        s_b, s_v = s.sem("b"), s.sem("v")
        with nc.Block() as block:
            @block.sync
            def _(sp):
                sp.dma_start(bias[:, :], bias_dram.partition_broadcast(P)).then_inc(s_b, 16)

            @block.vector
            def _(dve):
                ch = Chain(dve, s_v)
                ch.step(dve.tensor_scalar(den[:, :, :], c.acc[:, :, D:D + H], 1e-16, None, ALU.max))
                ch.step(dve.reciprocal(den[:, :, :], den[:, :, :]))
                a4 = c.acc[:, :, 0:D].rearrange("p t (h d) -> p t h d", h=H)
                ch.step(dve.tensor_tensor(a4, a4, den[:, :, :].unsqueeze(3).to_broadcast([P, NT, H, D // H]), ALU.mult))
                dve.wait_ge(s_b, 16)
                ch.step(dve.tensor_tensor(c.acc[:, :, 0:D], c.acc[:, :, 0:D],
                                          bias[:, :].unsqueeze(1).to_broadcast([P, NT, D]), ALU.add))


def batch_norm_add(nc, c, name, gamma_dram, beta_dram):
    with ExitStack() as ctx:
        s = Scope(nc, ctx, name)
        gamma = s.sb("gamma", [P, D])
        beta = s.sb("beta", [P, D])
        mean = s.sb("mean", [P, D])
        std = s.sb("std", [P, D])
        eps = s.sb("eps", [P, 1])
        sq = s.sb("sq", [P, 2, D])
        ps = s.psum("ps", [P, 2, 512])
        s_b, s_v, s_sum, s_dev, s_sq, s_sq_mm, s_var, s_std = (
            s.sem(x) for x in ("b", "v", "sum", "dev", "sq", "sq_mm", "var", "std"))
        FULL = NT - 1

        with nc.Block() as block:
            @block.sync
            def _(sp):
                sp.dma_start(gamma[:, :], gamma_dram.partition_broadcast(P)).then_inc(s_b, 16)
                sp.dma_start(beta[:, :], beta_dram.partition_broadcast(P)).then_inc(s_b, 16)

            @block.tensor
            def _(pe):
                pe.matmul(ps[:, 0, 0:D], c.ones[0:LAST, :], c.acc[0:LAST, NT - 1, 0:D], start=True, stop=False,
                          skip_group_check=True)
                loop(pe, FULL, lambda i: pe.matmul(
                    ps[:, 0, 0:D], c.ones[:, :], c.acc[:, bass.ds(i, 1), 0:D].rearrange("p a d -> p (a d)"),
                    start=False, stop=False, skip_group_check=True).then_inc(s_sum, 1))

                def squares(j, k):
                    pe.wait_ge(s_sq, j + 1)
                    M = LAST if isinstance(j, int) and j == NT - 1 else P
                    pe.matmul(ps[:, 1, 0:D], c.ones[0:M, :], sq[0:M, k, :], start=isinstance(j, int) and j == 0,
                              stop=False, skip_group_check=True).then_inc(s_sq_mm, 1)
                node_tiles(pe, squares)

            @block.scalar
            def _(act):
                act.wait_ge(s_dev, 1)

                def squares(j, k):
                    wait(act, s_sq_mm, j - 1)
                    act.wait_ge(s_dev, 1)
                    act.activation(sq[:, k, :], c.acc[:, bass.ds(j, 1), 0:D].rearrange("p a d -> p (a d)"),
                                   ACT.Square).then_inc(s_sq, 1)
                node_tiles(act, squares)
                act.wait_ge(s_var, 1)
                act.activation(std[:, :], std[:, :], ACT.Sqrt, bias=eps[:, 0:1]).then_inc(s_std, 1)

            @block.vector
            def _(dve):
                ch = Chain(dve, s_v)
                acc = c.acc[:, :, 0:D]

                def rows(ap):
                    return ap[:, :].unsqueeze(1).to_broadcast([P, NT, D])
                ch.step(dve.memset(eps[:, :], EPS))
                dve.wait_ge(s_sum, FULL)
                ch.step(dve.tensor_scalar(mean[:, :], ps[:, 0, 0:D], 1.0 / N, None, ALU.mult))
                dve.tensor_tensor(acc, acc, rows(mean), ALU.subtract).then_inc(s_dev, 1)
                dve.wait_ge(s_sq_mm, NT)
                dve.tensor_scalar(std[:, :], ps[:, 1, 0:D], 1.0 / N, None, ALU.mult).then_inc(s_var, 1)
                dve.wait_ge(s_std, 1)
                dve.wait_ge(s_b, 32)
                ch.step(dve.reciprocal(std[:, :], std[:, :]))
                ch.step(dve.tensor_tensor(std[:, :], std[:, :], gamma[:, :], ALU.mult))
                dve.wait_ge(s_dev, 1)
                ch.step(dve.tensor_tensor(acc, acc, rows(std), ALU.mult))
                ch.step(dve.tensor_tensor(acc, acc, rows(beta), ALU.add))
                ch.step(dve.tensor_tensor(c.x[:, :, :], c.x[:, :, :], acc, ALU.add))


def add_nodes(nc, c, name, relu):
    with ExitStack() as ctx:
        s = Scope(nc, ctx, name)
        s_v = s.sem("v")
        with nc.Block() as block:
            @block.vector
            def _(dve):
                ch = Chain(dve, s_v)
                if relu:
                    ch.step(dve.scalar_tensor_tensor(out=c.x[:, :, :], in0=c.acc[:, :, 0:D], scalar=0.0, in1=c.x[:, :, :],
                                                     op0=ALU.max, op1=ALU.add))
                else:
                    ch.step(dve.tensor_tensor(c.x[:, :, :], c.x[:, :, :], c.acc[:, :, 0:D], ALU.add))


def start_acc(nc, c, name, table_dram=None):
    with ExitStack() as ctx:
        s = Scope(nc, ctx, name)
        s_v = s.sem("v")
        with nc.Block() as block:
            if table_dram is None:
                @block.vector
                def _(dve):
                    dve.memset(c.acc[:, :, 0:D], 0.0).then_inc(s_v, 16)
                    dve.wait_ge(s_v, 16)
            else:
                @block.sync
                def _(sp):
                    sp.dma_start(c.acc[:, :, 0:D], table_dram.rearrange("(t p) d -> p t d", p=P)).then_inc(s_v, 16)
                    sp.wait_ge(s_v, 16)


def relation_tables(nc, c, name, w_dram, table_dram):
    PAIRS = RELS // 2
    RING = 5
    with ExitStack() as ctx:
        s = Scope(nc, ctx, name)
        h = s.sb("h", [P, 2, D])
        h_t = s.sb("h_t", [P, 2, 2, P])
        w = s.sb("w", [P, 2, RELS * D])
        stage = s.sb("stage", [P, 2, RELS * D])
        ps = s.psum("ps", [P, 8, 512])
        s_w, s_h, s_tr, s_ht, s_mm = (s.sem(x) for x in ("w", "h", "tr", "ht", "mm"))
        s_even, s_odd = s.sem("even"), s.sem("odd")
        s_out = [s.sem(f"out{k}") for k in range(2)]
        with nc.Block() as block:
            @block.sync
            def _(sp):
                for half in range(2):
                    sp.dma_start(w[:, half, :].rearrange("p (r n) -> p r n", r=RELS),
                                 w_dram[:, half * P:(half + 1) * P, :].rearrange("r p n -> p r n")).then_inc(s_w, 16)

                def body(j, k):
                    sp.wait_ge(s_even, (j + 1) * (PAIRS // 2))
                    sp.wait_ge(s_odd, (j + 1) * (PAIRS // 2))
                    sp.dma_start(table_dram[bass.ds(j * P, P), :], stage[:, k, :]).then_inc(s_out[k], 16)
                node_tiles(sp, body)
                sp.wait_ge(s_out[0], 16 * (NT - NT // 2))
                sp.wait_ge(s_out[1], 16 * (NT // 2))

            def copies(eng, copy, parity, sem, j, k):
                wait(eng, s_out[k], halves(j, k, 16))
                for m in range(parity, PAIRS, 2):
                    eng.wait_ge(s_mm, j * PAIRS + m + 1)
                    copy(stage[:, k, m * 512:(m + 1) * 512], ps[:, 2 + m % RING, :]).then_inc(sem, 1)

            @block.scalar
            def _(act):
                def hidden(j, k):
                    wait(act, s_tr, j - 1)
                    act.wait_ge(c.ready, 5)
                    act.activation(h[:, k, :], c.x[:, bass.ds(j, 1), :].rearrange("p a b -> p (a b)"), ACT.Relu,
                                   bias=c.shift[:, bass.ds(j, 1)], scale=c.rstd[:, bass.ds(j, 1)]).then_inc(s_h, 1)

                def body(j, k):
                    if not isinstance(j, int):
                        hidden(j + 1, 1 - k)
                    elif j + 1 < NT:
                        hidden(j + 1, 1 - k)
                    copies(act, act.copy, 0, s_even, j, k)
                hidden(0, 0)
                node_tiles(act, body)

            @block.vector
            def _(dve):
                def turned(j, k):
                    dve.wait_ge(s_tr, j + 1)
                    wait(dve, s_mm, (j - 1) * PAIRS)
                    dve.tensor_copy(h_t[:, k, :, :], ps[:, k, 0:D].rearrange("p (a b) -> p a b", a=2)).then_inc(s_ht, 1)

                def body(j, k):
                    if not isinstance(j, int) or j + 1 < NT:
                        turned(j + 1, 1 - k)
                    copies(dve, dve.tensor_copy, 1, s_odd, j, k)
                turned(0, 0)
                node_tiles(dve, body)

            @block.tensor
            def _(pe):
                def turn(j, k):
                    pe.wait_ge(s_h, j + 1)
                    wait(pe, s_ht, j - 1)
                    pe.wait_ge(c.ready, 5)
                    for half in range(2):
                        mm = pe.transpose(ps[:, k, half * P:(half + 1) * P], h[:, k, half * P:(half + 1) * P], c.ident[:, :])
                    mm.then_inc(s_tr, 1)

                def body(j, k):
                    if not isinstance(j, int) or j + 1 < NT:
                        turn(j + 1, 1 - k)
                    pe.wait_ge(s_ht, j + 1)
                    for m in range(PAIRS):
                        before = m - RING
                        at = j if before >= 0 else j - 1
                        before %= PAIRS
                        wait(pe, s_odd if before % 2 else s_even,
                             at * (PAIRS // 2) + before // 2 + 1 if started(at, 0) and not (isinstance(at, int) and at < 0) else 0)
                        for half in range(2):
                            mm = pe.matmul(ps[:, 2 + m % RING, :], h_t[:, k, half, :], w[:, half, m * 512:(m + 1) * 512],
                                           start=half == 0, stop=half == 1)
                        mm.then_inc(s_mm, 1)
                pe.wait_ge(s_w, 32)
                turn(0, 0)
                node_tiles(pe, body)


def inverse_degrees(nc, c, name):
    with ExitStack() as ctx:
        s = Scope(nc, ctx, name)
        s_a, s_v = s.sem("a"), s.sem("v")
        with nc.Block() as block:
            @block.scalar
            def _(act):
                act.activation(c.dinv[:, :], c.degree[:, :], ACT.Sqrt, bias=c.ones[:, 0:1]).then_inc(s_a, 1)

            @block.vector
            def _(dve):
                dve.wait_ge(s_a, 1)
                dve.reciprocal(c.dinv[:, :], c.dinv[:, :]).then_inc(s_v, 1)
                dve.wait_ge(s_v, 1)


def finish(nc, c, name, bias_dram, out_dram):
    PARTS = 7
    with ExitStack() as ctx:
        s = Scope(nc, ctx, name, last=True)
        bias = s.sb("bias", [P, D])
        s_b, s_v, s_part, s_out = s.sem("b"), s.sem("v"), s.sem("part"), s.sem("out")
        with nc.Block() as block:
            @block.sync
            def _(sp):
                sp.dma_start(bias[:, :], bias_dram.partition_broadcast(P)).then_inc(s_b, 16)
                for i, t in enumerate(range(0, NT, PARTS)):
                    sp.wait_ge(s_part, i + 1)
                    full = min(t + PARTS, NT - 1)
                    sp.dma_start(out_dram[t * P:full * P, :].rearrange("(t p) d -> p t d", p=P), c.x[:, t:full, :]) \
                        .then_inc(s_out, 16)
                sp.dma_start(out_dram[(NT - 1) * P:N, :], c.x[0:LAST, NT - 1, :]).then_inc(s_out, 16)
                sp.wait_ge(s_out, 16 * (NT // PARTS + 1))

            @block.vector
            def _(dve):
                ch = Chain(dve, s_v)
                dve.wait_ge(s_b, 16)
                for t in range(0, NT, PARTS):
                    acc = c.acc[:, t:t + PARTS, 0:D]
                    x = c.x[:, t:t + PARTS, :]
                    ch.step(dve.tensor_tensor(acc, acc, c.dinv[:, t:t + PARTS].unsqueeze(2).to_broadcast([P, PARTS, D]),
                                              ALU.mult))
                    ch.step(dve.tensor_tensor(acc, acc, bias[:, :].unsqueeze(1).to_broadcast([P, PARTS, D]), ALU.add))
                    dve.scalar_tensor_tensor(out=x, in0=acc, scalar=0.0, in1=x, op0=ALU.max, op1=ALU.add) \
                        .then_inc(s_part, 1)


def gnn_kernel(nc, a, out_dram):
    def dram(name, shape):
        return nc.dram_tensor(name, shape, F32, kind="Internal").ap()

    slots_by_dst = dram("slots_by_dst", (P, ST, 4))
    slots_by_src = dram("slots_by_src", (P, ST, 2))
    rows0, rows1, rows3 = (dram(f"rows{i}", (NPAD, D)) for i in (0, 1, 3))
    rows2 = dram("rows2", (NPAD, RELS * D))
    with ExitStack() as ctx:
        c = Scope(nc, ctx, "c", last=True)
        make_constants(nc, c)
        by_dst = Order(c, "by_dst", (("src", U32), ("src_rel", U32), ("norm", F32), ("dst", F32)))
        by_dst.key = by_dst.words[3]
        by_src = Order(c, "by_src", (("dst", U32), ("src", F32)))
        by_src.key = by_src.words[1]
        c.x = c.sb("x", [P, NT, D])
        c.rstd = c.sb("rstd", [P, NT])
        c.shift = c.sb("shift", [P, NT])
        c.degree = c.sb("degree", [P, NT])
        c.dinv = c.sb("dinv", [P, NT])
        load_nodes(nc, c, a["x"])
        sort_edges(nc, c, "sort_dst", a["dst"], dst_fields(a["src"], a["edge_type_20"], a["edge_weight1"]), 4,
                   slots_by_dst, by_dst)
        sort_edges(nc, c, "sort_src", a["src"], src_fields(a["dst"]), 2, slots_by_src, by_src)

        for layer, heads, order, rows in ((0, 8, by_dst, rows0), (1, 4, by_src, rows1)):
            with ExitStack() as layer_ctx:
                s = Scope(nc, layer_ctx, f"layer{layer}")
                c.att = s.sb("att", [P, NT, 2 * heads])
                c.seg_max = s.sb("seg_max", [P, NT, heads])
                c.pair = s.sb("pair", [P, NT, 2 * heads])
                gathered = s.sb("gathered", [P, ST, heads])
                small = dram(f"small{layer}", (NPAD, heads))
                layer_norm_stats(nc, c, f"ln{layer}")
                with ExitStack() as project_ctx:
                    w = Scope(nc, project_ctx, f"project{layer}").sb("w", [P, 2, D])
                    if layer == 0:
                        att = [a[n].rearrange("h d -> (h d)") for n in ("L0_gnn_att_src", "L0_gnn_att_dst")]
                        w_loads = [(w[:, :, :], a["L0_gnn_W"].rearrange("(k p) n -> p k n", p=P))]
                    else:
                        att = [a[n].rearrange("a h d -> (a h d)") for n in ("L1_gnn_att_dst", "L1_gnn_att_src")]
                        w_loads = [(w[:, k, :].rearrange("p (h c) -> p h c", h=heads),
                                    a["L1_gnn_weight"][:, k * P:(k + 1) * P, :].rearrange("h p c -> p h c"))
                                   for k in range(2)]
                    attention_scalars(nc, c, f"att{layer}", w, w_loads, att, heads, small)
                    project_and_gather(nc, c, f"proj{layer}", w, rows, layer == 0, order.words[0], heads, small, gathered,
                                       pool_groups=60 if layer == 0 else 44)
                segment_max(nc, c, f"max{layer}", order, heads, gathered, dram(f"ends{layer}", (P, 3)),
                            dram(f"carry{layer}", (P, 2)), dram(f"maxima{layer}", (P * ST, heads)))
                count_columns(nc, c, f"count{layer}", order)
                c.acc = s.sb("acc", [P, NT, D + heads])
                attention_nodes(nc, c, f"nodes{layer}", heads, rows, loops=layer == 0)
                gather_sum_attention(nc, c, f"sum{layer}", order, order.words[0], rows, heads, gathered)
                softmax_mean(nc, c, f"mean{layer}", heads, a[f"L{layer}_gnn_bias"])
                if layer == 0:
                    batch_norm_add(nc, c, "bn0", a["L0_gnn_gamma"], a["L0_gnn_beta"])
                else:
                    add_nodes(nc, c, "add1", relu=False)

        layer_norm_stats(nc, c, "ln2")
        relation_tables(nc, c, "proj2", a["L2_gnn_weight"], rows2)
        c.acc = c.sb("acc", [P, NT, D])
        start_acc(nc, c, "start2")
        gather_sum(nc, c, "sum2", by_dst, by_dst.words[1], rows2.rearrange("n (r d) -> (n r) d", r=RELS),
                   norm=by_dst.words[2])
        add_nodes(nc, c, "add2", relu=True)

        layer_norm_stats(nc, c, "ln3")
        count_columns(nc, c, "count3", by_dst)
        inverse_degrees(nc, c, "deg3")
        project_normed(nc, c, "proj3", a["L3_gnn_weight"], rows3,
                       [a[f"L3_gnn_{n}"] for n in ("gamma", "beta", "running_mean", "running_var")], c.dinv)
        start_acc(nc, c, "start3", rows3)
        gather_sum(nc, c, "sum3", by_dst, by_dst.words[0], rows3)
        finish(nc, c, "finish", a["L3_gnn_bias"], out_dram)


_INS = ["x", "src", "dst", "edge_type_20", "edge_weight1",
        "L0_gnn_W", "L0_gnn_att_src", "L0_gnn_att_dst", "L0_gnn_bias", "L0_gnn_gamma", "L0_gnn_beta",
        "L1_gnn_weight", "L1_gnn_att_src", "L1_gnn_att_dst", "L1_gnn_bias", "L2_gnn_weight",
        "L3_gnn_weight", "L3_gnn_bias", "L3_gnn_gamma", "L3_gnn_beta", "L3_gnn_running_mean", "L3_gnn_running_var"]


def kernel(**inputs):
    import concourse.bacc as bacc
    from concourse.bass_utils import run_bass_kernel_spmd

    nc = bacc.Bacc("TRN2", target_bir_lowering=False, num_devices=1)
    arrays, aps = {}, {}
    for name in _INS:
        array = np.ascontiguousarray(inputs[name])
        arrays[f"in_{name}"] = array
        aps[name] = nc.dram_tensor(f"in_{name}", array.shape, mybir.dt.from_np(array.dtype), kind="ExternalInput").ap()
    out = nc.dram_tensor("out_0", (N, D), F32, kind="ExternalOutput").ap()
    gnn_kernel(nc, aps, out)
    result = run_bass_kernel_spmd(nc, [arrays], core_ids=[0])
    return result.results[0]["out_0"]
```
